# Optimizing a Trainium2 kernel written in Bass

```python
import numpy as np
import jax
import jax.numpy as jnp

def _softmax(x, axis=-1):
    return jax.nn.softmax(x, axis=axis)

def _gelu(x):
    return jax.nn.gelu(x, approximate=True)

def _silu(x):
    return jax.nn.silu(x)

def _sigmoid(x):
    return jax.nn.sigmoid(x)

def _layernorm(x, axis=-1, eps=1e-05):
    m = jnp.mean(x, axis=axis, keepdims=True)
    v = jnp.var(x, axis=axis, keepdims=True)
    return (x - m) / jnp.sqrt(v + eps)

def _scatter_add(tgt, idx, src, axis=0):
    return tgt.at[idx].add(src)

def _segment_sum(src, seg, n):
    return jax.ops.segment_sum(src, seg, n)
kernel_name = 'mk_seq_preln_d2_jaxref_r8_0d22b3'

def setup_inputs(seed: int=0):
    np.random.seed(seed)
    _w = jnp.asarray

    def _L0_attn_setup():
        import jax, jax.numpy as jnp
        import numpy as np
        B, S, HID, NH = (8, 512, 128, 16)
        D = HID // NH
        LN_EPS = 1e-05

        def _l2norm(a):
            n = jnp.sqrt(jnp.sum(a * a, axis=-1, keepdims=True))
            return a / jnp.maximum(n, 1e-12)
        key = jax.random.key(seed)
        ks = jax.random.split(key, 8)
        s = 0.02
        x = jax.random.normal(ks[0], (B, S, HID), jnp.float32)
        Wq = jax.random.normal(ks[1], (HID, NH * D), jnp.float32) * s
        Wk = jax.random.normal(ks[2], (HID, NH * D), jnp.float32) * s
        Wv = jax.random.normal(ks[3], (HID, NH * D), jnp.float32) * s
        Wbeta = jax.random.normal(ks[4], (HID, NH), jnp.float32) * s
        Wg = jax.random.normal(ks[5], (HID, NH * D), jnp.float32) * s
        Wout = jax.random.normal(ks[6], (NH * D, HID), jnp.float32) * s
        ln_g = jnp.ones((NH * D,), jnp.float32)
        ln_b = jnp.zeros((NH * D,), jnp.float32)
        return {'x': x, 'Wq': Wq, 'Wk': Wk, 'Wv': Wv, 'Wbeta': Wbeta, 'Wg': Wg, 'Wout': Wout, 'ln_g': ln_g, 'ln_b': ln_b}
    _L0_attn_in = _L0_attn_setup()

    def _L0_ffn_setup():
        import jax, jax.numpy as jnp
        import numpy as np
        B, T, C, E, K, CAP, H = (8, 256, 128, 8, 2, 512, 512)
        key = jax.random.key(seed)
        ks = jax.random.split(key, 6)
        s = 0.02
        return {'x': jax.random.normal(ks[0], (B, T, C), jnp.float32), 'rw1': s * jax.random.normal(ks[1], (C, H), jnp.float32), 'rb1': jnp.zeros((H,), jnp.float32), 'rw2': s * jax.random.normal(ks[2], (H, E), jnp.float32), 'rb2': jnp.zeros((E,), jnp.float32), 'ew1': s * jax.random.normal(ks[3], (E, C, H), jnp.float32), 'eb1': jnp.zeros((E, H), jnp.float32), 'ew2': s * jax.random.normal(ks[4], (E, H, C), jnp.float32), 'eb2': jnp.zeros((E, C), jnp.float32)}
    _L0_ffn_in = _L0_ffn_setup()

    def _L1_attn_setup():
        import jax, jax.numpy as jnp
        import numpy as np
        B, T, HM = (2, 256, 128)
        HEADS = 16
        DK = HM // 2 // HEADS
        DV = HM // HEADS
        LOW_RANK = 16
        GATE_NORM = 16.0
        EPS = 1e-05

        def _ln(x, w, b):
            m = x.mean(-1, keepdims=True)
            v = ((x - m) ** 2).mean(-1, keepdims=True)
            return (x - m) * jax.lax.rsqrt(v + EPS) * w + b

        def _rms(x, w):
            return x * jax.lax.rsqrt((x * x).mean(-1, keepdims=True) + EPS) * w

        def _gla(q, k, v, gk):

            def step(S, inp):
                qt, kt, vt, gt = inp
                S = jnp.exp(gt)[..., None] * S + kt[..., None] * vt[..., None, :]
                return (S, jnp.einsum('bhk,bhkv->bhv', qt, S))
            xs = tuple((jnp.moveaxis(a, 1, 0) for a in (q, k, v, gk)))
            S0 = jnp.zeros((q.shape[0], q.shape[2], q.shape[3], v.shape[3]), q.dtype)
            _, o = jax.lax.scan(step, S0, xs)
            return jnp.moveaxis(o, 0, 1)
        key = jax.random.key(seed)
        ks = jax.random.split(key, 12)

        def p(k, shape, s=0.02):
            return jax.random.normal(k, shape, jnp.float32) * s
        return dict(x=jax.random.normal(ks[0], (B, T, HM), jnp.float32), ln_w=jnp.ones((HM,), jnp.float32), ln_b=jnp.zeros((HM,), jnp.float32), Wq=p(ks[1], (HM, HEADS * DK)), Wk=p(ks[2], (HM, HEADS * DK)), Wv=p(ks[3], (HM, HEADS * DV)), gk_w1=p(ks[4], (HM, LOW_RANK)), gk_w2=p(ks[5], (LOW_RANK, HEADS * DK)), gk_b2=jnp.zeros((HEADS * DK,), jnp.float32), Wg=p(ks[6], (HM, HEADS * DV)), rms_w=jnp.ones((DV,), jnp.float32), Wo=p(ks[7], (HEADS * DV, HM)), W1=p(ks[8], (HM, 2 * HM)), b1=jnp.zeros((2 * HM,), jnp.float32), W2=p(ks[9], (2 * HM, HM)), b2=jnp.zeros((HM,), jnp.float32))
    _L1_attn_in = _L1_attn_setup()

    def _L1_ffn_setup():
        import jax, jax.numpy as jnp
        import numpy as np
        E = 16
        K = 4
        B, S, H, I = (4, 128, 128, 256)
        key = jax.random.key(seed)
        k0, k1, k2, k3 = jax.random.split(key, 4)
        scale = 0.02
        return {'hidden_states': jax.random.normal(k0, (B, S, H), jnp.float32), 'router_w': jax.random.normal(k1, (H, E), jnp.float32) * scale, 'router_b': jnp.zeros((E,), jnp.float32), 'w1': jax.random.normal(k2, (E, H, I), jnp.float32) * scale, 'b1': jnp.zeros((E, I), jnp.float32), 'w2': jax.random.normal(k3, (E, I, H), jnp.float32) * scale, 'b2': jnp.zeros((E, H), jnp.float32)}
    _L1_ffn_in = _L1_ffn_setup()
    _d = {'L0_attn_x': _L0_attn_in['x'], 'L0_attn_Wq': _L0_attn_in['Wq'], 'L0_attn_Wk': _L0_attn_in['Wk'], 'L0_attn_Wv': _L0_attn_in['Wv'], 'L0_attn_Wbeta': _L0_attn_in['Wbeta'], 'L0_attn_Wg': _L0_attn_in['Wg'], 'L0_attn_Wout': _L0_attn_in['Wout'], 'L0_attn_ln_g': _L0_attn_in['ln_g'], 'L0_attn_ln_b': _L0_attn_in['ln_b'], 'L0_ffn_rw1': _L0_ffn_in['rw1'], 'L0_ffn_rb1': _L0_ffn_in['rb1'], 'L0_ffn_rw2': _L0_ffn_in['rw2'], 'L0_ffn_rb2': _L0_ffn_in['rb2'], 'L0_ffn_ew1': _L0_ffn_in['ew1'], 'L0_ffn_eb1': _L0_ffn_in['eb1'], 'L0_ffn_ew2': _L0_ffn_in['ew2'], 'L0_ffn_eb2': _L0_ffn_in['eb2'], 'L1_attn_ln_w': _L1_attn_in['ln_w'], 'L1_attn_ln_b': _L1_attn_in['ln_b'], 'L1_attn_Wq': _L1_attn_in['Wq'], 'L1_attn_Wk': _L1_attn_in['Wk'], 'L1_attn_Wv': _L1_attn_in['Wv'], 'L1_attn_gk_w1': _L1_attn_in['gk_w1'], 'L1_attn_gk_w2': _L1_attn_in['gk_w2'], 'L1_attn_gk_b2': _L1_attn_in['gk_b2'], 'L1_attn_Wg': _L1_attn_in['Wg'], 'L1_attn_rms_w': _L1_attn_in['rms_w'], 'L1_attn_Wo': _L1_attn_in['Wo'], 'L1_attn_W1': _L1_attn_in['W1'], 'L1_attn_b1': _L1_attn_in['b1'], 'L1_attn_W2': _L1_attn_in['W2'], 'L1_attn_b2': _L1_attn_in['b2'], 'L1_ffn_router_w': _L1_ffn_in['router_w'], 'L1_ffn_router_b': _L1_ffn_in['router_b'], 'L1_ffn_w1': _L1_ffn_in['w1'], 'L1_ffn_b1': _L1_ffn_in['b1'], 'L1_ffn_w2': _L1_ffn_in['w2'], 'L1_ffn_b2': _L1_ffn_in['b2']}
    _x0 = _d['L0_attn_x']
    _d['L0_attn_x'] = jax.random.normal(jax.random.fold_in(jax.random.key(seed), 1), (8, 512, 128), dtype=_x0.dtype)
    del _x0
    return _d

def reference(L0_attn_x, L0_attn_Wq, L0_attn_Wk, L0_attn_Wv, L0_attn_Wbeta, L0_attn_Wg, L0_attn_Wout, L0_attn_ln_g, L0_attn_ln_b, L0_ffn_rw1, L0_ffn_rb1, L0_ffn_rw2, L0_ffn_rb2, L0_ffn_ew1, L0_ffn_eb1, L0_ffn_ew2, L0_ffn_eb2, L1_attn_ln_w, L1_attn_ln_b, L1_attn_Wq, L1_attn_Wk, L1_attn_Wv, L1_attn_gk_w1, L1_attn_gk_w2, L1_attn_gk_b2, L1_attn_Wg, L1_attn_rms_w, L1_attn_Wo, L1_attn_W1, L1_attn_b1, L1_attn_W2, L1_attn_b2, L1_ffn_router_w, L1_ffn_router_b, L1_ffn_w1, L1_ffn_b1, L1_ffn_w2, L1_ffn_b2):

    def _L0_attn_ref(x, Wq, Wk, Wv, Wbeta, Wg, Wout, ln_g, ln_b):
        import jax, jax.numpy as jnp
        import numpy as np
        B, S, HID, NH = (8, 512, 128, 16)
        D = HID // NH
        LN_EPS = 1e-05

        def _l2norm(a):
            n = jnp.sqrt(jnp.sum(a * a, axis=-1, keepdims=True))
            return a / jnp.maximum(n, 1e-12)
        b, s, _ = x.shape
        nh = Wbeta.shape[1]
        d = Wq.shape[1] // nh
        q = _l2norm((x @ Wq).reshape(b, s, nh, d))
        k = _l2norm((x @ Wk).reshape(b, s, nh, d))
        v = (x @ Wv).reshape(b, s, nh, d)
        beta = jax.nn.sigmoid(x @ Wbeta)
        qT = jnp.moveaxis(q, 1, 0)
        kT = jnp.moveaxis(k, 1, 0)
        vT = jnp.moveaxis(v, 1, 0)
        bT = jnp.moveaxis(beta, 1, 0)
        state0 = jnp.zeros((b, nh, d, d), x.dtype)

        def step(state, inp):
            qt, kt, vt, bt = inp
            kk = kt[..., :, None] * kt[..., None, :]
            bb = bt[..., None, None]
            state = state * (1.0 - bb * kk) + bb * (vt[..., :, None] * kt[..., None, :])
            out_t = jnp.einsum('bhij,bhj->bhi', state, qt)
            return (state, out_t)
        _, outs = jax.lax.scan(step, state0, (qT, kT, vT, bT))
        out = jnp.moveaxis(outs, 0, 1).reshape(b, s, nh * d)
        mu = jnp.mean(out, axis=-1, keepdims=True)
        var = jnp.mean((out - mu) ** 2, axis=-1, keepdims=True)
        out = (out - mu) / jnp.sqrt(var + LN_EPS) * ln_g + ln_b
        out = out * jax.nn.silu(x @ Wg)
        return out @ Wout

    def _L0_ffn_ref(x, rw1, rb1, rw2, rb2, ew1, eb1, ew2, eb2):
        import jax, jax.numpy as jnp
        import numpy as np
        B, T, C, E, K, CAP, H = (8, 256, 128, 8, 2, 512, 512)
        Bx, Tx, Cx = x.shape
        N = Bx * Tx
        logits = jax.nn.relu(x @ rw1 + rb1) @ rw2 + rb2
        vals, ids = jax.lax.top_k(logits, K)
        probs = jax.nn.softmax(vals, axis=-1)
        ids_f = ids.reshape(N * K)
        probs_f = probs.reshape(N * K)
        xr = jnp.repeat(x.reshape(N, Cx), K, axis=0)
        m = jax.nn.one_hot(ids_f, E, dtype=jnp.int32)
        pos = jnp.cumsum(m, axis=0) - 1
        pos_tok = jnp.take_along_axis(pos, ids_f[:, None], axis=1)[:, 0]
        keep = (pos_tok < CAP).astype(x.dtype)
        pos_c = jnp.clip(pos_tok, 0, CAP - 1)
        disp = jnp.zeros((E, CAP, Cx), x.dtype).at[ids_f, pos_c].add(xr * keep[:, None])
        h = jax.nn.relu(jnp.einsum('enc,ech->enh', disp, ew1) + eb1[:, None, :])
        eo = jnp.einsum('enh,ehc->enc', h, ew2) + eb2[:, None, :]
        y = eo[ids_f, pos_c] * (probs_f * keep)[:, None]
        return y.reshape(Bx, Tx, K, Cx).sum(axis=2)

    def _L1_attn_ref(x, ln_w, ln_b, Wq, Wk, Wv, gk_w1, gk_w2, gk_b2, Wg, rms_w, Wo, W1, b1, W2, b2):
        import jax, jax.numpy as jnp
        import numpy as np
        B, T, HM = (2, 256, 128)
        HEADS = 16
        DK = HM // 2 // HEADS
        DV = HM // HEADS
        LOW_RANK = 16
        GATE_NORM = 16.0
        EPS = 1e-05

        def _ln(x, w, b):
            m = x.mean(-1, keepdims=True)
            v = ((x - m) ** 2).mean(-1, keepdims=True)
            return (x - m) * jax.lax.rsqrt(v + EPS) * w + b

        def _rms(x, w):
            return x * jax.lax.rsqrt((x * x).mean(-1, keepdims=True) + EPS) * w

        def _gla(q, k, v, gk):

            def step(S, inp):
                qt, kt, vt, gt = inp
                S = jnp.exp(gt)[..., None] * S + kt[..., None] * vt[..., None, :]
                return (S, jnp.einsum('bhk,bhkv->bhv', qt, S))
            xs = tuple((jnp.moveaxis(a, 1, 0) for a in (q, k, v, gk)))
            S0 = jnp.zeros((q.shape[0], q.shape[2], q.shape[3], v.shape[3]), q.dtype)
            _, o = jax.lax.scan(step, S0, xs)
            return jnp.moveaxis(o, 0, 1)
        Bb, Tt, _ = x.shape
        h = _ln(x, ln_w, ln_b)
        q = (h @ Wq).reshape(Bb, Tt, HEADS, DK)
        k = (h @ Wk).reshape(Bb, Tt, HEADS, DK)
        v = (h @ Wv).reshape(Bb, Tt, HEADS, DV)
        gk = jax.nn.log_sigmoid(h @ gk_w1 @ gk_w2 + gk_b2) / GATE_NORM
        gk = gk.reshape(Bb, Tt, HEADS, DK)
        o = _gla(q * DK ** (-0.5), k, v, gk)
        g = (h @ Wg).reshape(Bb, Tt, HEADS, DV)
        o = _rms(o, rms_w) * (g * jax.nn.sigmoid(g))
        x = x + o.reshape(Bb, Tt, HEADS * DV) @ Wo
        h2 = _ln(x, ln_w, ln_b)
        return x + jax.nn.gelu(h2 @ W1 + b1, approximate=False) @ W2 + b2

    def _L1_ffn_ref(hidden_states, router_w, router_b, w1, b1, w2, b2):
        import jax, jax.numpy as jnp
        import numpy as np
        E = 16
        K = 4
        B, S, H, I = (4, 128, 128, 256)
        b, s, h = hidden_states.shape
        logits = hidden_states @ router_w + router_b
        probs = jax.nn.softmax(logits, axis=-1)
        topw, topi = jax.lax.top_k(probs, K)
        topw = topw / jnp.sum(topw, axis=-1, keepdims=True)
        combine = jnp.sum(jax.nn.one_hot(topi, E, dtype=hidden_states.dtype) * topw[..., None], axis=2)
        x = hidden_states.reshape(b * s, h)
        c = combine.reshape(b * s, E)

        def body(acc, expert):
            w1e, b1e, w2e, b2e, ce = expert
            hmid = jax.nn.gelu(x @ w1e + b1e, approximate=False)
            return (acc + (hmid @ w2e + b2e) * ce[:, None], None)
        out, _ = jax.lax.scan(body, jnp.zeros_like(x), (w1, b1, w2, b2, c.T))
        return out.reshape(b, s, h)
    x = L0_attn_x
    x = x + _L0_attn_ref(_layernorm(x, axis=-1), L0_attn_Wq, L0_attn_Wk, L0_attn_Wv, L0_attn_Wbeta, L0_attn_Wg, L0_attn_Wout, L0_attn_ln_g, L0_attn_ln_b)
    x = x + _L0_ffn_ref(_layernorm(x, axis=-1), L0_ffn_rw1, L0_ffn_rb1, L0_ffn_rw2, L0_ffn_rb2, L0_ffn_ew1, L0_ffn_eb1, L0_ffn_ew2, L0_ffn_eb2)
    x = x + _L1_attn_ref(_layernorm(x, axis=-1), L1_attn_ln_w, L1_attn_ln_b, L1_attn_Wq, L1_attn_Wk, L1_attn_Wv, L1_attn_gk_w1, L1_attn_gk_w2, L1_attn_gk_b2, L1_attn_Wg, L1_attn_rms_w, L1_attn_Wo, L1_attn_W1, L1_attn_b1, L1_attn_W2, L1_attn_b2)
    x = x + _L1_ffn_ref(_layernorm(x, axis=-1), L1_ffn_router_w, L1_ffn_router_b, L1_ffn_w1, L1_ffn_b1, L1_ffn_w2, L1_ffn_b2)
    return x

_drawn_inputs = setup_inputs


def setup_inputs(seed=0):
    import zlib

    import numpy as np

    out = dict(_drawn_inputs(seed))
    spreads = {'L0_attn_ln_g': (1.0, 0.6),
     'L0_attn_ln_b': (0.0, 0.8),
     'L0_ffn_rb1': (0.0, 0.1),
     'L0_ffn_rb2': (0.0, 0.1),
     'L0_ffn_eb1': (0.0, 0.696),
     'L0_ffn_eb2': (0.0, 0.1),
     'L1_attn_ln_w': (1.0, 0.6),
     'L1_attn_ln_b': (0.0, 0.8),
     'L1_attn_gk_b2': (0.0, 0.8),
     'L1_attn_rms_w': (1.0, 0.6),
     'L1_attn_b1': (0.0, 0.8),
     'L1_attn_b2': (0.0, 0.1),
     'L1_ffn_router_b': (0.0, 0.474),
     'L1_ffn_b1': (0.0, 0.8),
     'L1_ffn_b2': (0.0, 0.318)}
    factors = {'L0_attn_Wbeta': 8.0,
     'L1_attn_Wq': 3.792,
     'L1_attn_Wk': 3.812,
     'L1_attn_Wv': 3.807,
     'L1_attn_gk_w1': 8.0,
     'L1_attn_gk_w2': 8.0,
     'L1_attn_Wg': 3.837,
     'L1_attn_Wo': 3.767,
     'L1_attn_W1': 2.895,
     'L1_attn_W2': 2.718,
     'L1_ffn_w1': 5.975,
     'L1_ffn_w2': 5.411}
    for name, (base, spread) in spreads.items():
        noise = np.random.default_rng([zlib.crc32(name.encode()), seed]).standard_normal(out[name].shape)
        drawn = base * np.exp(spread * noise) if base else spread * noise
        out[name] = jnp.asarray(drawn.astype(out[name].dtype))
    for name, factor in factors.items():
        out[name] = (out[name] * factor).astype(out[name].dtype)
    return out
```

```python
import concourse.bass as bass
from concourse import mybir
from contextlib import ExitStack


class Steps:

    def __init__(self, eng, sem):
        self.eng, self.sem, self.count = eng, sem, 0

    def done(self, ins):
        ins.then_inc(self.sem, 1)
        self.count += 1
        self.eng.wait_ge(self.sem, self.count)


def build(nc, I, out):
    f32, f16, i32, u32 = mybir.dt.float32, mybir.dt.float16, mybir.dt.int32, mybir.dt.uint32
    ALU = mybir.AluOpType
    ACT = mybir.ActivationFunctionType
    AX = mybir.AxisListType.X
    MUL, ADD, SUB, MAX = ALU.mult, ALU.add, ALU.subtract, ALU.max

    B, T, C = I["L0_attn_x"].shape
    NT = T // 128
    TILES = B * NT
    H = 16
    D = C // H
    DK = 4
    E0, CAP, HC0 = 8, 512, 4
    E1, TOP1, HC1 = 16, 4, 2
    EPS = 1e-5
    GATE_NORM = 16.0
    bts = bass.ts

    ctx = ExitStack()
    with ctx:
        def sb(name, shape, dt=f32):
            return ctx.enter_context(nc.sbuf_tensor(name, shape, dt))

        def sem(name):
            return ctx.enter_context(nc.semaphore(name))

        resid = sb("resid", [128, TILES, C])
        A = [sb(f"A{n}", [128, B * T]) for n in range(1, 8)]
        A1, A2, A3, A4, A5, A6, A7 = A
        scratch = sb("scratch", [128, 11 * 1024])

        def carve(k, n=1):
            return scratch[:, k * 1024:(k + n) * 1024]

        ident = sb("ident", [128, 128])
        ones = sb("ones", [128, 128])
        center = sb("center", [128, 128])
        tri = sb("tri", [128, 128])
        headsum = sb("headsum", [128, 240])
        expand = sb("expand", [128, B, 128])
        meanrow = sb("meanrow", [128, 15])
        spread = sb("spread", [8, B, 128])
        pick = sb("pick", [128, D, 128], f16)
        pickg = sb("pickg", [128, 2, DK, 128], f16)
        iota_i = sb("iota_i", [128, E1], i32)
        iota = sb("iota", [128, E1])
        epsc = sb("epsc", [128, 1])

        rows = sb("rows", [76, 128])
        cols = sb("cols", [128, 76])
        brow = sb("brow", [1, 152])
        bcast = sb("bcast", [128, 152])
        LNG, LNB, RB1, EB1, LNW1, LNB1, AB1, MB1, GKB, RMSW = 0, 1, 2, 6, 38, 39, 40, 42, 74, 75

        w_q, w_k, w_v, w_g, w_o = (sb(n, [128, 128]) for n in ("w_q", "w_k", "w_v", "w_g", "w_o"))
        w_b = sb("w_b", [128, H])
        w_brep = sb("w_brep", [128, 128])
        w_r1 = sb("w_r1", [128, 512])
        w_r2 = sb("w_r2", [128, HC0, E0])
        eb2 = sb("eb2", [E0, C])
        u_q, u_k = sb("u_q", [128, 64]), sb("u_k", [128, 64])
        u_v, u_g, u_o = (sb(n, [128, 128]) for n in ("u_v", "u_g", "u_o"))
        u_qrep, u_krep = sb("u_qrep", [128, DK, 128]), sb("u_krep", [128, DK, 128])
        u_gk1, u_gk2 = sb("u_gk1", [128, 16]), sb("u_gk2", [16, 64])
        u_1, u_2 = sb("u_1", [128, 256]), sb("u_2", [128, 2, C])
        u_r = sb("u_r", [128, E1])
        mb2 = sb("mb2", [E1, C])

        stats = sb("stats", [128, TILES, 6])
        mean = sb("mean", [128, TILES])
        var = sb("var", [128, TILES])
        rstd = sb("rstd", [128, TILES])
        tmpa = sb("tmpa", [128, TILES])
        tmpb = sb("tmpb", [128, TILES])
        coef1 = sb("coef", [128, TILES, E1])
        coef0 = coef1[:, :, 0:E0]

        PS = ctx.enter_context(nc.psum_tensor("PS", [128, 8, 512], f32))

        def bank(n, k=1):
            return PS[:, n, :] if k == 1 else PS[:, n:n + k, :]

        HEAD = 4

        def at(n, k=0):
            return n + (HEAD + 1 - k)

        SIGNALS = {
            "pool": ["bk_ready", "bk_low", "r0_c", "r1_c", "yg_ready"],
            "act": ["xT1", "q_copied", "k_copied", "beta", "sgm1", "sq_k", "q_high", "bk_high",
                    "r0_coef", "r0_decay", "r0_o", "o_sq", "xT5", "hid5",
                    "m0_cs", "m0_cT", "m0_hid", "m1_cs", "m1_cT", "m1_hid",
                    "hT7", "g1", "gk_copied", "sgm7", "r1_coef", "r1_o", "o1_sq", "hT11", "hid11",
                    "xs12", "xs_copied"],
            "dve": ["stats0", "xn1", "v_copied", "sg_1", "bk_in", "q_norm", "r0_kk", "r0_scanned", "r0_prod",
                    "y_raw", "y_ready", "x_added", "stats4", "xn5", "lg5_added", "m0_bias", "m0_acc", "m0_stats",
                    "m1_bias", "m1_acc", "z_ready", "z_stats", "xn7", "v_copied7", "sg_7",
                    "r1_scanned", "r1_prod", "y1_raw", "yg1_ready", "z_added", "stats10",
                    "xn11", "x_z", "x_b2", "mlp_added", "stats11", "xn12", "lg12_added"],
            "pe": ["tr1", "proj_q", "proj_k", "proj_b", "proj_g", "proj_v", "ss_k", "rk_mm", "rq_mm",
                   "r0_bk", "r0_q", "r0_acc", "centred", "o_var", "o_spread", "proj_o",
                   "tr5", "hid5_mm", "lg5_mm",
                   "m0_cT_mm", "m0_hid_mm", "m0_out_mm", "m0_bias_mm", "m1_cT_mm", "m1_hid_mm", "m1_out_mm", "m1_bias_mm",
                   "tr7", "v_mm7", "g_mm7", "g1_mm", "gk_mm", "r1_k", "r1_e", "r1_q", "r1_acc",
                   "rms_mm", "rms_spread", "proj_o1", "tr11", "hid11_mm", "mlp_mm", "tr12", "lg12_mm"],
        }
        signals = {n: sem(n) for v in SIGNALS.values() for n in v}

        def S(name):
            return signals[name]

        def start_signals(eng, who):
            for n in SIGNALS[who]:
                eng.sem_inc(S(n), HEAD)

        stage_done, s_x, s_w, s_wm0, s_wm1, s_out = (
            sem(n) for n in ("stage_done", "x_loaded", "w_loaded", "moe0_loaded", "moe1_loaded", "out_written"))
        s_const, s_colsT, s_cols = sem("consts_ready"), sem("cols_transposed"), sem("cols_ready")
        s_nrm, s_rn, s_ostd, s_orstd = sem("norms"), sem("norm_reciprocals"), sem("o_std"), sem("o_rstd")
        s_diff, s_exp, s_mask, s_counts = (sem("rt5_" + n) for n in ("diff", "exp", "mask", "counts"))
        s_ln, s_log, s_high = (sem("gate_" + n) for n in ("ln", "log", "high"))
        s_rms, s_rmsr, s_sub, s_exp12 = sem("rms_std"), sem("rms_reciprocal"), sem("rt12_sub"), sem("rt12_exp")
        s_dve = sem("dve_steps")
        s_act = sem("act_steps8")
        s_pool = sem("pool_steps0")
        s_var, s_std = sem("token_variances"), sem("token_deviations")

        def stage_end(eng, k):
            eng.drain().then_inc(stage_done, 1)
            eng.wait_ge(stage_done, 4 * (k + 1))

        q0, k0, v0, sg0, bk0 = A1, A2, A3, A4, A5
        q_hl = A6[:, :].bitcast(f16).rearrange("p (s n) -> p s n", s=2)
        bk_hl = A7[:, :].bitcast(f16).rearrange("p (s n) -> p s n", s=2)
        o0 = A1
        xT0 = A2
        e0w1 = A6[:, :].rearrange("p (e h) -> p e h", e=E0)
        e0w2 = A7[:, :].rearrange("p (e i c) -> p e i c", e=E0, c=C)
        z = A1[:, :].rearrange("p (n c) -> p n c", c=C)
        hT1, v1, sg1 = A2, A3, A4
        gate = A5[:, 0:2048]
        gate_hl = A5[:, 2048:4096].bitcast(f16).rearrange("p (s n) -> p s n", s=2)
        o1 = A3
        xT1 = A2
        e1w1 = A6[:, :].rearrange("p (e h) -> p e h", e=E1)
        e1w2 = A7[:, :].rearrange("p (e i c) -> p e i c", e=E1, c=C)

        xn = [carve(0)[:, u * 512:(u + 1) * 512].rearrange("p (n c) -> p n c", c=C) for u in range(2)]
        xT = [carve(1)[:, u * 512:(u + 1) * 512] for u in range(2)]
        sgm = [carve(2)[:, u * 512:(u + 1) * 512] for u in range(2)]

        def pair(k):
            return carve(k).rearrange("p (j t) -> p j t", j=2)

        cs = [pair(0), pair(1)]
        kk = [pair(2), pair(3)]
        decay = [pair(4), pair(5)]
        cbuf = [pair(6), pair(7)]
        state = pair(8)
        prod = [pair(9), pair(10)]

        def halves(k):
            return [carve(k)[:, u * 512:(u + 1) * 512] for u in range(2)]

        y = halves(3)
        yg = halves(4)
        sq = halves(5)
        sqk = halves(6)
        nrm = carve(7)
        rn = carve(8)
        hid = [carve(2 * u + 2, 2).rearrange("p (i t) -> p i t", i=4) for u in range(2)]
        cstage = carve(6)[:, 0:64].rearrange("p (n e) -> p n e", n=4)
        cT = carve(7)[0:16, 0:512]
        g1s = carve(7)[0:16, 0:512]
        hT2 = halves(8)
        logits = carve(9)[:, 0:512].rearrange("p (n e) -> p n e", n=TILES)
        ga, gb, gm = (scratch[:, 2048 * k:2048 * (k + 1)] for k in range(3))

        top = carve(10)[:, 0:256].rearrange("p (n e) -> p n e", e=8)
        idx = carve(10)[:, 256:512].bitcast(u32).rearrange("p (n e) -> p n e", e=8)
        idf = carve(10)[:, 512:640].rearrange("p (n e) -> p n e", e=4)
        oh0, oh1, picked, place = (carve(8)[:, k * 256:(k + 1) * 256].rearrange("p (n e) -> p n e", e=E0)
                                   for k in range(4))
        oh, ohw = (carve(8)[:, k * 512:(k + 1) * 512].rearrange("p (n e) -> p n e", e=E1) for k in range(2))

        block = ctx.enter_context(nc.Block())

        @block.sync
        def _(sp):
            xv = I["L0_attn_x"].rearrange("b (n p) c -> b p n c", p=128)
            for b in range(B):
                sp.dma_start(resid[:, b * NT:(b + 1) * NT, :], xv[b]).then_inc(s_x, 16)
            count = 0

            def load(dst, src):
                nonlocal count
                sp.dma_start(dst, src).then_inc(s_w, 16)
                count += 1

            def row(v, n=128):
                return v.rearrange("(a n) -> a n", n=n)

            load(w_q[:, :], I["L0_attn_Wq"])
            load(w_k[:, :], I["L0_attn_Wk"])
            load(w_v[:, :], I["L0_attn_Wv"])
            load(w_g[:, :], I["L0_attn_Wg"])
            load(w_b[:, :], I["L0_attn_Wbeta"])
            load(w_o[:, :], I["L0_attn_Wout"])
            load(rows[LNG:LNG + 1, :], row(I["L0_attn_ln_g"]))
            load(rows[LNB:LNB + 1, :], row(I["L0_attn_ln_b"]))
            load(rows[RB1:RB1 + 4, :], row(I["L0_ffn_rb1"]))
            load(rows[EB1:EB1 + 32, :], I["L0_ffn_eb1"].rearrange("e (i n) -> (e i) n", n=128))
            load(rows[LNW1:LNW1 + 1, :], row(I["L1_attn_ln_w"]))
            load(rows[LNB1:LNB1 + 1, :], row(I["L1_attn_ln_b"]))
            load(rows[AB1:AB1 + 2, :], row(I["L1_attn_b1"]))
            load(rows[MB1:MB1 + 32, :], I["L1_ffn_b1"].rearrange("e (i n) -> (e i) n", n=128))
            for k in range(2):
                load(rows[GKB:GKB + 1, 64 * k:64 * k + 64], row(I["L1_attn_gk_b2"], 64))
            load(rows[RMSW:RMSW + 1, :].rearrange("a (h v) -> a h v", v=D),
                 row(I["L1_attn_rms_w"], D).unsqueeze(1).to_broadcast([1, H, D]))
            load(brow[:, 0:8], row(I["L0_ffn_rb2"], 8))
            load(brow[:, 8:24], row(I["L1_ffn_router_b"], 16))
            load(brow[:, 24:152], row(I["L1_attn_b2"]))
            load(w_r1[:, :], I["L0_ffn_rw1"])
            load(w_r2[:, :, :], I["L0_ffn_rw2"].rearrange("(i p) e -> p i e", p=128))
            load(eb2[:, :], I["L0_ffn_eb2"])
            load(u_q[:, :], I["L1_attn_Wq"])
            load(u_k[:, :], I["L1_attn_Wk"])
            load(u_v[:, :], I["L1_attn_Wv"])
            load(u_g[:, :], I["L1_attn_Wg"])
            load(u_o[:, :], I["L1_attn_Wo"])
            load(u_gk1[:, :], I["L1_attn_gk_w1"])
            load(u_gk2[:, :], I["L1_attn_gk_w2"])
            load(u_1[:, :], I["L1_attn_W1"])
            load(u_2[:, :, :], I["L1_attn_W2"].rearrange("(i p) c -> p i c", p=128))
            load(u_r[:, :], I["L1_ffn_router_w"])
            load(mb2[:, :], I["L1_ffn_b2"])
            assert count == W_LOADS
            sp.wait_ge(stage_done, 4 * 4)
            sp.dma_start(e0w1, I["L0_ffn_ew1"].rearrange("e c h -> c e h")).then_inc(s_wm0, 16)
            sp.dma_start(e0w2, I["L0_ffn_ew2"].rearrange("e (i p) c -> p e i c", p=128)).then_inc(s_wm0, 16)
            sp.wait_ge(stage_done, 4 * 7)
            sp.dma_start(e1w1, I["L1_ffn_w1"].rearrange("e c h -> c e h")).then_inc(s_wm1, 16)
            sp.dma_start(e1w2, I["L1_ffn_w2"].rearrange("e (i p) c -> p e i c", p=128)).then_inc(s_wm1, 16)
            ov = out.rearrange("b (n p) c -> b p n c", p=128)
            for b in range(B):
                sp.wait_ge(S("m1_acc"), at((b + 1) * E1 - 1))
                sp.dma_start(ov[b], resid[:, b * NT:(b + 1) * NT, :]).then_inc(s_out, 16)
            sp.wait_ge(s_out, 16 * B)

        @block.gpsimd
        def _(pool):
            start_signals(pool, "pool")
            st = Steps(pool, s_pool)
            pool.memset(epsc[:, :], EPS)
            pool.memset(ident[:, :], 0.0)
            pool.memset(ones[:, :], 1.0)
            pool.memset(center[:, :], -1.0 / C)
            pool.memset(tri[:, :], 1.0)
            pool.memset(headsum[:, :], 1.0)
            pool.memset(expand[:, :, :], 0.0)
            pool.memset(meanrow[:, :], 0.0)
            pool.memset(spread[:, :, :], 0.0)
            pool.memset(pick[:, :, :], 0.0)
            pool.iota(iota_i[:, :], pattern=[[1, E1]], base=0, channel_multiplier=0)
            st.done(pool.memset(pickg[:, :, :, :], 0.0))
            sel = pool.affine_select
            sel(out=ident[:, :], in_=ident[:, :], compare_op=ALU.not_equal, fill=1.0, base=0,
                pattern=[[-1, 128]], channel_multiplier=1)
            sel(out=center[:, :], in_=center[:, :], compare_op=ALU.not_equal, fill=1.0 - 1.0 / C, base=0,
                pattern=[[-1, 128]], channel_multiplier=1)
            sel(out=tri[:, :], in_=tri[:, :], compare_op=ALU.is_gt, fill=0.0, base=0,
                pattern=[[1, 128]], channel_multiplier=-1)
            sel(out=headsum[:, :], in_=headsum[:, :], compare_op=ALU.is_ge, fill=0.0, base=112 * D,
                pattern=[[-D, 240]], channel_multiplier=1)
            sel(out=expand[:, :, :].rearrange("p b (h i) -> p b h i", i=D),
                in_=expand[:, :, :].rearrange("p b (h i) -> p b h i", i=D),
                compare_op=ALU.not_equal, fill=1.0, base=0, pattern=[[-H, B], [-1, H], [0, D]], channel_multiplier=1)
            sel(out=spread[:, :, :], in_=spread[:, :, :], compare_op=ALU.not_equal, fill=1.0, base=0,
                pattern=[[-1, B], [0, 128]], channel_multiplier=1)
            pool.memset(meanrow[:, 7:8], 1.0 / C)
            sel(out=pick[:, :, :].rearrange("p j (h i) -> p j h i", i=D),
                in_=pick[:, :, :].rearrange("p j (h i) -> p j h i", i=D),
                compare_op=ALU.not_equal, fill=1.0, base=0, pattern=[[-1, D], [-D, H], [0, D]], channel_multiplier=1)
            for u in range(2):
                sel(out=pickg[:, u, :, :].rearrange("p k (h i) -> p k h i", i=D),
                    in_=pickg[:, u, :, :].rearrange("p k (h i) -> p k h i", i=D),
                    compare_op=ALU.not_equal, fill=1.0, base=-64 * u, pattern=[[-1, DK], [-DK, H], [0, D]],
                    channel_multiplier=1)
            st.done(pool.tensor_copy(iota[:, :], iota_i[:, :]))
            sel(out=headsum[:, :], in_=headsum[:, :], compare_op=ALU.is_ge, fill=0.0, base=D - 1 - 112 * D,
                pattern=[[D, 240]], channel_multiplier=-1).then_inc(s_const, 1)
            stage_end(pool, 0)
            stage_end(pool, 1)

            for b in range(B):
                c = bts(b, T)
                pool.wait_ge(S("bk_in"), at(b))
                pool.tensor_tensor(bk0[:, c], k0[:, c], bk0[:, c], MUL).then_inc(S("bk_ready"), 1)
                pool.wait_ge(S("q_high"), at(b))
                pool.tensor_tensor(q_hl[:, 1, c], q0[:, c], q_hl[:, 0, c], SUB)
                pool.wait_ge(S("bk_high"), at(b))
                pool.wait_ge(S("bk_ready"), at(b))
                pool.tensor_tensor(bk_hl[:, 1, c], bk0[:, c], bk_hl[:, 0, c], SUB)
            stage_end(pool, 2)

            def additions(pre, v, pairs):
                for b in range(B):
                    for p in range(pairs):
                        n = b * pairs + p
                        pool.wait_ge(S(pre + "coef"), at(n))
                        pool.wait_ge(S(pre + "scanned"), at(n, 2))
                        pool.tensor_tensor(cbuf[p % 2], cs[p % 2],
                                           v[:, bts(b, T)].unsqueeze(1).to_broadcast([128, 2, T]),
                                           MUL).then_inc(S(pre + "c"), 1)

            additions("r0_", v0, D // 2)
            stage_end(pool, 3)

            for b in range(B):
                u = b % 2
                pool.wait_ge(S("y_ready"), at(b))
                pool.wait_ge(S("proj_o"), at(b, 2))
                pool.tensor_tensor(yg[u], y[u], sg0[:, bts(b, T)], MUL).then_inc(S("yg_ready"), 1)
            for k in range(4, 9):
                stage_end(pool, k)
            additions("r1_", v1, DK // 2)
            for k in range(9, 13):
                stage_end(pool, k)
            pool.drain().then_inc(stage_done, 1)

        @block.scalar
        def _(act):
            A_ = nc.scalar.activation

            def norm_std(n):
                act.wait_ge(s_var, n + 1)
                A_(rstd[:, :], var[:, :], ACT.Sqrt, bias=epsc[:, 0:1]).then_inc(s_std, 1)

            start_signals(act, "act")
            act.wait_ge(s_const, 1)
            act.wait_ge(s_colsT, 1)
            A_(cols[:, :], bank(0)[:, 0:76], ACT.Copy)
            A_(bcast[:, :], bank(1)[:, 0:152], ACT.Copy)
            norm_std(0)
            stage_end(act, 0)

            with act.Fori(0, B // 2) as i:
                for u in range(2):
                    b = 2 * i + u
                    c = bts(b, T)
                    act.wait_ge(S("tr1"), at(b))
                    act.wait_ge(S("proj_v"), at(b, 2))
                    A_(xT[u], bank(u), ACT.Copy).then_inc(S("xT1"), 1)
                    act.wait_ge(S("proj_q"), at(b))
                    A_(q0[:, c], bank(2), ACT.Copy).then_inc(S("q_copied"), 1)
                    act.wait_ge(S("proj_k"), at(b))
                    A_(k0[:, c], bank(3), ACT.Copy).then_inc(S("k_copied"), 1)
                    act.wait_ge(S("proj_b"), at(b))
                    A_(bk0[:, c], bank(6), ACT.Sigmoid).then_inc(S("beta"), 1)
                    act.wait_ge(S("proj_g"), at(b))
                    act.wait_ge(S("sg_1"), at(b, 2))
                    A_(sgm[u], bank(5), ACT.Sigmoid).then_inc(S("sgm1"), 1)
            stage_end(act, 1)

            for b in range(B):
                act.wait_ge(S("ss_k"), at(b, 2))
                A_(sq[b % 2], q0[:, bts(b, T)], ACT.Square)
                A_(sqk[b % 2], k0[:, bts(b, T)], ACT.Square).then_inc(S("sq_k"), 1)
            act.wait_ge(S("ss_k"), at(B - 1))
            A_(nrm[:, 0:512], bank(0), ACT.Sqrt).then_inc(s_nrm, 1)
            A_(nrm[:, 512:1024], bank(1), ACT.Sqrt).then_inc(s_nrm, 1)
            for b in range(B):
                c = bts(b, T)
                act.wait_ge(S("q_norm"), at(b))
                A_(q_hl[:, 0, c], q0[:, c], ACT.Copy).then_inc(S("q_high"), 1)
                act.wait_ge(S("bk_ready"), at(b))
                A_(bk_hl[:, 0, c], bk0[:, c], ACT.Copy).then_inc(S("bk_high"), 1)
            stage_end(act, 2)

            def outputs(pre, dst, b, u, pairs):
                act.wait_ge(S(pre + "acc"), at(b * pairs + pairs - 1))
                A_(dst[:, bts(b, T)], bank(6 + u), ACT.Copy).then_inc(S(pre + "o"), 1)

            def decays(b, u, first):
                for p in range(D // 2):
                    n = b * (D // 2) + p
                    act.wait_ge(S("r0_bk"), at(n))
                    act.wait_ge(S("r0_c"), at(n, 2))
                    act.wait_ge(S("r0_kk"), at(n, 2))
                    A_(cs[p % 2], bank(2 * (p % 2), 2), ACT.Copy).then_inc(S("r0_coef"), 1)
                    act.wait_ge(S("r0_kk"), at(n))
                    act.wait_ge(S("r0_scanned"), at(n, 2))
                    A_(decay[p % 2], kk[p % 2], ACT.Identity, scale=-1.0, bias=1.0).then_inc(S("r0_decay"), 1)
                    if p == 1 and not first:
                        outputs("r0_", o0, b - 1, 1 - u, D // 2)

            decays(0, 0, True)
            decays(1, 1, False)
            with act.Fori(1, B // 2) as i:
                for u in range(2):
                    decays(2 * i + u, u, False)
            outputs("r0_", o0, B - 1, 1, D // 2)
            stage_end(act, 3)

            for b in range(B):
                act.wait_ge(S("centred"), at(b))
                act.wait_ge(S("o_var"), at(b, 2))
                A_(o0[:, bts(b, T)], bank(b % 2), ACT.Copy)
                A_(sq[b % 2], bank(b % 2), ACT.Square).then_inc(S("o_sq"), 1)
            act.wait_ge(S("o_var"), at(B - 1))
            A_(nrm[0:B, 0:512], bank(2)[0:B, :], ACT.Sqrt, bias=epsc[0:B, 0:1]).then_inc(s_ostd, 1)
            norm_std(1)
            stage_end(act, 4)

            with act.Fori(0, B // 2) as i:
                for u in range(2):
                    b = 2 * i + u
                    act.wait_ge(S("tr5"), at(b))
                    A_(xT0[:, bts(b, T)], bank(u), ACT.Copy).then_inc(S("xT5"), 1)
                    act.wait_ge(S("lg5_mm"), at(b, 2))
                    for h in range(HC0):
                        act.wait_ge(S("hid5_mm"), at(b * HC0 + h))
                        A_(hid[u][:, h, :], bank(2 + h), ACT.Relu,
                           bias=cols[:, RB1 + h:RB1 + h + 1]).then_inc(S("hid5"), 1)
            act.wait_ge(s_diff, 1)
            A_(tmpb[:, :], tmpa[:, :], ACT.Exp).then_inc(s_exp, 1)
            stage_end(act, 5)

            def experts(pre, E, HC, coef, func, bias0):
                with act.Fori(0, B) as b:
                    act.wait_ge(S(pre + "cT_mm"), at(b, 1))
                    A_(cstage[:, :, 0:E], coef[:, bts(b, NT), :], ACT.Copy).then_inc(S(pre + "cs"), 1)
                    act.wait_ge(S(pre + "cT_mm"), at(b))
                    act.wait_ge(S(pre + "bias_mm"), at(b, 1))
                    A_(cT[0:E, :], bank(6)[0:E, :], ACT.Copy).then_inc(S(pre + "cT"), 1)
                    for e in range(E):
                        n = b * E + e
                        act.wait_ge(S(pre + "out_mm"), at(n, 2))
                        for h in range(HC):
                            act.wait_ge(S(pre + "hid_mm"), at(n * HC + h))
                            A_(hid[e % 2][:, h, :], bank((e * HC + h) % 4), func,
                               bias=cols[:, bias0 + e * HC + h:bias0 + e * HC + h + 1]).then_inc(S(pre + "hid"), 1)

            experts("m0_", E0, HC0, coef0, ACT.Relu, EB1)
            norm_std(2)
            stage_end(act, 6)

            norm_std(3)
            with act.Fori(0, B // 2) as i:
                for u in range(2):
                    b = 2 * i + u
                    half = slice(64 * u, 64 * u + 64)
                    act.wait_ge(S("tr7"), at(b))
                    A_(hT1[:, bts(b, T)], bank(u), ACT.Identity, scale=cols[:, LNW1:LNW1 + 1],
                       bias=cols[:, LNB1:LNB1 + 1]).then_inc(S("hT7"), 1)
                    act.wait_ge(S("g1_mm"), at(b))
                    act.wait_ge(S("gk_mm"), at(b, 1))
                    A_(g1s, bank(4)[0:16, :], ACT.Copy).then_inc(S("g1"), 1)
                    act.wait_ge(S("gk_mm"), at(b))
                    A_(gate[half, bts(i, T)], bank(5)[half, :], ACT.Identity,
                       bias=cols[half, GKB:GKB + 1]).then_inc(S("gk_copied"), 1)
                    act.wait_ge(S("g_mm7"), at(b))
                    act.wait_ge(S("sg_7"), at(b, 2))
                    A_(sgm[u], bank(3), ACT.Sigmoid).then_inc(S("sgm7"), 1)
            stage_end(act, 7)

            st = Steps(act, s_act)
            st.done(A_(ga, gate, ACT.Abs))
            st.done(A_(gb, ga, ACT.Exp, scale=-1.0))
            A_(ga, gb, ACT.Ln, bias=1.0).then_inc(s_ln, 1)
            act.wait_ge(s_log, 1)
            st.done(A_(gate, gb, ACT.Exp, scale=1.0 / GATE_NORM))
            A_(gate_hl[:, 0, :], gate, ACT.Copy).then_inc(s_high, 1)
            stage_end(act, 8)

            def keys(b, u, first):
                for p in range(DK // 2):
                    n = b * (DK // 2) + p
                    act.wait_ge(S("r1_k"), at(n))
                    act.wait_ge(S("r1_c"), at(n, 2))
                    A_(cs[p % 2], bank(0, 2), ACT.Copy).then_inc(S("r1_coef"), 1)
                    if p == 1 and not first:
                        outputs("r1_", o1, b - 1, 1 - u, DK // 2)

            keys(0, 0, True)
            keys(1, 1, False)
            with act.Fori(1, B // 2) as i:
                for u in range(2):
                    keys(2 * i + u, u, False)
            outputs("r1_", o1, B - 1, 1, DK // 2)
            stage_end(act, 9)

            for b in range(B):
                act.wait_ge(S("rms_mm"), at(b, 2))
                A_(sq[b % 2], o1[:, bts(b, T)], ACT.Square).then_inc(S("o1_sq"), 1)
            act.wait_ge(S("rms_mm"), at(B - 1))
            A_(nrm[:, 0:512], bank(0), ACT.Sqrt, scale=1.0 / D, bias=epsc[:, 0:1]).then_inc(s_rms, 1)
            norm_std(4)
            stage_end(act, 10)

            with act.Fori(0, B // 2) as i:
                for u in range(2):
                    b = 2 * i + u
                    act.wait_ge(S("tr11"), at(b))
                    act.wait_ge(S("hid11_mm"), at(2 * b + 1, 4))
                    A_(hT2[u], bank(u), ACT.Identity, scale=cols[:, LNW1:LNW1 + 1],
                       bias=cols[:, LNB1:LNB1 + 1]).then_inc(S("hT11"), 1)
                    act.wait_ge(S("mlp_mm"), at(b, 2))
                    for h in range(2):
                        act.wait_ge(S("hid11_mm"), at(2 * b + h))
                        A_(hid[u][:, h, :], bank(2 + h), ACT.Gelu,
                           bias=cols[:, AB1 + h:AB1 + h + 1]).then_inc(S("hid11"), 1)
            norm_std(5)
            stage_end(act, 11)

            with act.Fori(0, B // 2) as i:
                for u in range(2):
                    b = 2 * i + u
                    act.wait_ge(S("tr12"), at(b))
                    act.wait_ge(S("lg12_mm"), at(b, 2))
                    A_(xT[u], bank(u), ACT.Copy).then_inc(S("xs12"), 1)
                    act.wait_ge(S("xs12"), at(b))
                    A_(xT1[:, bts(b, T)], xT[u], ACT.Copy).then_inc(S("xs_copied"), 1)
            act.wait_ge(s_sub, 1)
            A_(coef1[:, :, :], logits, ACT.Exp).then_inc(s_exp12, 1)
            stage_end(act, 12)

            experts("m1_", E1, HC1, coef1, ACT.Gelu, MB1)
            act.drain().then_inc(stage_done, 1)

        @block.vector
        def _(dve):
            V = nc.vector
            TT, TS, STT = V.tensor_tensor, V.tensor_scalar, V.scalar_tensor_tensor

            def tile_stats(src, b):
                for t in range(NT):
                    last = V.bn_stats(stats[:, b * NT + t, :], src[:, b * NT + t, :])
                return last

            def norm_scalars(st, n):
                me, mo, ve, vo = (stats[:, :, k] for k in (1, 4, 2, 5))
                TT(tmpb[:, :], me, mo, SUB)
                TT(var[:, :], ve, vo, ADD)
                st.done(TT(tmpa[:, :], me, mo, ADD))
                TS(mean[:, :], tmpa[:, :], 0.5, None, MUL)
                st.done(STT(out=tmpb[:, :], in0=tmpb[:, :], scalar=0.25, in1=tmpb[:, :], op0=MUL, op1=MUL))
                STT(out=var[:, :], in0=var[:, :], scalar=1.0 / C, in1=tmpb[:, :], op0=MUL, op1=ADD).then_inc(s_var, 1)
                dve.wait_ge(s_std, n + 1)
                st.done(V.reciprocal(rstd[:, :], rstd[:, :]))

            def normalise(dst, src, b):
                for t in range(NT):
                    g = b * NT + t
                    last = TS(dst(t), src[:, g, :], mean[:, bass.ds(g, 1)], rstd[:, bass.ds(g, 1)], SUB, MUL)
                return last

            start_signals(dve, "dve")
            st = Steps(dve, s_dve)
            dve.wait_ge(s_x, 16 * B)
            with dve.Fori(0, B) as b:
                tile_stats(resid, b).then_inc(S("stats0"), 1)
            dve.wait_ge(S("stats0"), at(B - 1))
            dve.wait_ge(s_const, 1)
            norm_scalars(st, 0)
            dve.wait_ge(s_w, 16 * W_LOADS)
            V.tensor_copy(w_brep[:, :].rearrange("p (h i) -> p h i", i=D),
                          w_b[:, :].unsqueeze(2).to_broadcast([128, H, D]))
            for k in range(DK):
                V.tensor_copy(u_krep[:, k, :].rearrange("p (h i) -> p h i", i=D),
                              u_k[:, :].rearrange("p (h k) -> p k h", k=DK)[:, k, :].unsqueeze(2).to_broadcast([128, H, D]))
                TS(u_qrep[:, k, :].rearrange("p (h i) -> p h i", i=D),
                   u_q[:, :].rearrange("p (h k) -> p k h", k=DK)[:, k, :].unsqueeze(2).to_broadcast([128, H, D]),
                   float(DK) ** -0.5, None, MUL)
            stage_end(dve, 0)

            with dve.Fori(0, B // 2) as i:
                for u in range(2):
                    b = 2 * i + u
                    c = bts(b, T)
                    dve.wait_ge(S("tr1"), at(b, 2))
                    normalise(lambda t: xn[u][:, t, :], resid, b).then_inc(S("xn1"), 1)
                    dve.wait_ge(S("sgm1"), at(b))
                    TT(sg0[:, c], bank(5), sgm[u], MUL).then_inc(S("sg_1"), 1)
                    dve.wait_ge(S("proj_v"), at(b))
                    V.tensor_copy(v0[:, c], bank(4)).then_inc(S("v_copied"), 1)
            stage_end(dve, 1)

            for s in range(2):
                dve.wait_ge(s_nrm, s + 1)
                half = slice(512 * s, 512 * s + 512)
                st.done(TS(nrm[:, half], nrm[:, half], 1e-12, None, MAX))
                V.reciprocal(rn[:, half], nrm[:, half]).then_inc(s_rn, 1)
            for b in range(B):
                c = bts(b, T)
                dve.wait_ge(S("rk_mm"), at(b))
                TT(k0[:, c], k0[:, c], bank(4 + b % 2), MUL).then_inc(S("bk_in"), 1)
                dve.wait_ge(S("rq_mm"), at(b))
                TT(q0[:, c], q0[:, c], bank(2 + b % 2), MUL).then_inc(S("q_norm"), 1)
            stage_end(dve, 2)

            def beta_kk(b, p):
                n = b * (D // 2) + p
                dve.wait_ge(S("r0_coef"), at(n))
                dve.wait_ge(S("r0_decay"), at(n, 2))
                TT(kk[p % 2], cs[p % 2], k0[:, bts(b, T)].unsqueeze(1).to_broadcast([128, 2, T]),
                   MUL).then_inc(S("r0_kk"), 1)

            def scan(pre, n, p, decays):
                dve.wait_ge(S(pre + "c"), at(n))
                dve.wait_ge(S(pre + "prod"), at(n, 1))
                for j in range(2):
                    last = V.tensor_tensor_scan(out=state[:, j, :], data0=decays[:, j, :], data1=cbuf[p % 2][:, j, :],
                                                initial=0.0, op0=MUL, op1=ADD)
                last.then_inc(S(pre + "scanned"), 1)

            def read_out(pre, n, p):
                dve.wait_ge(S(pre + "scanned"), at(n))
                dve.wait_ge(S(pre + "q"), at(n))
                dve.wait_ge(S(pre + "acc"), at(n, 2))
                TT(prod[p % 2], bank(4, 2), state, MUL).then_inc(S(pre + "prod"), 1)

            def recur0(b, last):
                for p in range(D // 2):
                    n = b * (D // 2) + p
                    if p < D // 2 - 1:
                        beta_kk(b, p + 1)
                    elif not last:
                        beta_kk(b + 1, 0)
                    dve.wait_ge(S("r0_decay"), at(n))
                    scan("r0_", n, p, decay[p % 2])
                    read_out("r0_", n, p)

            beta_kk(0, 0)
            with dve.Fori(0, B - 1) as b:
                recur0(b, False)
            recur0(B - 1, True)
            stage_end(dve, 3)

            dve.wait_ge(s_ostd, 1)
            V.reciprocal(rn[0:B, 0:512], nrm[0:B, 0:512]).then_inc(s_orstd, 1)

            def add_projection(b, dst, proj, added, stat):
                u = b % 2
                dve.wait_ge(S(proj), at(b))
                xs = dst[:, b * NT:(b + 1) * NT, :]
                TT(xs, xs, bank(5 + u).rearrange("p (n c) -> p n c", c=C), ADD).then_inc(S(added), 1)
                dve.wait_ge(S(added), at(b))
                tile_stats(dst, b).then_inc(S(stat), 1)

            for b in range(B):
                u = b % 2
                dve.wait_ge(S("o_spread"), at(b))
                dve.wait_ge(S("yg_ready"), at(b, 2))
                TT(y[u], o0[:, bts(b, T)], bank(3 + u), MUL).then_inc(S("y_raw"), 1)
                dve.wait_ge(S("y_raw"), at(b))
                TS(y[u], y[u], cols[:, LNG:LNG + 1], cols[:, LNB:LNB + 1], MUL, ADD).then_inc(S("y_ready"), 1)
                if b >= 1:
                    add_projection(b - 1, resid, "proj_o", "x_added", "stats4")
            add_projection(B - 1, resid, "proj_o", "x_added", "stats4")
            dve.wait_ge(S("stats4"), at(B - 1))
            norm_scalars(st, 1)
            stage_end(dve, 4)

            with dve.Fori(0, B // 2) as i:
                for u in range(2):
                    b = 2 * i + u
                    dve.wait_ge(S("tr5"), at(b, 2))
                    normalise(lambda t: xn[u][:, t, :], resid, b).then_inc(S("xn5"), 1)
                    dve.wait_ge(S("lg5_mm"), at(b))
                    TT(logits[:, bts(b, NT), 0:E0], bank(6)[:, 0:NT * E0].rearrange("p (n e) -> p n e", e=E0),
                       bcast[:, 0:E0].unsqueeze(1).to_broadcast([128, NT, E0]), ADD).then_inc(S("lg5_added"), 1)

            def over(v, E):
                return v.unsqueeze(2).to_broadcast([128, TILES, E])

            def one_hot(dst, k, E):
                return TT(dst, iota[:, 0:E].unsqueeze(1).to_broadcast([128, TILES, E]), over(idf[:, :, k], E), ALU.is_equal)

            dve.wait_ge(S("lg5_added"), at(B - 1))
            for g in range(TILES):
                last = V.max(top[:, g, :], logits[:, g, 0:E0])
            st.done(last)
            TT(tmpa[:, :], top[:, :, 1], top[:, :, 0], SUB).then_inc(s_diff, 1)
            for g in range(TILES):
                last = V.max_index(idx[:, g, :], top[:, g, :], logits[:, g, 0:E0])
            st.done(last)
            st.done(V.tensor_copy(idf, idx[:, :, 0:4]))
            one_hot(oh0, 0, E0)
            st.done(one_hot(oh1, 1, E0))
            TT(picked, oh0, oh1, ADD).then_inc(s_mask, 1)
            dve.wait_ge(s_exp, 1)
            st.done(TS(tmpa[:, :], tmpb[:, :], 1.0, None, ADD))
            st.done(V.reciprocal(tmpa[:, :], tmpa[:, :]))
            TT(oh0, oh0, over(tmpa[:, :], E0), MUL)
            st.done(TT(tmpb[:, :], tmpb[:, :], tmpa[:, :], MUL))
            st.done(TT(oh1, oh1, over(tmpb[:, :], E0), MUL))
            TT(oh0, oh0, oh1, ADD)
            dve.wait_ge(s_counts, 1)
            before = bank(0)[:, 0:TILES * E0].rearrange("p (n e) -> p n e", e=E0)
            total = bank(1)[:, 0:TILES * E0].rearrange("p (n e) -> p n e", e=E0)
            for e in range(E0):
                last = V.tensor_tensor_scan(out=place[:, :, e], data0=ones[:, 0:TILES], data1=total[:, :, e],
                                            initial=0.0, op0=MUL, op1=ADD)
            st.done(last)
            st.done(TT(place, place, total, SUB))
            st.done(TT(place, place, before, ADD))
            STT(out=coef0, in0=place, scalar=float(CAP), in1=oh0, op0=ALU.is_lt, op1=MUL)
            stage_end(dve, 5)

            def combine(pre, E, coef, final):
                with dve.Fori(0, B) as b:
                    xs = resid[:, bts(b, NT), :]
                    dve.wait_ge(S(pre + "bias_mm"), at(b))
                    TT(xs, xs, bank(7).rearrange("p (n c) -> p n c", c=C), ADD).then_inc(S(pre + "bias"), 1)
                    dve.wait_ge(S(pre + "bias"), at(b))
                    for e in range(E):
                        n = b * E + e
                        dve.wait_ge(S(pre + "out_mm"), at(n))
                        for t in range(NT):
                            g = b * NT + t
                            last = STT(out=resid[:, g, :], in0=bank(4 + e % 2)[:, t * C:(t + 1) * C],
                                       scalar=coef[:, g, e:e + 1], in1=resid[:, g, :], op0=MUL, op1=ADD)
                        last.then_inc(S(pre + "acc"), 1)
                        dve.wait_ge(S(pre + "acc"), at(n))
                    if not final:
                        tile_stats(resid, b).then_inc(S(pre + "stats"), 1)

            combine("m0_", E0, coef0, False)
            dve.wait_ge(S("m0_stats"), at(B - 1))
            norm_scalars(st, 2)
            stage_end(dve, 6)

            with dve.Fori(0, B) as b:
                normalise(lambda t: z[:, b * NT + t, :], resid, b).then_inc(S("z_ready"), 1)
                dve.wait_ge(S("z_ready"), at(b))
                tile_stats(z, b).then_inc(S("z_stats"), 1)
            dve.wait_ge(S("z_stats"), at(B - 1))
            norm_scalars(st, 3)
            with dve.Fori(0, B // 2) as i:
                for u in range(2):
                    b = 2 * i + u
                    c = bts(b, T)
                    dve.wait_ge(S("tr7"), at(b, 2))
                    normalise(lambda t: xn[u][:, t, :], z, b).then_inc(S("xn7"), 1)
                    dve.wait_ge(S("v_mm7"), at(b))
                    V.tensor_copy(v1[:, c], bank(2)).then_inc(S("v_copied7"), 1)
                    dve.wait_ge(S("sgm7"), at(b))
                    TT(sg1[:, c], bank(3), sgm[u], MUL).then_inc(S("sg_7"), 1)
            stage_end(dve, 7)

            st.done(TS(gm, gate, 0.0, None, ALU.min))
            dve.wait_ge(s_ln, 1)
            TT(gb, gm, ga, SUB).then_inc(s_log, 1)
            dve.wait_ge(s_high, 1)
            TT(gate_hl[:, 1, :], gate, gate_hl[:, 0, :], SUB)
            stage_end(dve, 8)

            with dve.Fori(0, B) as b:
                for p in range(DK // 2):
                    n = b * (DK // 2) + p
                    dve.wait_ge(S("r1_e"), at(n))
                    scan("r1_", n, p, bank(2, 2))
                    read_out("r1_", n, p)
            stage_end(dve, 9)

            dve.wait_ge(s_rms, 1)
            V.reciprocal(rn[:, 0:512], nrm[:, 0:512]).then_inc(s_rmsr, 1)
            for b in range(B):
                u = b % 2
                dve.wait_ge(S("rms_spread"), at(b))
                TT(y[u], o1[:, bts(b, T)], bank(3 + u), MUL).then_inc(S("y1_raw"), 1)
                dve.wait_ge(S("y1_raw"), at(b))
                dve.wait_ge(S("proj_o1"), at(b, 2))
                STT(out=yg[u], in0=y[u], scalar=cols[:, RMSW:RMSW + 1], in1=sg1[:, bts(b, T)],
                    op0=MUL, op1=MUL).then_inc(S("yg1_ready"), 1)
                if b >= 1:
                    add_projection(b - 1, z, "proj_o1", "z_added", "stats10")
            add_projection(B - 1, z, "proj_o1", "z_added", "stats10")
            dve.wait_ge(S("stats10"), at(B - 1))
            norm_scalars(st, 4)
            stage_end(dve, 10)

            with dve.Fori(0, B // 2) as i:
                for u in range(2):
                    b = 2 * i + u
                    dve.wait_ge(S("tr11"), at(b, 2))
                    normalise(lambda t: xn[u][:, t, :], z, b).then_inc(S("xn11"), 1)
                    xs, zs = resid[:, bts(b, NT), :], z[:, bts(b, NT), :]
                    TT(xs, xs, zs, ADD).then_inc(S("x_z"), 1)
                    dve.wait_ge(S("x_z"), at(b))
                    TT(xs, xs, bcast[:, 24:152].unsqueeze(1).to_broadcast([128, NT, C]), ADD).then_inc(S("x_b2"), 1)
                    dve.wait_ge(S("x_b2"), at(b))
                    dve.wait_ge(S("mlp_mm"), at(b))
                    TT(xs, xs, bank(4 + u).rearrange("p (n c) -> p n c", c=C), ADD).then_inc(S("mlp_added"), 1)
                    dve.wait_ge(S("mlp_added"), at(b))
                    tile_stats(resid, b).then_inc(S("stats11"), 1)
            dve.wait_ge(S("stats11"), at(B - 1))
            norm_scalars(st, 5)
            stage_end(dve, 11)

            with dve.Fori(0, B // 2) as i:
                for u in range(2):
                    b = 2 * i + u
                    dve.wait_ge(S("tr12"), at(b, 2))
                    normalise(lambda t: xn[u][:, t, :], resid, b).then_inc(S("xn12"), 1)
                    dve.wait_ge(S("lg12_mm"), at(b))
                    TT(logits[:, bts(b, NT), :], bank(6)[:, 0:NT * E1].rearrange("p (n e) -> p n e", e=E1),
                       bcast[:, 8:8 + E1].unsqueeze(1).to_broadcast([128, NT, E1]), ADD).then_inc(S("lg12_added"), 1)
            dve.wait_ge(S("lg12_added"), at(B - 1))
            st.done(V.tensor_reduce(out=tmpa[:, :], in_=logits, axis=AX, op=MAX))
            TT(logits, logits, over(tmpa[:, :], E1), SUB).then_inc(s_sub, 1)
            dve.wait_ge(s_exp12, 1)
            st.done(V.tensor_reduce(out=tmpa[:, :], in_=coef1[:, :, :], axis=AX, op=ADD))
            st.done(V.reciprocal(tmpa[:, :], tmpa[:, :]))
            st.done(TT(logits, coef1[:, :, :], over(tmpa[:, :], E1), MUL))
            for g in range(TILES):
                last = V.max(top[:, g, :], logits[:, g, :])
            st.done(last)
            V.tensor_reduce(out=tmpb[:, :], in_=top[:, :, 0:TOP1], axis=AX, op=ADD)
            for g in range(TILES):
                last = V.max_index(idx[:, g, :], top[:, g, :], logits[:, g, :])
            st.done(last)
            V.tensor_copy(idf, idx[:, :, 0:4])
            st.done(V.reciprocal(tmpb[:, :], tmpb[:, :]))
            st.done(TT(top[:, :, 0:TOP1], top[:, :, 0:TOP1], over(tmpb[:, :], TOP1), MUL))
            for k in range(TOP1):
                st.done(one_hot(oh, k, E1))
                if k == 0:
                    st.done(TT(coef1[:, :, :], oh, over(top[:, :, k], E1), MUL))
                else:
                    st.done(TT(ohw, oh, over(top[:, :, k], E1), MUL))
                    st.done(TT(coef1[:, :, :], coef1[:, :, :], ohw, ADD))
            stage_end(dve, 12)

            combine("m1_", E1, coef1, True)
            dve.drain().then_inc(stage_done, 1)

        @block.tensor
        def _(pe):
            def mm(o, l, r, start=True, stop=True):
                return nc.tensor.matmul(o, l, r, start=start, stop=stop)

            def tile(v, t):
                return v[:, t * 128:(t + 1) * 128]

            def transposes(dst, src):
                for t in range(NT):
                    last = nc.tensor.transpose(tile(dst, t), src[:, t, :], ident[:, :])
                return last

            def tokens_out(dst, act_T, w):
                for t in range(NT):
                    last = mm(tile(dst, t), tile(act_T, t), w)
                return last

            start_signals(pe, "pe")
            pe.wait_ge(s_const, 1)
            pe.wait_ge(s_w, 16 * W_LOADS)
            nc.tensor.transpose(bank(0)[:, 0:76], rows[:, :], ident[0:76, 0:76])
            mm(bank(1)[:, 0:152], ones[0:1, :], brow[:, :]).then_inc(s_colsT, 1)
            stage_end(pe, 0)

            with pe.Fori(0, B // 2) as i:
                for u in range(2):
                    b = 2 * i + u
                    pe.wait_ge(S("xn1"), at(b))
                    pe.wait_ge(S("xT1"), at(b, 2))
                    transposes(bank(u), xn[u]).then_inc(S("tr1"), 1)
                    pe.wait_ge(S("xT1"), at(b))
                    pe.wait_ge(S("q_copied"), at(b, 1))
                    mm(bank(2), w_q[:, :], xT[u]).then_inc(S("proj_q"), 1)
                    pe.wait_ge(S("k_copied"), at(b, 1))
                    mm(bank(3), w_k[:, :], xT[u]).then_inc(S("proj_k"), 1)
                    pe.wait_ge(S("beta"), at(b, 1))
                    mm(bank(6), w_brep[:, :], xT[u]).then_inc(S("proj_b"), 1)
                    pe.wait_ge(S("sg_1"), at(b, 1))
                    mm(bank(5), w_g[:, :], xT[u]).then_inc(S("proj_g"), 1)
                    pe.wait_ge(S("v_copied"), at(b, 1))
                    mm(bank(4), w_v[:, :], xT[u]).then_inc(S("proj_v"), 1)
            stage_end(pe, 1)

            for b in range(B):
                window = headsum[:, 112 - H * b:240 - H * b]
                pe.wait_ge(S("sq_k"), at(b))
                mm(bank(0), window, sq[b % 2], start=b == 0, stop=b == B - 1)
                mm(bank(1), window, sqk[b % 2], start=b == 0, stop=b == B - 1).then_inc(S("ss_k"), 1)
            pe.wait_ge(s_rn, 2)
            for b in range(B):
                pe.wait_ge(S("bk_in"), at(b, 2))
                mm(bank(4 + b % 2), expand[:, b, :], rn[:, 512:1024]).then_inc(S("rk_mm"), 1)
                pe.wait_ge(S("q_norm"), at(b, 2))
                mm(bank(2 + b % 2), expand[:, b, :], rn[:, 0:512]).then_inc(S("rq_mm"), 1)
            stage_end(pe, 2)

            def picked_pair(dst, weights, src, b):
                for j in range(2):
                    for s in range(2):
                        last = mm(bank(dst + j), weights(j), src[:, s, bts(b, T)], start=s == 0, stop=s == 1)
                return last

            def beta_k(b, p):
                n = b * (D // 2) + p
                pe.wait_ge(S("r0_coef"), at(n, 2))
                picked_pair(2 * (p % 2), lambda j: pick[:, 2 * p + j, :], bk_hl, b).then_inc(S("r0_bk"), 1)

            def sum_up(pre, b, p, u, pairs):
                n = b * pairs + p
                pe.wait_ge(S(pre + "prod"), at(n))
                if p == 0:
                    pe.wait_ge(S(pre + "o"), at(b, 2))
                for j in range(2):
                    last = mm(bank(6 + u), ident[:, :], prod[p % 2][:, j, :],
                              start=p == 0 and j == 0, stop=p == pairs - 1 and j == 1)
                last.then_inc(S(pre + "acc"), 1)

            def recur0(b, u, first=False, last=False):
                P = D // 2
                for p in range(P):
                    n = b * P + p
                    if p < P - 1:
                        beta_k(b, p + 1)
                    elif not last:
                        beta_k(b + 1, 0)
                    pe.wait_ge(S("r0_prod"), at(n, 1))
                    picked_pair(4, lambda j: pick[:, 2 * p + j, :], q_hl, b).then_inc(S("r0_q"), 1)
                    if p:
                        sum_up("r0_", b, p - 1, u, P)
                    elif not first:
                        sum_up("r0_", b - 1, P - 1, 1 - u, P)

            beta_k(0, 0)
            recur0(0, 0, first=True)
            recur0(1, 1)
            with pe.Fori(1, B // 2 - 1) as i:
                for u in range(2):
                    recur0(2 * i + u, u)
            recur0(B - 2, 0)
            recur0(B - 1, 1, last=True)
            sum_up("r0_", B - 1, D // 2 - 1, 1, D // 2)
            stage_end(pe, 3)

            def variance(b):
                pe.wait_ge(S("o_sq"), at(b))
                mm(bank(2)[0:B, :], meanrow[:, 7 - b:15 - b], sq[b % 2],
                   start=b == 0, stop=b == B - 1).then_inc(S("o_var"), 1)

            for b in range(B):
                pe.wait_ge(S("o_sq"), at(b, 2))
                mm(bank(b % 2), center[:, :], o0[:, bts(b, T)]).then_inc(S("centred"), 1)
                if b:
                    variance(b - 1)
            variance(B - 1)
            pe.wait_ge(s_orstd, 1)

            def project0(b):
                u = b % 2
                pe.wait_ge(S("yg_ready"), at(b))
                pe.wait_ge(S("x_added"), at(b, 2))
                tokens_out(bank(5 + u), yg[u], w_o[:, :]).then_inc(S("proj_o"), 1)

            for b in range(B):
                pe.wait_ge(S("y_raw"), at(b, 2))
                mm(bank(3 + b % 2), spread[:, b, :], rn[0:B, 0:512]).then_inc(S("o_spread"), 1)
                if b:
                    project0(b - 1)
            project0(B - 1)
            stage_end(pe, 4)

            with pe.Fori(0, B // 2) as i:
                for u in range(2):
                    b = 2 * i + u
                    pe.wait_ge(S("xn5"), at(b))
                    pe.wait_ge(S("xT5"), at(b, 2))
                    transposes(bank(u), xn[u]).then_inc(S("tr5"), 1)
                    pe.wait_ge(S("xT5"), at(b))
                    for h in range(HC0):
                        pe.wait_ge(S("hid5"), at(b * HC0 + h, HC0))
                        mm(bank(2 + h), tile(w_r1, h), xT0[:, bts(b, T)]).then_inc(S("hid5_mm"), 1)
                    pe.wait_ge(S("hid5"), at(b * HC0 + HC0 - 1))
                    pe.wait_ge(S("lg5_added"), at(b, 1))
                    for t in range(NT):
                        for h in range(HC0):
                            last = mm(bank(6)[:, t * E0:(t + 1) * E0], tile(hid[u][:, h, :], t), w_r2[:, h, :],
                                      start=h == 0, stop=h == HC0 - 1)
                    last.then_inc(S("lg5_mm"), 1)
            pe.wait_ge(s_mask, 1)
            flat = picked.rearrange("p n e -> p (n e)")
            mm(bank(0)[:, 0:TILES * E0], tri[:, :], flat)
            mm(bank(1)[:, 0:TILES * E0], ones[:, :], flat).then_inc(s_counts, 1)
            stage_end(pe, 5)

            def experts(pre, E, HC, x_T, w1, w2, b2):
                with pe.Fori(0, B) as b:
                    def hidden(e):
                        for h in range(HC):
                            n = (b * E + e) * HC + h
                            pe.wait_ge(S(pre + "hid"), at(n, 4))
                            mm(bank((e * HC + h) % 4), w1[:, e, h * 128:(h + 1) * 128],
                               x_T[:, bts(b, T)]).then_inc(S(pre + "hid_mm"), 1)

                    def outputs(e):
                        n = b * E + e
                        pe.wait_ge(S(pre + "hid"), at(n * HC + HC - 1))
                        pe.wait_ge(S(pre + "acc"), at(n, 2))
                        for t in range(NT):
                            for h in range(HC):
                                last = mm(tile(bank(4 + e % 2), t), tile(hid[e % 2][:, h, :], t), w2[:, e, h, :],
                                          start=h == 0, stop=h == HC - 1)
                        last.then_inc(S(pre + "out_mm"), 1)

                    pe.wait_ge(S(pre + "cs"), at(b))
                    pe.wait_ge(S(pre + "cT"), at(b, 1))
                    for t in range(NT):
                        last = nc.tensor.transpose(tile(bank(6)[0:E, :], t), cstage[:, t, 0:E], ident[:, :])
                    last.then_inc(S(pre + "cT_mm"), 1)
                    hidden(0)
                    pe.wait_ge(S(pre + "cT"), at(b))
                    pe.wait_ge(S(pre + "bias"), at(b, 1))
                    tokens_out(bank(7), cT[0:E, :], b2[:, :]).then_inc(S(pre + "bias_mm"), 1)
                    for e in range(E):
                        if e < E - 1:
                            hidden(e + 1)
                        outputs(e)

            pe.wait_ge(s_wm0, 32)
            experts("m0_", E0, HC0, xT0, e0w1, e0w2, eb2)
            stage_end(pe, 6)

            with pe.Fori(0, B // 2) as i:
                for u in range(2):
                    b = 2 * i + u
                    h_T = hT1[:, bts(b, T)]
                    pe.wait_ge(S("xn7"), at(b))
                    pe.wait_ge(S("hT7"), at(b, 2))
                    transposes(bank(u), xn[u]).then_inc(S("tr7"), 1)
                    pe.wait_ge(S("hT7"), at(b))
                    pe.wait_ge(S("g1"), at(b, 1))
                    mm(bank(4)[0:16, :], u_gk1[:, :], h_T).then_inc(S("g1_mm"), 1)
                    pe.wait_ge(S("v_copied7"), at(b, 1))
                    mm(bank(2), u_v[:, :], h_T).then_inc(S("v_mm7"), 1)
                    pe.wait_ge(S("g1"), at(b))
                    pe.wait_ge(S("gk_copied"), at(b, 1))
                    mm(bank(5)[64 * u:64 * u + 64, :], u_gk2[:, :], g1s).then_inc(S("gk_mm"), 1)
                    pe.wait_ge(S("sg_7"), at(b, 1))
                    mm(bank(3), u_g[:, :], h_T).then_inc(S("g_mm7"), 1)
            stage_end(pe, 7)
            stage_end(pe, 8)

            def recur1(b, half, u, first=False):
                P = DK // 2
                for p in range(P):
                    n = b * P + p
                    pe.wait_ge(S("r1_coef"), at(n, 1))
                    for j in range(2):
                        last = mm(bank(j), u_krep[:, 2 * p + j, :], hT1[:, bts(b, T)])
                    last.then_inc(S("r1_k"), 1)
                    pe.wait_ge(S("r1_scanned"), at(n, 1))
                    picked_pair(2, lambda j: pickg[:, u, 2 * p + j, :], gate_hl, half).then_inc(S("r1_e"), 1)
                    pe.wait_ge(S("r1_prod"), at(n, 1))
                    for j in range(2):
                        last = mm(bank(4 + j), u_qrep[:, 2 * p + j, :], hT1[:, bts(b, T)])
                    last.then_inc(S("r1_q"), 1)
                    if p:
                        sum_up("r1_", b, p - 1, u, P)
                    elif not first:
                        sum_up("r1_", b - 1, P - 1, 1 - u, P)

            recur1(0, 0, 0, first=True)
            recur1(1, 0, 1)
            with pe.Fori(1, B // 2) as i:
                for u in range(2):
                    recur1(2 * i + u, i, u)
            sum_up("r1_", B - 1, DK // 2 - 1, 1, DK // 2)
            stage_end(pe, 9)

            for b in range(B):
                pe.wait_ge(S("o1_sq"), at(b))
                mm(bank(0), headsum[:, 112 - H * b:240 - H * b], sq[b % 2],
                   start=b == 0, stop=b == B - 1).then_inc(S("rms_mm"), 1)
            pe.wait_ge(s_rmsr, 1)

            def project1(b):
                u = b % 2
                pe.wait_ge(S("yg1_ready"), at(b))
                pe.wait_ge(S("z_added"), at(b, 2))
                tokens_out(bank(5 + u), yg[u], u_o[:, :]).then_inc(S("proj_o1"), 1)

            for b in range(B):
                pe.wait_ge(S("y1_raw"), at(b, 2))
                mm(bank(3 + b % 2), expand[:, b, :], rn[:, 0:512]).then_inc(S("rms_spread"), 1)
                if b:
                    project1(b - 1)
            project1(B - 1)
            stage_end(pe, 10)

            with pe.Fori(0, B // 2) as i:
                for u in range(2):
                    b = 2 * i + u
                    pe.wait_ge(S("xn11"), at(b))
                    pe.wait_ge(S("hT11"), at(b, 2))
                    transposes(bank(u), xn[u]).then_inc(S("tr11"), 1)
                    pe.wait_ge(S("hT11"), at(b))
                    for h in range(2):
                        pe.wait_ge(S("hid11"), at(2 * b + h, 2))
                        mm(bank(2 + h), tile(u_1, h), hT2[u]).then_inc(S("hid11_mm"), 1)
                    pe.wait_ge(S("hid11"), at(2 * b + 1))
                    pe.wait_ge(S("mlp_added"), at(b, 2))
                    for t in range(NT):
                        for h in range(2):
                            last = mm(tile(bank(4 + u), t), tile(hid[u][:, h, :], t), u_2[:, h, :],
                                      start=h == 0, stop=h == 1)
                    last.then_inc(S("mlp_mm"), 1)
            stage_end(pe, 11)

            with pe.Fori(0, B // 2) as i:
                for u in range(2):
                    b = 2 * i + u
                    pe.wait_ge(S("xn12"), at(b))
                    pe.wait_ge(S("xs12"), at(b, 2))
                    transposes(bank(u), xn[u]).then_inc(S("tr12"), 1)
                    pe.wait_ge(S("xs12"), at(b))
                    pe.wait_ge(S("lg12_added"), at(b, 1))
                    for t in range(NT):
                        last = mm(bank(6)[:, t * E1:(t + 1) * E1], tile(xT[u], t), u_r[:, :])
                    last.then_inc(S("lg12_mm"), 1)
            stage_end(pe, 12)

            pe.wait_ge(s_wm1, 32)
            experts("m1_", E1, HC1, xT1, e1w1, e1w2, mb2)
            pe.drain().then_inc(stage_done, 1)


W_LOADS = 34

_INS = ["L0_attn_x", "L0_attn_Wq", "L0_attn_Wk", "L0_attn_Wv", "L0_attn_Wbeta", "L0_attn_Wg", "L0_attn_Wout",
        "L0_attn_ln_g", "L0_attn_ln_b", "L0_ffn_rw1", "L0_ffn_rb1", "L0_ffn_rw2", "L0_ffn_rb2", "L0_ffn_ew1",
        "L0_ffn_eb1", "L0_ffn_ew2", "L0_ffn_eb2", "L1_attn_ln_w", "L1_attn_ln_b", "L1_attn_Wq", "L1_attn_Wk",
        "L1_attn_Wv", "L1_attn_gk_w1", "L1_attn_gk_w2", "L1_attn_gk_b2", "L1_attn_Wg", "L1_attn_rms_w", "L1_attn_Wo",
        "L1_attn_W1", "L1_attn_b1", "L1_attn_W2", "L1_attn_b2", "L1_ffn_router_w", "L1_ffn_router_b", "L1_ffn_w1",
        "L1_ffn_b1", "L1_ffn_w2", "L1_ffn_b2"]


def kernel(**inputs):
    import numpy as _np
    import concourse.bacc as _bacc
    from concourse import mybir as _mybir
    from concourse.bass_utils import run_bass_kernel_spmd as _run

    nc = _bacc.Bacc("TRN2", target_bir_lowering=False, num_devices=1)
    arrays, aps = {}, {}
    for name in _INS:
        a = _np.ascontiguousarray(inputs[name])
        arrays["in_" + name] = a
        aps[name] = nc.dram_tensor("in_" + name, a.shape, _mybir.dt.from_np(a.dtype), kind="ExternalInput").ap()
    shape = inputs["L0_attn_x"].shape
    out = nc.dram_tensor("out_x", shape, _mybir.dt.float32, kind="ExternalOutput").ap()
    build(nc, aps, out)
    r = _run(nc, [arrays], core_ids=[0])
    return r.results[0]["out_x"]
```

```python
import concourse.bass as bass
from concourse import mybir
from contextlib import ExitStack


class Steps:

    def __init__(self, eng, sem):
        self.eng, self.sem, self.count = eng, sem, 0

    def done(self, ins):
        ins.then_inc(self.sem, 1)
        self.count += 1
        self.eng.wait_ge(self.sem, self.count)


class LoopSteps:

    def __init__(self, eng, sem, base, per_round):
        self.eng, self.sem, self.base, self.per_round, self.value = eng, sem, base, per_round, 0

    def round(self, r, earlier=0):
        self.value = r * self.per_round + (self.base + earlier)

    def done(self, ins):
        ins.then_inc(self.sem, 1)
        self.value = self.value + 1
        self.eng.wait_ge(self.sem, self.value)


def build(nc, I, out):
    f32, f16, i32, u32 = mybir.dt.float32, mybir.dt.float16, mybir.dt.int32, mybir.dt.uint32
    ALU = mybir.AluOpType
    ACT = mybir.ActivationFunctionType
    AX = mybir.AxisListType.X
    MUL, ADD, SUB, MAX = ALU.mult, ALU.add, ALU.subtract, ALU.max

    B, T, C = I["L0_attn_x"].shape
    NT = T // 128
    TILES = B * NT
    H = 16
    D = C // H
    DK = 4
    E0, TOP0, CAP, HC0 = 8, 2, 512, 4
    ROWS = E0 * CAP
    E1, TOP1, HC1 = 16, 4, 2
    EPS = 1e-5
    GATE_NORM = 16.0
    SCALE = 1024.0
    bts = bass.ts

    ctx = ExitStack()
    with ctx:
        def sb(name, shape, dt=f32):
            return ctx.enter_context(nc.sbuf_tensor(name, shape, dt))

        def sem(name):
            return ctx.enter_context(nc.semaphore(name))

        resid = sb("resid", [128, TILES, C])
        A = [sb(f"A{n}", [128, B * T]) for n in range(1, 8)]
        A1, A2, A3, A4, A5, A6, A7 = A
        scratch = sb("scratch", [128, 11 * 1024])

        def carve(k, n=1):
            return scratch[:, k * 1024:(k + n) * 1024]

        ident = sb("ident", [128, 128])
        ones = sb("ones", [128, 128])
        center = sb("center", [128, 128])
        ones16 = sb("ones16", [128, 128], f16)
        tri = sb("tri", [128, 128], f16)
        headsum = sb("headsum", [128, 240])
        expand = sb("expand", [128, B, 128])
        meanrow = sb("meanrow", [128, 15])
        spread = sb("spread", [8, B, 128])
        pick = sb("pick", [128, D, 128], f16)
        pickg = sb("pickg", [128, 2, DK, 128], f16)
        iota_i = sb("iota_i", [128, E1], i32)
        iota = sb("iota", [128, E1])
        epsc = sb("epsc", [128, 1])

        rows = sb("rows", [76, 128])
        cols = sb("cols", [128, 76])
        brow = sb("brow", [1, 152])
        bcast = sb("bcast", [128, 152])
        LNG, LNB, RB1, EB1, LNW1, LNB1, AB1, MB1, GKB, RMSW = 0, 1, 2, 6, 38, 39, 40, 42, 74, 75

        w_q, w_k, w_v, w_g, w_o = (sb(n, [128, 128]) for n in ("w_q", "w_k", "w_v", "w_g", "w_o"))
        w_b = sb("w_b", [128, H])
        w_brep = sb("w_brep", [128, 128])
        w_r1 = sb("w_r1", [128, 512])
        w_r2 = sb("w_r2", [128, HC0, E0])
        eb2 = sb("eb2", [E0, C])
        u_kq = sb("u_kq", [128, 2, 64])
        u_v, u_g, u_o = (sb(n, [128, 128]) for n in ("u_v", "u_g", "u_o"))
        u_gk1, u_gk2 = sb("u_gk1", [128, 16]), sb("u_gk2", [16, 64])
        u_1, u_2 = sb("u_1", [128, 256]), sb("u_2", [128, 2, C])
        u_r = sb("u_r", [128, E1])
        mb2 = sb("mb2", [E1, C])

        stats = sb("stats", [128, TILES, 6])
        mean = sb("mean", [128, TILES])
        var = sb("var", [128, TILES])
        rstd = sb("rstd", [128, TILES])
        tmpa = sb("tmpa", [128, TILES])
        tmpb = sb("tmpb", [128, TILES])
        coef1 = sb("coef", [128, TILES, E1])

        PS = ctx.enter_context(nc.psum_tensor("PS", [128, 8, 512], f32))

        def bank(n, k=1):
            return PS[:, n, :] if k == 1 else PS[:, n:n + k, :]

        disp = nc.dram_tensor("disp", (ROWS, C), f32).ap()
        eo_rows = nc.dram_tensor("eo_rows", (ROWS, C), f32).ap()

        HEAD = 4

        def at(n, k=0):
            return n + (HEAD + 1 - k)

        SIGNALS = {
            "pool": ["bk_ready", "m1_low", "r0_c", "r1_c", "yg_ready"],
            "act": ["xT1", "q_copied", "k_copied", "beta", "sgm1", "sq_k", "q_high", "bk_high",
                    "r0_coef", "r0_decay", "r0_o", "o_sq", "xT5", "hid5",
                    "xn5_kept", "lg5_T", "xdT", "m0_hid", "x_std", "m1_cs", "m1_cT", "m1_hid", "m1_high",
                    "hT7", "kq_high", "v_copied7", "g1", "gk_copied", "sgm7", "r1_coef", "r1_o", "o1_sq", "hT11", "hid11",
                    "xs12", "x_high"],
            "dve": ["stats", "xn1", "v_copied", "sg_1", "bk_in", "q_norm", "r0_kk", "r0_scanned", "r0_prod",
                    "y_raw", "y_ready", "x_added", "xn5", "lg5_added", "picked", "placed", "slots", "eo", "moe_added", "x_var",
                    "m1_bias", "m1_acc", "xn7", "kq_low", "sg_7",
                    "r1_scanned", "r1_prod", "y1_raw", "yg1_ready", "z_added",
                    "xn11", "mlp_added", "xn12", "x_low", "lg12_added"],
            "pe": ["tr1", "proj_q", "proj_k", "proj_b", "proj_g", "proj_v", "ss_k", "rk_mm", "rq_mm",
                   "r0_bk", "r0_q", "r0_acc", "centred", "o_var", "o_spread", "proj_o",
                   "tr5", "hid5_mm", "lgT5_mm", "lg5_mm", "counts", "trd",
                   "m0_hid_mm", "m0_out_mm", "m1_cT_mm", "m1_hid_mm", "m1_out_mm", "m1_bias_mm",
                   "tr7", "kq_mm", "v_mm7", "g_mm7", "g1_mm", "gk_mm", "r1_k", "r1_e", "r1_q", "r1_acc",
                   "rms_mm", "rms_spread", "proj_o1", "tr11", "hid11_mm", "mlp_mm", "tr12", "lg12_mm"],
        }
        signals = {n: sem(n) for v in SIGNALS.values() for n in v}

        def S(name):
            return signals[name]

        def start_signals(eng, who):
            for n in SIGNALS[who]:
                eng.sem_inc(S(n), HEAD)

        stage_done, s_x, s_w, s_wm0, s_wm1, s_out = (
            sem(n) for n in ("stage_done", "x_loaded", "w_loaded", "moe0_loaded", "moe1_loaded", "out_written"))
        s_const, s_colsT, s_cols = sem("consts_ready"), sem("cols_transposed"), sem("cols_ready")
        s_nrm, s_rn = sem("norms"), sem("norm_reciprocals")
        s_diff, s_exp = sem("logits_less_largest"), sem("their_exp")
        s_eb2_mm, s_eb2 = sem("eb2_spread"), sem("eb2_copied")
        s_zeroed, s_scattered, s_eo = sem("disp_zeroed"), sem("tokens_scattered"), sem("eo_written")
        s_disp = [sem(f"disp_loaded{k}") for k in range(E0 // 2)]
        s_gathered = [sem(f"eo_gathered{u}") for u in range(2)]
        s_ln_high, s_log = sem("gate_ln_then_high"), sem("gate_log")
        s_carried = sem("waits_carried")
        s_dve, s_links = sem("dve_steps"), sem("dve_loop_steps")
        s_act = sem("act_steps8")
        s_pool = sem("pool_steps0")
        s_var, s_std = sem("token_variances"), sem("token_deviations")

        def stage_end(eng, k):
            eng.drain().then_inc(stage_done, 1)
            eng.wait_ge(stage_done, 4 * (k + 1))

        def wait_apart(eng):
            eng.sem_inc(s_carried, 1)

        def skewed(eng, body):
            for b in range(2):
                body(b, b % 2, b == 0, False, 0)
            with eng.Fori(1, B // 2 - 1) as i:
                for u in range(2):
                    body(2 * i + u, u, False, False, i)
            for b in range(B - 2, B):
                body(b, b % 2, False, b == B - 1, b // 2)

        def there(b, k):
            return not isinstance(b, int) or b + k < B

        q0, k0, v0, sg0, bk0 = A1, A2, A3, A4, A5
        q_hl = A6[:, :].bitcast(f16).rearrange("p (s n) -> p s n", s=2)
        bk_hl = A7[:, :].bitcast(f16).rearrange("p (s n) -> p s n", s=2)
        o0 = A1
        xn5 = A3[:, :].rearrange("p (n c) -> p n c", c=C)
        eb2_rep = A2[:, 0:E0 * C].rearrange("p (e c) -> p e c", c=C)
        xd = A5[:, :].rearrange("p (n c) -> p n c", c=C)
        eo = A4[:, :].rearrange("p (n c) -> p n c", c=C)
        e0w1 = A6[:, :].rearrange("p (e h) -> p e h", e=E0)
        e0w2 = A7[:, :].rearrange("p (e i c) -> p e i c", e=E0, c=C)
        z = A1[:, :].rearrange("p (n c) -> p n c", c=C)
        v1, sg1 = A3, A4
        kq_hl = A2[:, :].bitcast(f16).rearrange("p (s n) -> p s n", s=2)
        gate = A5[:, 0:2048]
        gate_hl = A5[:, 2048:4096].bitcast(f16).rearrange("p (s n) -> p s n", s=2)
        o1 = A3
        x_hl = A2[:, :].bitcast(f16).rearrange("p (s n) -> p s n", s=2)
        e1w1, e1w2 = A6, A7
        w1_hl = A3[:, :].bitcast(f16).rearrange("p (s n) -> p s n", s=2)
        w2_hl = A4[:, :].bitcast(f16).rearrange("p (s n) -> p s n", s=2)

        xn = [carve(0)[:, u * 512:(u + 1) * 512].rearrange("p (n c) -> p n c", c=C) for u in range(2)]
        xT = [carve(1)[:, u * 512:(u + 1) * 512] for u in range(2)]
        sgm = [carve(2)[:, u * 512:(u + 1) * 512] for u in range(2)]

        def pair(k):
            return carve(k).rearrange("p (j t) -> p j t", j=2)

        cs = [pair(0), pair(1)]
        kk = [pair(2), pair(3)]
        decay = [pair(4), pair(5)]
        cbuf = [pair(6), pair(7)]
        state = pair(8)
        prod = [pair(9), pair(10)]

        def halves(k):
            return [carve(k)[:, u * 512:(u + 1) * 512] for u in range(2)]

        y = halves(3)
        yg = halves(4)
        sq = halves(5)
        sqk = halves(6)
        nrm = carve(7)
        rn = carve(8)
        hid = [carve(2 * u + 2, 2).rearrange("p (i t) -> p i t", i=4) for u in range(2)]
        cstage = carve(8)[:, 0:64].rearrange("p (n e) -> p n e", n=4)
        cT = carve(8)[0:16, 512:1024]
        g1s = carve(7)[0:16, 0:512]
        hT2 = halves(8)
        h_full = [carve(n) for n in range(2)]
        h_high = [carve(4 + n)[:, 0:512].bitcast(f16) for n in range(4)]
        h_low = [carve(4 + n)[:, 512:1024].bitcast(f16) for n in range(4)]
        logits = carve(9)[:, 0:512].rearrange("p (n e) -> p n e", n=TILES)
        ga, gb, gm = (scratch[:, 2048 * k:2048 * (k + 1)] for k in range(3))

        top = carve(10)[:, 0:256].rearrange("p (n e) -> p n e", e=8)
        idx = carve(10)[:, 256:512].bitcast(u32).rearrange("p (n e) -> p n e", e=8)
        idf = carve(10)[:, 512:640].rearrange("p (n e) -> p n e", e=4)
        top0 = carve(10)[:, 0:64].rearrange("p (k n) -> p k n", k=TOP0)
        keep = carve(10)[:, 64:128].rearrange("p (k n) -> p k n", k=TOP0)
        coef0 = carve(10)[:, 128:192].rearrange("p (k n) -> p k n", k=TOP0)
        slot = carve(10)[:, 192:256].bitcast(i32).rearrange("p (k n) -> p k n", k=TOP0)
        slot_to = carve(10)[:, 256:320].bitcast(i32).rearrange("p (k n) -> p k n", k=TOP0)
        small = carve(9)

        def routing(col, n, dt=f32):
            return [small[:, 512 * u + col:512 * u + col + n].bitcast(dt) if dt != f32
                    else small[:, 512 * u + col:512 * u + col + n] for u in range(2)]

        def by_expert(v):
            return v.rearrange("p (n e) -> p n e", e=E0)

        lg5 = [by_expert(v) for v in routing(0, 32)]
        top5 = [by_expert(v) for v in routing(32, 32)]
        idx5 = [by_expert(v) for v in routing(64, 32, u32)]
        picked = routing(96, 32, f16)
        oh5 = [v.rearrange("p (k n e) -> p k n e", k=TOP0, e=E0) for v in routing(128, 64)]
        id5 = [v.rearrange("p (k n) -> p k n", k=TOP0) for v in routing(192, 8)]
        lg5_T = carve(8)[0:E0, 512:1024]
        place = by_expert(carve(8)[:, 0:32])
        placed = carve(8)[:, 32:96].rearrange("p (k n e) -> p k n e", k=TOP0, e=E0)
        pos, clipped, over_cap, row = (carve(8)[:, 96 + 8 * k:104 + 8 * k].rearrange("p (k n) -> p k n", k=TOP0)
                                       for k in range(4))
        carry = carve(8)[:, 128:136]
        xdT = halves(0)
        fetched = [v[:, :].rearrange("p (n c) -> p n c", c=C) for v in (A6, A7)]
        oh, ohw = (carve(8)[:, k * 512:(k + 1) * 512].rearrange("p (n e) -> p n e", e=E1) for k in range(2))

        block = ctx.enter_context(nc.Block())

        @block.sync
        def _(sp):
            xv = I["L0_attn_x"].rearrange("b (n p) c -> b p n c", p=128)
            for b in range(B):
                sp.dma_start(resid[:, b * NT:(b + 1) * NT, :], xv[b]).then_inc(s_x, 16)
            count = 0

            def load(dst, src):
                nonlocal count
                sp.dma_start(dst, src).then_inc(s_w, 16)
                count += 1

            def row(v, n=128):
                return v.rearrange("(a n) -> a n", n=n)

            load(w_q[:, :], I["L0_attn_Wq"])
            load(w_k[:, :], I["L0_attn_Wk"])
            load(w_v[:, :], I["L0_attn_Wv"])
            load(w_g[:, :], I["L0_attn_Wg"])
            load(w_b[:, :], I["L0_attn_Wbeta"])
            load(w_o[:, :], I["L0_attn_Wout"])
            load(rows[LNG:LNG + 1, :], row(I["L0_attn_ln_g"]))
            load(rows[LNB:LNB + 1, :], row(I["L0_attn_ln_b"]))
            load(rows[RB1:RB1 + 4, :], row(I["L0_ffn_rb1"]))
            load(rows[EB1:EB1 + 32, :], I["L0_ffn_eb1"].rearrange("e (i n) -> (e i) n", n=128))
            load(rows[LNW1:LNW1 + 1, :], row(I["L1_attn_ln_w"]))
            load(rows[LNB1:LNB1 + 1, :], row(I["L1_attn_ln_b"]))
            load(rows[AB1:AB1 + 2, :], row(I["L1_attn_b1"]))
            load(rows[MB1:MB1 + 32, :], I["L1_ffn_b1"].rearrange("e (i n) -> (e i) n", n=128))
            for k in range(2):
                load(rows[GKB:GKB + 1, 64 * k:64 * k + 64], row(I["L1_attn_gk_b2"], 64))
            load(rows[RMSW:RMSW + 1, :].rearrange("a (h v) -> a h v", v=D),
                 row(I["L1_attn_rms_w"], D).unsqueeze(1).to_broadcast([1, H, D]))
            load(brow[:, 0:8], row(I["L0_ffn_rb2"], 8))
            load(brow[:, 8:24], row(I["L1_ffn_router_b"], 16))
            load(brow[:, 24:152], row(I["L1_attn_b2"]))
            load(w_r1[:, :], I["L0_ffn_rw1"])
            load(w_r2[:, :, :], I["L0_ffn_rw2"].rearrange("(i p) e -> p i e", p=128))
            load(eb2[:, :], I["L0_ffn_eb2"])
            load(u_kq[:, 1, :], I["L1_attn_Wq"])
            load(u_kq[:, 0, :], I["L1_attn_Wk"])
            load(u_v[:, :], I["L1_attn_Wv"])
            load(u_g[:, :], I["L1_attn_Wg"])
            load(u_o[:, :], I["L1_attn_Wo"])
            load(u_gk1[:, :], I["L1_attn_gk_w1"])
            load(u_gk2[:, :], I["L1_attn_gk_w2"])
            load(u_1[:, :], I["L1_attn_W1"])
            load(u_2[:, :, :], I["L1_attn_W2"].rearrange("(i p) c -> p i c", p=128))
            load(u_r[:, :], I["L1_ffn_router_w"])
            load(mb2[:, :], I["L1_ffn_b2"])
            assert count == W_LOADS
            sp.wait_ge(s_const, 1)
            for k in range(ROWS * C // (128 * 1024)):
                sp.dma_start(disp[bts(k, 1024), :].rearrange("(p r) c -> p (r c)", p=128), carve(10)).then_inc(s_zeroed, 16)
            sp.wait_ge(stage_done, 4 * 4)
            sp.dma_start(e0w1, I["L0_ffn_ew1"].rearrange("e c h -> c e h")).then_inc(s_wm0, 16)
            sp.dma_start(e0w2, I["L0_ffn_ew2"].rearrange("e (i p) c -> p e i c", p=128)).then_inc(s_wm0, 16)
            sp.wait_ge(s_scattered, 16 * TOP0 * TILES)
            dv, ev = (v.rearrange("(n p) c -> p n c", p=128) for v in (disp, eo_rows))
            for k in range(E0 // 2):
                sp.dma_start(xd[:, bts(k, 2 * NT), :], dv[:, bts(k, 2 * NT), :]).then_inc(s_disp[k], 16)
            for e in range(E0):
                sp.wait_ge(S("eo"), at(e))
                sp.dma_start(ev[:, bts(e, NT), :], eo[:, bts(e, NT), :]).then_inc(s_eo, 16)
            sp.wait_ge(stage_done, 4 * 8)
            sp.dma_start(e1w1[:, :].rearrange("p (e h) -> p e h", e=E1), I["L1_ffn_w1"].rearrange("e c h -> c e h")).then_inc(s_wm1, 16)
            sp.dma_start(e1w2[:, :].rearrange("p (e i c) -> p e i c", e=E1, c=C),
                         I["L1_ffn_w2"].rearrange("e (i p) c -> p e i c", p=128)).then_inc(s_wm1, 16)
            ov = out.rearrange("b (n p) c -> b p n c", p=128)
            for b in range(B):
                sp.wait_ge(S("m1_acc"), at((b + 1) * E1 - 1))
                sp.dma_start(ov[b], resid[:, b * NT:(b + 1) * NT, :]).then_inc(s_out, 16)
            sp.wait_ge(s_out, 16 * B)

        @block.gpsimd
        def _(pool):
            start_signals(pool, "pool")
            st = Steps(pool, s_pool)
            pool.memset(epsc[:, :], EPS)
            pool.memset(carve(10), 0.0)
            pool.memset(ident[:, :], 0.0)
            pool.memset(ones[:, :], 1.0)
            pool.memset(center[:, :], -1.0 / C)
            pool.memset(tri[:, :], 1.0)
            pool.memset(ones16[:, :], 1.0)
            pool.memset(headsum[:, :], 1.0)
            pool.memset(expand[:, :, :], 0.0)
            pool.memset(meanrow[:, :], 0.0)
            pool.memset(spread[:, :, :], 0.0)
            pool.memset(pick[:, :, :], 0.0)
            pool.iota(iota_i[:, :], pattern=[[1, E1]], base=0, channel_multiplier=0)
            st.done(pool.memset(pickg[:, :, :, :], 0.0))
            sel = pool.affine_select
            sel(out=ident[:, :], in_=ident[:, :], compare_op=ALU.not_equal, fill=1.0, base=0,
                pattern=[[-1, 128]], channel_multiplier=1)
            sel(out=center[:, :], in_=center[:, :], compare_op=ALU.not_equal, fill=1.0 - 1.0 / C, base=0,
                pattern=[[-1, 128]], channel_multiplier=1)
            sel(out=tri[:, :], in_=tri[:, :], compare_op=ALU.is_gt, fill=0.0, base=0,
                pattern=[[1, 128]], channel_multiplier=-1)
            sel(out=headsum[:, :], in_=headsum[:, :], compare_op=ALU.is_ge, fill=0.0, base=112 * D,
                pattern=[[-D, 240]], channel_multiplier=1)
            sel(out=expand[:, :, :].rearrange("p b (h i) -> p b h i", i=D),
                in_=expand[:, :, :].rearrange("p b (h i) -> p b h i", i=D),
                compare_op=ALU.not_equal, fill=1.0, base=0, pattern=[[-H, B], [-1, H], [0, D]], channel_multiplier=1)
            sel(out=spread[:, :, :], in_=spread[:, :, :], compare_op=ALU.not_equal, fill=1.0, base=0,
                pattern=[[-1, B], [0, 128]], channel_multiplier=1)
            pool.memset(meanrow[:, 7:8], 1.0 / C)
            sel(out=pick[:, :, :].rearrange("p j (h i) -> p j h i", i=D),
                in_=pick[:, :, :].rearrange("p j (h i) -> p j h i", i=D),
                compare_op=ALU.not_equal, fill=1.0, base=0, pattern=[[-1, D], [-D, H], [0, D]], channel_multiplier=1)
            for u in range(2):
                sel(out=pickg[:, u, :, :].rearrange("p k (h i) -> p k h i", i=D),
                    in_=pickg[:, u, :, :].rearrange("p k (h i) -> p k h i", i=D),
                    compare_op=ALU.not_equal, fill=1.0, base=-64 * u, pattern=[[-1, DK], [-DK, H], [0, D]],
                    channel_multiplier=1)
            st.done(pool.tensor_copy(iota[:, :], iota_i[:, :]))
            sel(out=headsum[:, :], in_=headsum[:, :], compare_op=ALU.is_ge, fill=0.0, base=D - 1 - 112 * D,
                pattern=[[D, 240]], channel_multiplier=-1).then_inc(s_const, 1)
            stage_end(pool, 0)
            stage_end(pool, 1)

            for b in range(B):
                c = bts(b, T)
                pool.wait_ge(S("bk_in"), at(b))
                pool.tensor_tensor(bk0[:, c], k0[:, c], bk0[:, c], MUL).then_inc(S("bk_ready"), 1)
                pool.wait_ge(S("q_high"), at(b))
                pool.tensor_tensor(q_hl[:, 1, c], q0[:, c], q_hl[:, 0, c], SUB)
                pool.wait_ge(S("bk_high"), at(b))
                pool.wait_ge(S("bk_ready"), at(b))
                pool.tensor_tensor(bk_hl[:, 1, c], bk0[:, c], bk_hl[:, 0, c], SUB)
            stage_end(pool, 2)

            def additions(pre, v, pairs):
                for b in range(B):
                    for p in range(pairs):
                        n = b * pairs + p
                        pool.wait_ge(S(pre + "coef"), at(n))
                        pool.wait_ge(S(pre + "scanned"), at(n, 2))
                        pool.tensor_tensor(cbuf[p % 2], cs[p % 2],
                                           v[:, bts(b, T)].unsqueeze(1).to_broadcast([128, 2, T]),
                                           MUL).then_inc(S(pre + "c"), 1)

            additions("r0_", v0, D // 2)
            stage_end(pool, 3)

            for b in range(B):
                u = b % 2
                pool.wait_ge(S("y_ready"), at(b))
                pool.wait_ge(S("proj_o"), at(b, 2))
                pool.tensor_tensor(yg[u], y[u], sg0[:, bts(b, T)], MUL).then_inc(S("yg_ready"), 1)
            stage_end(pool, 4)

            pool.wait_ge(s_zeroed, 16 * (ROWS * C // (128 * 1024)))
            for b in range(B):
                pool.wait_ge(S("slots"), at(b))
                pool.wait_ge(S("xn5_kept"), at(b))
                for t in range(b * NT, (b + 1) * NT):
                    for k in range(TOP0):
                        pool.indirect_dma_start(out=disp[:, :], in_=xn5[:, t, :], in_offset=None,
                                                out_offset=bass.IndirectOffsetOnAxis(ap=slot_to[:, k, t:t + 1], axis=0),
                                                bounds_check=ROWS - 1, oob_is_err=False).then_inc(s_scattered, 16)
            stage_end(pool, 5)
            stage_end(pool, 6)

            pool.wait_ge(s_eo, 16 * E0)
            for b in range(B):
                if b >= 2:
                    pool.wait_ge(s_gathered[b % 2], 16 * TOP0 * NT * (b // 2))
                for t in range(NT):
                    for k in range(TOP0):
                        g = b * NT + t
                        pool.indirect_dma_start(out=fetched[k][:, g, :], out_offset=None, in_=eo_rows[:, :],
                                                in_offset=bass.IndirectOffsetOnAxis(ap=slot[:, k, g:g + 1], axis=0),
                                                bounds_check=ROWS - 1,
                                                oob_is_err=False).then_inc(s_gathered[b % 2], 16)
            stage_end(pool, 7)
            stage_end(pool, 8)
            additions("r1_", v1, DK // 2)
            stage_end(pool, 9)
            stage_end(pool, 10)

            pool.wait_ge(s_wm1, 32)
            for w, hl in ((e1w1, w1_hl), (e1w2, w2_hl)):
                st.done(pool.tensor_scalar(w[:, :], w[:, :], SCALE, 1.0, MUL, MUL))
                st.done(pool.tensor_copy(hl[:, 0, :], w[:, :]))
                st.done(pool.tensor_tensor(hl[:, 1, :], w[:, :], hl[:, 0, :], SUB))
            stage_end(pool, 11)
            stage_end(pool, 12)

            for n in range(B * E1):
                pool.wait_ge(S("m1_high"), at(n))
                pool.wait_ge(S("m1_out_mm"), at(n, 4))
                pool.tensor_tensor(h_low[n % 4], h_full[n % 2], h_high[n % 4], SUB).then_inc(S("m1_low"), 1)
            pool.drain().then_inc(stage_done, 1)

        @block.scalar
        def _(act):
            A_ = nc.scalar.activation

            def norm_std(n):
                act.wait_ge(s_var, n + 1)
                A_(rstd[:, :], var[:, :], ACT.Sqrt, bias=epsc[:, 0:1]).then_inc(s_std, 1)

            start_signals(act, "act")
            act.wait_ge(s_const, 1)
            act.wait_ge(s_colsT, 1)
            A_(cols[:, :], bank(0)[:, 0:76], ACT.Copy)
            A_(bcast[:, :], bank(1)[:, 0:152], ACT.Copy)
            norm_std(0)
            stage_end(act, 0)

            def xT_copy(b, u):
                act.wait_ge(S("tr1"), at(b))
                act.wait_ge(S("proj_v"), at(b, 2))
                A_(xT[u], bank(u), ACT.Copy).then_inc(S("xT1"), 1)

            def stage1(b, u, first, last, i):
                c = bts(b, T)
                if not last:
                    xT_copy(b + 1, 1 - u)
                act.wait_ge(S("proj_q"), at(b))
                A_(q0[:, c], bank(2), ACT.Copy).then_inc(S("q_copied"), 1)
                act.wait_ge(S("proj_k"), at(b))
                A_(k0[:, c], bank(3), ACT.Copy).then_inc(S("k_copied"), 1)
                act.wait_ge(S("proj_b"), at(b))
                A_(bk0[:, c], bank(6), ACT.Sigmoid).then_inc(S("beta"), 1)
                act.wait_ge(S("proj_g"), at(b))
                act.wait_ge(S("sg_1"), at(b, 2))
                A_(sgm[u], bank(5), ACT.Sigmoid).then_inc(S("sgm1"), 1)

            xT_copy(0, 0)
            skewed(act, stage1)
            stage_end(act, 1)

            for b in range(B):
                act.wait_ge(S("ss_k"), at(b, 2))
                A_(sq[b % 2], q0[:, bts(b, T)], ACT.Square)
                A_(sqk[b % 2], k0[:, bts(b, T)], ACT.Square).then_inc(S("sq_k"), 1)
            act.wait_ge(S("ss_k"), at(B - 1))
            A_(nrm[:, 0:512], bank(0), ACT.Sqrt).then_inc(s_nrm, 1)
            A_(nrm[:, 512:1024], bank(1), ACT.Sqrt).then_inc(s_nrm, 1)
            for b in range(B):
                c = bts(b, T)
                act.wait_ge(S("q_norm"), at(b))
                A_(q_hl[:, 0, c], q0[:, c], ACT.Copy).then_inc(S("q_high"), 1)
                act.wait_ge(S("bk_ready"), at(b))
                A_(bk_hl[:, 0, c], bk0[:, c], ACT.Copy).then_inc(S("bk_high"), 1)
            stage_end(act, 2)

            def outputs(pre, dst, b, u, pairs):
                act.wait_ge(S(pre + "acc"), at(b * pairs + pairs - 1))
                A_(dst[:, bts(b, T)], bank(6 + u), ACT.Copy).then_inc(S(pre + "o"), 1)

            def decays(b, u, first):
                for p in range(D // 2):
                    n = b * (D // 2) + p
                    act.wait_ge(S("r0_bk"), at(n))
                    act.wait_ge(S("r0_c"), at(n, 2))
                    act.wait_ge(S("r0_kk"), at(n, 2))
                    A_(cs[p % 2], bank(2 * (p % 2), 2), ACT.Copy).then_inc(S("r0_coef"), 1)
                    act.wait_ge(S("r0_kk"), at(n))
                    act.wait_ge(S("r0_scanned"), at(n, 2))
                    A_(decay[p % 2], kk[p % 2], ACT.Identity, scale=-1.0, bias=1.0).then_inc(S("r0_decay"), 1)
                    if p == 1 and not first:
                        outputs("r0_", o0, b - 1, 1 - u, D // 2)

            decays(0, 0, True)
            decays(1, 1, False)
            with act.Fori(1, B // 2) as i:
                for u in range(2):
                    decays(2 * i + u, u, False)
            outputs("r0_", o0, B - 1, 1, D // 2)
            stage_end(act, 3)

            for b in range(B):
                act.wait_ge(S("centred"), at(b))
                act.wait_ge(S("o_var"), at(b, 2))
                A_(o0[:, bts(b, T)], bank(b % 2), ACT.Copy)
                A_(sq[b % 2], bank(b % 2), ACT.Square).then_inc(S("o_sq"), 1)
            act.wait_ge(S("o_var"), at(B - 1))
            A_(nrm[0:B, 0:512], bank(2)[0:B, :], ACT.Sqrt, bias=epsc[0:B, 0:1]).then_inc(s_nrm, 1)
            norm_std(1)
            stage_end(act, 4)

            def xT5_copy(b, u):
                act.wait_ge(S("xn5"), at(b))
                wait_apart(act)
                A_(xn5[:, bts(b, NT), :], xn[u], ACT.Copy).then_inc(S("xn5_kept"), 1)
                act.wait_ge(S("tr5"), at(b))
                A_(xT[u], bank(u), ACT.Copy).then_inc(S("xT5"), 1)

            def router_hidden(b, u):
                act.wait_ge(S("lgT5_mm"), at(b, 2))
                for h in range(HC0):
                    act.wait_ge(S("hid5_mm"), at(b * HC0 + h))
                    A_(hid[u][:, h, :], bank(2 + h), ACT.Relu,
                       bias=cols[:, RB1 + h:RB1 + h + 1]).then_inc(S("hid5"), 1)

            def stage5(b, u, first, last, i):
                if there(b, 1):
                    router_hidden(b + 1, 1 - u)
                if there(b, 2):
                    xT5_copy(b + 2, u)
                act.wait_ge(S("lgT5_mm"), at(b))
                act.wait_ge(S("lg5_mm"), at(b, 1))
                A_(lg5_T, bank(6)[0:E0, :], ACT.Copy).then_inc(S("lg5_T"), 1)

            xT5_copy(0, 0)
            router_hidden(0, 0)
            xT5_copy(1, 1)
            skewed(act, stage5)
            stage_end(act, 5)

            act.wait_ge(s_diff, 1)
            A_(tmpb[:, :], tmpa[:, :], ACT.Exp).then_inc(s_exp, 1)

            def xdT_copy(e):
                act.wait_ge(S("trd"), at(e))
                A_(xdT[e % 2], bank(e % 2), ACT.Copy).then_inc(S("xdT"), 1)

            def hidden0(e):
                act.wait_ge(S("m0_out_mm"), at(e, 2))
                for h in range(HC0):
                    n = e * HC0 + h
                    act.wait_ge(S("m0_hid_mm"), at(n))
                    A_(hid[e % 2][:, h, :], bank(2 + h), ACT.Relu,
                       bias=cols[:, EB1 + n:EB1 + n + 1]).then_inc(S("m0_hid"), 1)

            xdT_copy(0)
            xdT_copy(1)
            for e in range(E0):
                hidden0(e)
                if e < E0 - 2:
                    xdT_copy(e + 2)
            stage_end(act, 6)

            def deviations(b, k):
                act.wait_ge(S("x_var"), at(2 * b + k))
                wait_apart(act)
                A_(rstd[:, bts(b, NT)], var[:, bts(b, NT)], ACT.Sqrt, bias=epsc[:, 0:1]).then_inc(S("x_std"), 1)

            def hT_copy(b, u):
                act.wait_ge(S("tr7"), at(b))
                A_(xT[u], bank(u), ACT.Identity, scale=cols[:, LNW1:LNW1 + 1],
                   bias=cols[:, LNB1:LNB1 + 1]).then_inc(S("hT7"), 1)

            def stage7(b, u, first, last, i):
                half = slice(64 * u, 64 * u + 64)
                act.wait_ge(S("g1_mm"), at(b))
                act.wait_ge(S("gk_mm"), at(b, 1))
                A_(g1s, bank(4)[0:16, :], ACT.Copy).then_inc(S("g1"), 1)
                act.wait_ge(S("kq_mm"), at(b))
                A_(kq_hl[:, 0, bts(b, T)], bank(6), ACT.Copy).then_inc(S("kq_high"), 1)
                act.wait_ge(S("v_mm7"), at(b))
                A_(v1[:, bts(b, T)], bank(2), ACT.Copy).then_inc(S("v_copied7"), 1)
                if there(b, 1):
                    deviations(b + 1, 1)
                if there(b, 2):
                    deviations(b + 2, 0)
                if there(b, 1):
                    hT_copy(b + 1, 1 - u)
                act.wait_ge(S("g_mm7"), at(b))
                act.wait_ge(S("sg_7"), at(b, 2))
                A_(sgm[u], bank(3 + 4 * u), ACT.Sigmoid).then_inc(S("sgm7"), 1)
                act.wait_ge(S("gk_mm"), at(b))
                A_(gate[half, bts(i, T)], bank(5)[half, :], ACT.Identity,
                   bias=cols[half, GKB:GKB + 1]).then_inc(S("gk_copied"), 1)

            deviations(0, 0)
            deviations(0, 1)
            deviations(1, 0)
            hT_copy(0, 0)
            skewed(act, stage7)
            stage_end(act, 7)

            st = Steps(act, s_act)
            st.done(A_(ga, gate, ACT.Abs))
            st.done(A_(gb, ga, ACT.Exp, scale=-1.0))
            A_(ga, gb, ACT.Ln, bias=1.0).then_inc(s_ln_high, 1)
            act.wait_ge(s_log, 1)
            st.done(A_(gate, gb, ACT.Exp, scale=1.0 / GATE_NORM))
            A_(gate_hl[:, 0, :], gate, ACT.Copy).then_inc(s_ln_high, 1)
            stage_end(act, 8)

            def keys(b, u, first):
                for p in range(DK // 2):
                    n = b * (DK // 2) + p
                    act.wait_ge(S("r1_k"), at(n))
                    act.wait_ge(S("r1_c"), at(n, 2))
                    A_(cs[p % 2], bank(0, 2), ACT.Copy).then_inc(S("r1_coef"), 1)
                    if p == 1 and not first:
                        outputs("r1_", o1, b - 1, 1 - u, DK // 2)

            keys(0, 0, True)
            keys(1, 1, False)
            with act.Fori(1, B // 2) as i:
                for u in range(2):
                    keys(2 * i + u, u, False)
            outputs("r1_", o1, B - 1, 1, DK // 2)
            stage_end(act, 9)

            for b in range(B):
                act.wait_ge(S("rms_mm"), at(b, 2))
                A_(sq[b % 2], o1[:, bts(b, T)], ACT.Square).then_inc(S("o1_sq"), 1)
            act.wait_ge(S("rms_mm"), at(B - 1))
            A_(nrm[:, 0:512], bank(0), ACT.Sqrt, scale=1.0 / D, bias=epsc[:, 0:1]).then_inc(s_nrm, 1)
            norm_std(2)
            stage_end(act, 10)

            def hT2_copy(b, u):
                act.wait_ge(S("tr11"), at(b))
                act.wait_ge(S("hid11_mm"), at(2 * b + 1, 4))
                A_(hT2[u], bank(u), ACT.Identity, scale=cols[:, LNW1:LNW1 + 1],
                   bias=cols[:, LNB1:LNB1 + 1]).then_inc(S("hT11"), 1)

            def stage11(b, u, first, last, i):
                act.wait_ge(S("mlp_mm"), at(b, 2))
                for h in range(2):
                    act.wait_ge(S("hid11_mm"), at(2 * b + h))
                    A_(hid[u][:, h, :], bank(2 + h), ACT.Gelu,
                       bias=cols[:, AB1 + h:AB1 + h + 1]).then_inc(S("hid11"), 1)
                if not last:
                    hT2_copy(b + 1, 1 - u)

            hT2_copy(0, 0)
            skewed(act, stage11)
            norm_std(3)
            stage_end(act, 11)

            def xs_copy(b, u):
                act.wait_ge(S("tr12"), at(b))
                act.wait_ge(S("lg12_mm"), at(b, 2))
                act.wait_ge(S("x_low"), at(b, 2))
                A_(xT[u], bank(u), ACT.Copy).then_inc(S("xs12"), 1)
                act.wait_ge(S("xs12"), at(b))
                A_(x_hl[:, 0, bts(b, T)], xT[u], ACT.Copy).then_inc(S("x_high"), 1)

            def stage12(b, u, first, last, i):
                if not last:
                    xs_copy(b + 1, 1 - u)

            xs_copy(0, 0)
            skewed(act, stage12)
            act.wait_ge(s_diff, 2)
            A_(coef1[:, :, :], logits, ACT.Exp).then_inc(s_exp, 1)
            stage_end(act, 12)

            def coefficients_staged(b):
                act.wait_ge(S("m1_cT_mm"), at(b, 1))
                A_(cstage, coef1[:, bts(b, NT), :], ACT.Copy).then_inc(S("m1_cs"), 1)

            def coefficients_transposed(b):
                act.wait_ge(S("m1_cT_mm"), at(b))
                act.wait_ge(S("m1_bias_mm"), at(b, 1))
                A_(cT, bank(6)[0:E1, :], ACT.Copy).then_inc(S("m1_cT"), 1)

            with act.Fori(0, B) as b:
                for e in range(E1):
                    n = b * E1 + e
                    act.wait_ge(S("m1_low"), at(n, 2))
                    for h in range(HC1):
                        act.wait_ge(S("m1_hid_mm"), at(n * HC1 + h))
                        A_(h_full[e % 2][:, h * T:(h + 1) * T], bank((e * HC1 + h) % 4), ACT.Gelu, scale=1.0 / SCALE,
                           bias=cols[:, MB1 + e * HC1 + h:MB1 + e * HC1 + h + 1]).then_inc(S("m1_hid"), 1)
                    act.wait_ge(S("m1_hid"), at(n * HC1 + HC1 - 1))
                    act.wait_ge(S("m1_out_mm"), at(n, 4))
                    A_(h_high[e % 4], h_full[e % 2], ACT.Copy).then_inc(S("m1_high"), 1)
                    if e == 1:
                        coefficients_staged(b)
                    if e == 4:
                        coefficients_transposed(b)
            act.drain().then_inc(stage_done, 1)

        @block.vector
        def _(dve):
            V = nc.vector
            TT, TS, STT = V.tensor_tensor, V.tensor_scalar, V.scalar_tensor_tensor

            def tile_stats(src, b):
                for t in range(NT):
                    last = V.bn_stats(stats[:, b * NT + t, :], src[:, b * NT + t, :])
                return last

            def norm_scalars(st, n):
                me, mo, ve, vo = (stats[:, :, k] for k in (1, 4, 2, 5))
                TT(tmpb[:, :], me, mo, SUB)
                TT(var[:, :], ve, vo, ADD)
                st.done(TT(tmpa[:, :], me, mo, ADD))
                TS(mean[:, :], tmpa[:, :], 0.5, None, MUL)
                st.done(STT(out=tmpb[:, :], in0=tmpb[:, :], scalar=0.25, in1=tmpb[:, :], op0=MUL, op1=MUL))
                STT(out=var[:, :], in0=var[:, :], scalar=1.0 / C, in1=tmpb[:, :], op0=MUL, op1=ADD).then_inc(s_var, 1)
                dve.wait_ge(s_std, n + 1)
                st.done(V.reciprocal(rstd[:, :], rstd[:, :]))

            def normalise(dst, src, b):
                for t in range(NT):
                    g = b * NT + t
                    last = TS(dst(t), src[:, g, :], mean[:, bass.ds(g, 1)], rstd[:, bass.ds(g, 1)], SUB, MUL)
                return last

            start_signals(dve, "dve")
            st = Steps(dve, s_dve)
            dve.wait_ge(s_x, 16 * B)
            with dve.Fori(0, B) as b:
                tile_stats(resid, b).then_inc(S("stats"), 1)
            dve.wait_ge(S("stats"), at(B - 1))
            dve.wait_ge(s_const, 1)
            norm_scalars(st, 0)
            dve.wait_ge(s_w, 16 * W_LOADS)
            V.tensor_copy(w_brep[:, :].rearrange("p (h i) -> p h i", i=D),
                          w_b[:, :].unsqueeze(2).to_broadcast([128, H, D]))
            TS(u_kq[:, 1, :], u_kq[:, 1, :], float(DK) ** -0.5, None, MUL)
            stage_end(dve, 0)

            def xn_ahead(b, u, src, transposed, ready):
                dve.wait_ge(S(transposed), at(b, 2))
                normalise(lambda t: xn[u][:, t, :], src, b).then_inc(S(ready), 1)

            def stage1(b, u, first, last, i):
                c = bts(b, T)
                if not last:
                    xn_ahead(b + 1, 1 - u, resid, "tr1", "xn1")
                dve.wait_ge(S("sgm1"), at(b))
                TT(sg0[:, c], bank(5), sgm[u], MUL).then_inc(S("sg_1"), 1)
                dve.wait_ge(S("proj_v"), at(b))
                V.tensor_copy(v0[:, c], bank(4)).then_inc(S("v_copied"), 1)

            xn_ahead(0, 0, resid, "tr1", "xn1")
            skewed(dve, stage1)
            stage_end(dve, 1)

            for s in range(2):
                dve.wait_ge(s_nrm, s + 1)
                half = slice(512 * s, 512 * s + 512)
                st.done(TS(nrm[:, half], nrm[:, half], 1e-12, None, MAX))
                V.reciprocal(rn[:, half], nrm[:, half]).then_inc(s_rn, 1)
            for b in range(B):
                c = bts(b, T)
                dve.wait_ge(S("rk_mm"), at(b))
                TT(k0[:, c], k0[:, c], bank(4 + b % 2), MUL).then_inc(S("bk_in"), 1)
                dve.wait_ge(S("rq_mm"), at(b))
                TT(q0[:, c], q0[:, c], bank(2 + b % 2), MUL).then_inc(S("q_norm"), 1)
            stage_end(dve, 2)

            def beta_kk(b, p):
                n = b * (D // 2) + p
                dve.wait_ge(S("r0_coef"), at(n))
                dve.wait_ge(S("r0_decay"), at(n, 2))
                TT(kk[p % 2], cs[p % 2], k0[:, bts(b, T)].unsqueeze(1).to_broadcast([128, 2, T]),
                   MUL).then_inc(S("r0_kk"), 1)

            def scan(pre, n, p, decays):
                dve.wait_ge(S(pre + "c"), at(n))
                dve.wait_ge(S(pre + "prod"), at(n, 1))
                for j in range(2):
                    last = V.tensor_tensor_scan(out=state[:, j, :], data0=decays[:, j, :], data1=cbuf[p % 2][:, j, :],
                                                initial=0.0, op0=MUL, op1=ADD)
                last.then_inc(S(pre + "scanned"), 1)

            def read_out(pre, n, p):
                dve.wait_ge(S(pre + "scanned"), at(n))
                dve.wait_ge(S(pre + "q"), at(n))
                dve.wait_ge(S(pre + "acc"), at(n, 2))
                TT(prod[p % 2], bank(4, 2), state, MUL).then_inc(S(pre + "prod"), 1)

            def recur0(b, last):
                for p in range(D // 2):
                    n = b * (D // 2) + p
                    if p < D // 2 - 1:
                        beta_kk(b, p + 1)
                    elif not last:
                        beta_kk(b + 1, 0)
                    dve.wait_ge(S("r0_decay"), at(n))
                    scan("r0_", n, p, decay[p % 2])
                    read_out("r0_", n, p)

            dve.wait_ge(s_zeroed, 16 * (ROWS * C // (128 * 1024)))
            beta_kk(0, 0)
            with dve.Fori(0, B - 1) as b:
                recur0(b, False)
            recur0(B - 1, True)
            stage_end(dve, 3)

            dve.wait_ge(s_nrm, 3)
            V.reciprocal(rn[0:B, 0:512], nrm[0:B, 0:512]).then_inc(s_rn, 1)

            def add_projection(b, dst, proj, added):
                u = b % 2
                dve.wait_ge(S(proj), at(b))
                xs = dst[:, b * NT:(b + 1) * NT, :]
                TT(xs, xs, bank(5 + u).rearrange("p (n c) -> p n c", c=C), ADD).then_inc(S(added), 1)
                dve.wait_ge(S(added), at(b))
                tile_stats(dst, b).then_inc(S("stats"), 1)

            for b in range(B):
                u = b % 2
                dve.wait_ge(S("o_spread"), at(b))
                dve.wait_ge(S("yg_ready"), at(b, 2))
                TT(y[u], o0[:, bts(b, T)], bank(3 + u), MUL).then_inc(S("y_raw"), 1)
                dve.wait_ge(S("y_raw"), at(b))
                TS(y[u], y[u], cols[:, LNG:LNG + 1], cols[:, LNB:LNB + 1], MUL, ADD).then_inc(S("y_ready"), 1)
                if b >= 1:
                    add_projection(b - 1, resid, "proj_o", "x_added")
            add_projection(B - 1, resid, "proj_o", "x_added")
            dve.wait_ge(S("stats"), at(2 * B - 1))
            norm_scalars(st, 1)
            stage_end(dve, 4)

            ROUTE, PLACE = 5, 5
            links = LoopSteps(dve, s_links, 0, ROUTE + PLACE)

            def route(b, u):
                links.round(b)
                dve.wait_ge(S("lg5_mm"), at(b))
                TT(lg5[u], bank(6)[:, 0:NT * E0].rearrange("p (n e) -> p n e", e=E0),
                   bcast[:, 0:E0].unsqueeze(1).to_broadcast([128, NT, E0]), ADD).then_inc(S("lg5_added"), 1)
                dve.wait_ge(S("lg5_added"), at(b))
                wait_apart(dve)
                for t in range(NT):
                    last = V.max(top5[u][:, t, :], lg5[u][:, t, :])
                links.done(last)
                links.done(V.tensor_copy(top0[:, :, bts(b, NT)], top5[u][:, :, 0:TOP0].rearrange("p n k -> p k n")))
                wait_apart(dve)
                for t in range(NT):
                    last = V.max_index(idx5[u][:, t, :], top5[u][:, t, :], lg5[u][:, t, :])
                links.done(last)
                links.done(V.tensor_copy(id5[u], idx5[u][:, :, 0:TOP0].rearrange("p n k -> p k n")))
                links.done(TT(oh5[u], iota[:, 0:E0].unsqueeze(1).unsqueeze(1).to_broadcast([128, TOP0, NT, E0]),
                              id5[u].unsqueeze(3).to_broadcast([128, TOP0, NT, E0]), ALU.is_equal))
                TT(by_expert(picked[u][:, 0:NT * E0]), oh5[u][:, 0], oh5[u][:, 1], ADD).then_inc(S("picked"), 1)

            def place_picks(b, u):
                links.round(b, ROUTE)
                dve.wait_ge(S("counts"), at(b))
                links.done(TT(place, by_expert(bank(7)[:, 0:NT * E0]),
                              carry.unsqueeze(1).to_broadcast([128, NT, E0]), ADD))
                TT(carry, carry, bank(7)[:, NT * E0:NT * E0 + E0], ADD).then_inc(S("placed"), 1)
                links.done(TT(placed, oh5[u], place.unsqueeze(1).to_broadcast([128, TOP0, NT, E0]), MUL))
                links.done(V.tensor_reduce(out=pos, in_=placed, axis=AX, op=ADD))
                TS(keep[:, :, bts(b, NT)], pos, float(CAP), None, ALU.is_lt)
                TS(over_cap, pos, float(CAP), float(ROWS), ALU.is_ge, MUL)
                links.done(TS(clipped, pos, float(CAP - 1), None, ALU.min))
                links.done(STT(out=row, in0=id5[u], scalar=float(CAP), in1=clipped, op0=MUL, op1=ADD))
                V.tensor_copy(slot[:, :, bts(b, NT)], row)
                TT(slot_to[:, :, bts(b, NT)], row, over_cap, ADD).then_inc(S("slots"), 1)

            def xn5_ahead(b, u):
                dve.wait_ge(S("xn5_kept"), at(b, 2))
                xn_ahead(b, u, resid, "tr5", "xn5")

            def stage5(b, u, first, last, i):
                if there(b, 2):
                    xn5_ahead(b + 2, u)
                if not first:
                    place_picks(b - 1, 1 - u)
                route(b, u)

            V.memset(carry, 0.0)
            xn5_ahead(0, 0)
            xn5_ahead(1, 1)
            skewed(dve, stage5)
            place_picks(B - 1, 1)
            stage_end(dve, 5)

            TT(tmpa[:, :], top0[:, 1, :], top0[:, 0, :], SUB).then_inc(s_diff, 1)
            dve.wait_ge(s_eb2_mm, 1)
            V.tensor_copy(eb2_rep, bank(6, 2).rearrange("p k (e c) -> p (k e) c", c=C)).then_inc(s_eb2, 1)
            dve.wait_ge(s_exp, 1)
            st.done(TS(tmpa[:, :], tmpb[:, :], 1.0, None, ADD))
            st.done(V.reciprocal(tmpa[:, :], tmpa[:, :]))
            st.done(TT(tmpb[:, :], tmpb[:, :], tmpa[:, :], MUL))
            TT(coef0[:, 0, :], keep[:, 0, :], tmpa[:, :], MUL)
            TT(coef0[:, 1, :], keep[:, 1, :], tmpb[:, :], MUL)
            dve.wait_ge(s_eb2, 1)
            for e in range(E0):
                dve.wait_ge(S("m0_out_mm"), at(e))
                TT(eo[:, bts(e, NT), :], bank(6 + e % 2).rearrange("p (n c) -> p n c", c=C),
                   eb2_rep[:, e, :].unsqueeze(1).to_broadcast([128, NT, C]), ADD).then_inc(S("eo"), 1)
            stage_end(dve, 6)

            COMBINE, MAKE_Z, MAKE_H = 4, 5, 1
            links7 = LoopSteps(dve, s_links, B * (ROUTE + PLACE) + COMBINE, COMBINE + MAKE_Z + MAKE_H)

            def variances(src, b):
                ts = bts(b, NT)
                wait_apart(dve)
                links7.done(tile_stats(src, b))
                TT(tmpb[:, ts], stats[:, ts, 1], stats[:, ts, 4], SUB)
                TT(var[:, ts], stats[:, ts, 2], stats[:, ts, 5], ADD)
                links7.done(TT(tmpa[:, ts], stats[:, ts, 1], stats[:, ts, 4], ADD))
                TS(mean[:, ts], tmpa[:, ts], 0.5, None, MUL)
                links7.done(STT(out=tmpb[:, ts], in0=tmpb[:, ts], scalar=0.25, in1=tmpb[:, ts], op0=MUL, op1=MUL))
                STT(out=var[:, ts], in0=var[:, ts], scalar=1.0 / C, in1=tmpb[:, ts], op0=MUL,
                    op1=ADD).then_inc(S("x_var"), 1)

            def invert(b, k):
                dve.wait_ge(S("x_std"), at(2 * b + k))
                wait_apart(dve)
                links7.done(V.reciprocal(rstd[:, bts(b, NT)], rstd[:, bts(b, NT)]))

            def combine(b, u, i):
                links7.round(b, -COMBINE)
                if not isinstance(b, int) or b:
                    links7.round(b - 1, MAKE_Z)
                dve.wait_ge(s_gathered[u], 16 * TOP0 * NT * (i + 1))
                for k in range(TOP0):
                    for t in range(NT):
                        g = b * NT + t
                        last = STT(out=resid[:, g, :], in0=fetched[k][:, g, :], scalar=coef0[:, k, bass.ds(g, 1)],
                                   in1=resid[:, g, :], op0=MUL, op1=ADD)
                    if k < TOP0 - 1:
                        links7.done(last)
                last.then_inc(S("moe_added"), 1)
                dve.wait_ge(S("moe_added"), at(b))
                variances(resid, b)

            def make_z(b):
                links7.round(b)
                invert(b, 0)
                links7.done(normalise(lambda t: z[:, b * NT + t, :], resid, b))
                variances(z, b)

            def make_h(b, u):
                links7.round(b, MAKE_Z + (COMBINE if there(b, 1) else 0))
                invert(b, 1)
                dve.wait_ge(S("tr7"), at(b, 2))
                normalise(lambda t: xn[u][:, t, :], z, b).then_inc(S("xn7"), 1)

            def silu(b, u):
                dve.wait_ge(S("sgm7"), at(b))
                TT(sg1[:, bts(b, T)], bank(3 + 4 * u), sgm[u], MUL).then_inc(S("sg_7"), 1)

            def stage7(b, u, first, last, i):
                c = bts(b, T)
                if there(b, 1):
                    make_z(b + 1)
                if there(b, 2):
                    combine(b + 2, u, i + 1)
                if not first:
                    silu(b - 1, 1 - u)
                if there(b, 1):
                    make_h(b + 1, 1 - u)
                dve.wait_ge(S("kq_high"), at(b))
                TT(kq_hl[:, 1, c], bank(6), kq_hl[:, 0, c], SUB).then_inc(S("kq_low"), 1)

            combine(0, 0, 0)
            make_z(0)
            combine(1, 1, 0)
            make_h(0, 0)
            skewed(dve, stage7)
            silu(B - 1, 1)
            stage_end(dve, 7)

            st.done(TS(gm, gate, 0.0, None, ALU.min))
            dve.wait_ge(s_ln_high, 1)
            TT(gb, gm, ga, SUB).then_inc(s_log, 1)
            dve.wait_ge(s_ln_high, 2)
            TT(gate_hl[:, 1, :], gate, gate_hl[:, 0, :], SUB)
            stage_end(dve, 8)

            with dve.Fori(0, B) as b:
                for p in range(DK // 2):
                    n = b * (DK // 2) + p
                    dve.wait_ge(S("r1_e"), at(n))
                    scan("r1_", n, p, bank(2, 2))
                    read_out("r1_", n, p)
            stage_end(dve, 9)

            dve.wait_ge(s_nrm, 4)
            V.reciprocal(rn[:, 0:512], nrm[:, 0:512]).then_inc(s_rn, 1)
            for b in range(B):
                u = b % 2
                dve.wait_ge(S("rms_spread"), at(b))
                TT(y[u], o1[:, bts(b, T)], bank(3 + u), MUL).then_inc(S("y1_raw"), 1)
                dve.wait_ge(S("y1_raw"), at(b))
                dve.wait_ge(S("proj_o1"), at(b, 2))
                STT(out=yg[u], in0=y[u], scalar=cols[:, RMSW:RMSW + 1], in1=sg1[:, bts(b, T)],
                    op0=MUL, op1=MUL).then_inc(S("yg1_ready"), 1)
                if b >= 1:
                    add_projection(b - 1, z, "proj_o1", "z_added")
            add_projection(B - 1, z, "proj_o1", "z_added")
            dve.wait_ge(S("stats"), at(3 * B - 1))
            norm_scalars(st, 2)
            stage_end(dve, 10)

            links11 = LoopSteps(dve, s_links, B * (ROUTE + PLACE) + B * (COMBINE + MAKE_Z + MAKE_H), 2)

            def mlp_add(b, u):
                xs, zs = resid[:, bts(b, NT), :], z[:, bts(b, NT), :]
                links11.round(b)
                links11.done(TT(xs, xs, zs, ADD))
                links11.done(TT(xs, xs, bcast[:, 24:152].unsqueeze(1).to_broadcast([128, NT, C]), ADD))
                dve.wait_ge(S("mlp_mm"), at(b))
                TT(xs, xs, bank(4 + u).rearrange("p (n c) -> p n c", c=C), ADD).then_inc(S("mlp_added"), 1)
                dve.wait_ge(S("mlp_added"), at(b))
                tile_stats(resid, b).then_inc(S("stats"), 1)

            def stage11(b, u, first, last, i):
                if not last:
                    xn_ahead(b + 1, 1 - u, z, "tr11", "xn11")
                if not first:
                    mlp_add(b - 1, 1 - u)

            xn_ahead(0, 0, z, "tr11", "xn11")
            skewed(dve, stage11)
            mlp_add(B - 1, 1)
            dve.wait_ge(S("stats"), at(4 * B - 1))
            norm_scalars(st, 3)
            stage_end(dve, 11)

            def over(v, E):
                return v.unsqueeze(2).to_broadcast([128, TILES, E])

            def one_hot(dst, k, E):
                return TT(dst, iota[:, 0:E].unsqueeze(1).to_broadcast([128, TILES, E]), over(idf[:, :, k], E), ALU.is_equal)

            def stage12(b, u, first, last, i):
                if not last:
                    xn_ahead(b + 1, 1 - u, resid, "tr12", "xn12")
                dve.wait_ge(S("x_high"), at(b))
                TT(x_hl[:, 1, bts(b, T)], xT[u], x_hl[:, 0, bts(b, T)], SUB).then_inc(S("x_low"), 1)
                dve.wait_ge(S("lg12_mm"), at(b))
                TT(logits[:, bts(b, NT), :], bank(6)[:, 0:NT * E1].rearrange("p (n e) -> p n e", e=E1),
                   bcast[:, 8:8 + E1].unsqueeze(1).to_broadcast([128, NT, E1]), ADD).then_inc(S("lg12_added"), 1)

            xn_ahead(0, 0, resid, "tr12", "xn12")
            skewed(dve, stage12)
            dve.wait_ge(S("lg12_added"), at(B - 1))
            st.done(V.tensor_reduce(out=tmpa[:, :], in_=logits, axis=AX, op=MAX))
            TT(logits, logits, over(tmpa[:, :], E1), SUB).then_inc(s_diff, 1)
            dve.wait_ge(s_exp, 2)
            st.done(V.tensor_reduce(out=tmpa[:, :], in_=coef1[:, :, :], axis=AX, op=ADD))
            st.done(V.reciprocal(tmpa[:, :], tmpa[:, :]))
            st.done(TT(logits, coef1[:, :, :], over(tmpa[:, :], E1), MUL))
            for g in range(TILES):
                last = V.max(top[:, g, :], logits[:, g, :])
            st.done(last)
            V.tensor_reduce(out=tmpb[:, :], in_=top[:, :, 0:TOP1], axis=AX, op=ADD)
            for g in range(TILES):
                last = V.max_index(idx[:, g, :], top[:, g, :], logits[:, g, :])
            st.done(last)
            V.tensor_copy(idf, idx[:, :, 0:4])
            st.done(V.reciprocal(tmpb[:, :], tmpb[:, :]))
            st.done(TT(top[:, :, 0:TOP1], top[:, :, 0:TOP1], over(tmpb[:, :], TOP1), MUL))
            for k in range(TOP1):
                st.done(one_hot(oh, k, E1))
                if k == 0:
                    st.done(TT(coef1[:, :, :], oh, over(top[:, :, k], E1), MUL))
                else:
                    st.done(TT(ohw, oh, over(top[:, :, k], E1), MUL))
                    st.done(TT(coef1[:, :, :], coef1[:, :, :], ohw, ADD))
            TS(mb2[:, :], mb2[:, :], SCALE, None, MUL)
            TS(coef1[:, :, :], coef1[:, :, :], 1.0 / SCALE, None, MUL)
            stage_end(dve, 12)

            with dve.Fori(0, B) as b:
                for e in range(E1):
                    n = b * E1 + e
                    dve.wait_ge(S("m1_out_mm"), at(n))
                    dve.wait_ge(S("m1_acc"), at(n, 1))
                    for t in range(NT):
                        g = b * NT + t
                        last = STT(out=resid[:, g, :], in0=bank(4 + e % 2)[:, t * C:(t + 1) * C],
                                   scalar=coef1[:, g, e:e + 1], in1=resid[:, g, :], op0=MUL, op1=ADD)
                    last.then_inc(S("m1_acc"), 1)
                    if e == 6:
                        dve.wait_ge(S("m1_acc"), at(n))
                        dve.wait_ge(S("m1_bias_mm"), at(b))
                        xs = resid[:, bts(b, NT), :]
                        TT(xs, xs, bank(7).rearrange("p (n c) -> p n c", c=C), ADD).then_inc(S("m1_bias"), 1)
                        dve.wait_ge(S("m1_bias"), at(b))
            dve.drain().then_inc(stage_done, 1)

        @block.tensor
        def _(pe):
            def mm(o, l, r, start=True, stop=True):
                return nc.tensor.matmul(o, l, r, start=start, stop=stop)

            def tile(v, t):
                return v[:, t * 128:(t + 1) * 128]

            def transposes(dst, src):
                for t in range(NT):
                    last = nc.tensor.transpose(tile(dst, t), src[:, t, :], ident[:, :])
                return last

            def tokens_out(dst, act_T, w):
                for t in range(NT):
                    last = mm(tile(dst, t), tile(act_T, t), w)
                return last

            start_signals(pe, "pe")
            pe.wait_ge(s_const, 1)
            pe.wait_ge(s_w, 16 * W_LOADS)
            nc.tensor.transpose(bank(0)[:, 0:76], rows[:, :], ident[0:76, 0:76])
            mm(bank(1)[:, 0:152], ones[0:1, :], brow[:, :]).then_inc(s_colsT, 1)
            stage_end(pe, 0)

            def transpose_ahead(b, u, ready, copied, done):
                pe.wait_ge(S(ready), at(b))
                pe.wait_ge(S(copied), at(b, 2))
                transposes(bank(u), xn[u]).then_inc(S(done), 1)

            def stage1(b, u, first, last, i):
                if not last:
                    transpose_ahead(b + 1, 1 - u, "xn1", "xT1", "tr1")
                pe.wait_ge(S("xT1"), at(b))
                for n, w, free, done in ((2, w_q, "q_copied", "proj_q"), (3, w_k, "k_copied", "proj_k"),
                                         (6, w_brep, "beta", "proj_b"), (5, w_g, "sg_1", "proj_g"),
                                         (4, w_v, "v_copied", "proj_v")):
                    pe.wait_ge(S(free), at(b, 1))
                    mm(bank(n), w[:, :], xT[u]).then_inc(S(done), 1)

            transpose_ahead(0, 0, "xn1", "xT1", "tr1")
            skewed(pe, stage1)
            stage_end(pe, 1)

            for b in range(B):
                window = headsum[:, 112 - H * b:240 - H * b]
                pe.wait_ge(S("sq_k"), at(b))
                mm(bank(0), window, sq[b % 2], start=b == 0, stop=b == B - 1)
                mm(bank(1), window, sqk[b % 2], start=b == 0, stop=b == B - 1).then_inc(S("ss_k"), 1)
            pe.wait_ge(s_rn, 2)
            for b in range(B):
                pe.wait_ge(S("bk_in"), at(b, 2))
                mm(bank(4 + b % 2), expand[:, b, :], rn[:, 512:1024]).then_inc(S("rk_mm"), 1)
                pe.wait_ge(S("q_norm"), at(b, 2))
                mm(bank(2 + b % 2), expand[:, b, :], rn[:, 0:512]).then_inc(S("rq_mm"), 1)
            stage_end(pe, 2)

            def picked_pair(dst, weights, src, b):
                for j in range(2):
                    for s in range(2):
                        last = mm(bank(dst + j), weights(j), src[:, s, bts(b, T)], start=s == 0, stop=s == 1)
                return last

            def beta_k(b, p):
                n = b * (D // 2) + p
                pe.wait_ge(S("r0_coef"), at(n, 2))
                picked_pair(2 * (p % 2), lambda j: pick[:, 2 * p + j, :], bk_hl, b).then_inc(S("r0_bk"), 1)

            def sum_up(pre, b, p, u, pairs):
                n = b * pairs + p
                pe.wait_ge(S(pre + "prod"), at(n))
                if p == 0:
                    pe.wait_ge(S(pre + "o"), at(b, 2))
                for j in range(2):
                    last = mm(bank(6 + u), ident[:, :], prod[p % 2][:, j, :],
                              start=p == 0 and j == 0, stop=p == pairs - 1 and j == 1)
                last.then_inc(S(pre + "acc"), 1)

            def recur0(b, u, first=False, last=False):
                P = D // 2
                for p in range(P):
                    n = b * P + p
                    pe.wait_ge(S("r0_prod"), at(n, 1))
                    picked_pair(4, lambda j: pick[:, 2 * p + j, :], q_hl, b).then_inc(S("r0_q"), 1)
                    if p < P - 2:
                        beta_k(b, p + 2)
                    elif not last:
                        beta_k(b + 1, p + 2 - P)
                    if p:
                        sum_up("r0_", b, p - 1, u, P)
                    elif not first:
                        sum_up("r0_", b - 1, P - 1, 1 - u, P)

            beta_k(0, 0)
            beta_k(0, 1)
            recur0(0, 0, first=True)
            recur0(1, 1)
            with pe.Fori(1, B // 2 - 1) as i:
                for u in range(2):
                    recur0(2 * i + u, u)
            recur0(B - 2, 0)
            recur0(B - 1, 1, last=True)
            sum_up("r0_", B - 1, D // 2 - 1, 1, D // 2)
            stage_end(pe, 3)

            def variance(b):
                pe.wait_ge(S("o_sq"), at(b))
                mm(bank(2)[0:B, :], meanrow[:, 7 - b:15 - b], sq[b % 2],
                   start=b == 0, stop=b == B - 1).then_inc(S("o_var"), 1)

            for b in range(B):
                pe.wait_ge(S("o_sq"), at(b, 2))
                mm(bank(b % 2), center[:, :], o0[:, bts(b, T)]).then_inc(S("centred"), 1)
                if b:
                    variance(b - 1)
            variance(B - 1)
            pe.wait_ge(s_rn, 3)

            def project0(b):
                u = b % 2
                pe.wait_ge(S("yg_ready"), at(b))
                pe.wait_ge(S("x_added"), at(b, 2))
                tokens_out(bank(5 + u), yg[u], w_o[:, :]).then_inc(S("proj_o"), 1)

            for b in range(B):
                pe.wait_ge(S("y_raw"), at(b, 2))
                mm(bank(3 + b % 2), spread[:, b, :], rn[0:B, 0:512]).then_inc(S("o_spread"), 1)
                if b:
                    project0(b - 1)
            project0(B - 1)
            stage_end(pe, 4)

            def count_picks(b, u):
                pe.wait_ge(S("picked"), at(b))
                pe.wait_ge(S("placed"), at(b, 1))
                N = NT * E0
                mm(bank(7)[:, 0:N], tri[:, :], picked[u][:, 0:N], stop=False)
                for t in range(1, NT):
                    mm(bank(7)[:, t * E0:N], ones16[:, :], picked[u][:, 0:N - t * E0], start=False, stop=t == NT - 1)
                for t in range(NT):
                    last = mm(bank(7)[:, N:N + E0], ones16[:, :], picked[u][:, t * E0:(t + 1) * E0],
                              start=t == 0, stop=t == NT - 1)
                last.then_inc(S("counts"), 1)

            def router_hidden(b, u):
                pe.wait_ge(S("xT5"), at(b))
                for h in range(HC0):
                    pe.wait_ge(S("hid5"), at(b * HC0 + h, HC0))
                    mm(bank(2 + h), tile(w_r1, h), xT[u]).then_inc(S("hid5_mm"), 1)

            def stage5(b, u, first, last, i):
                if there(b, 1):
                    router_hidden(b + 1, 1 - u)
                if there(b, 2):
                    transpose_ahead(b + 2, u, "xn5", "xT5", "tr5")
                pe.wait_ge(S("hid5"), at(b * HC0 + HC0 - 1))
                pe.wait_ge(S("lg5_added"), at(b, 1))
                for h in range(HC0):
                    last_mm = mm(bank(6)[0:E0, :], w_r2[:, h, :], hid[u][:, h, :], start=h == 0, stop=h == HC0 - 1)
                last_mm.then_inc(S("lgT5_mm"), 1)
                if not first:
                    count_picks(b - 1, 1 - u)
                pe.wait_ge(S("lg5_T"), at(b))
                wait_apart(pe)
                for t in range(NT):
                    last_mm = nc.tensor.transpose(bank(6)[:, t * E0:(t + 1) * E0], tile(lg5_T, t), ident[0:E0, 0:E0])
                last_mm.then_inc(S("lg5_mm"), 1)

            transpose_ahead(0, 0, "xn5", "xT5", "tr5")
            router_hidden(0, 0)
            transpose_ahead(1, 1, "xn5", "xT5", "tr5")
            skewed(pe, stage5)
            count_picks(B - 1, 1)
            stage_end(pe, 5)

            def transpose_rows(e):
                pe.wait_ge(s_disp[e // 2], 16)
                pe.wait_ge(S("xdT"), at(e, 2))
                transposes(bank(e % 2), xd[:, bts(e, NT), :]).then_inc(S("trd"), 1)

            def hidden0(e):
                pe.wait_ge(S("xdT"), at(e))
                for h in range(HC0):
                    pe.wait_ge(S("m0_hid"), at(e * HC0 + h, HC0))
                    mm(bank(2 + h), e0w1[:, e, h * 128:(h + 1) * 128], xdT[e % 2]).then_inc(S("m0_hid_mm"), 1)

            def outputs0(e):
                pe.wait_ge(S("m0_hid"), at(e * HC0 + HC0 - 1))
                pe.wait_ge(S("eo"), at(e, 2))
                for t in range(NT):
                    for h in range(HC0):
                        last = mm(tile(bank(6 + e % 2), t), tile(hid[e % 2][:, h, :], t), e0w2[:, e, h, :],
                                  start=h == 0, stop=h == HC0 - 1)
                last.then_inc(S("m0_out_mm"), 1)

            for e in range(E0):
                last = mm(tile(bank(6 + e // 4), e % 4), spread[:, e, :], eb2[:, :])
            last.then_inc(s_eb2_mm, 1)
            pe.wait_ge(s_wm0, 32)
            transpose_rows(0)
            transpose_rows(1)
            hidden0(0)
            pe.wait_ge(s_eb2, 1)
            for e in range(E0):
                if e < E0 - 1:
                    hidden0(e + 1)
                if e < E0 - 2:
                    transpose_rows(e + 2)
                outputs0(e)
            stage_end(pe, 6)

            def stage7(b, u, first, last, i):
                h_T = xT[u]
                pe.wait_ge(S("hT7"), at(b))
                pe.wait_ge(S("g1"), at(b, 1))
                mm(bank(4)[0:16, :], u_gk1[:, :], h_T).then_inc(S("g1_mm"), 1)
                pe.wait_ge(S("kq_low"), at(b, 1))
                mm(bank(6), u_kq[:, :, :].rearrange("p s n -> p (s n)"), h_T).then_inc(S("kq_mm"), 1)
                pe.wait_ge(S("v_copied7"), at(b, 1))
                mm(bank(2), u_v[:, :], h_T).then_inc(S("v_mm7"), 1)
                pe.wait_ge(S("sg_7"), at(b, 2))
                mm(bank(3 + 4 * u), u_g[:, :], h_T).then_inc(S("g_mm7"), 1)
                pe.wait_ge(S("g1"), at(b))
                pe.wait_ge(S("gk_copied"), at(b, 1))
                mm(bank(5)[64 * u:64 * u + 64, :], u_gk2[:, :], g1s).then_inc(S("gk_mm"), 1)
                if not last:
                    transpose_ahead(b + 1, 1 - u, "xn7", "hT7", "tr7")

            transpose_ahead(0, 0, "xn7", "hT7", "tr7")
            skewed(pe, stage7)
            stage_end(pe, 7)
            stage_end(pe, 8)

            def recur1(b, half, u, first=False):
                P = DK // 2
                for p in range(P):
                    n = b * P + p
                    pe.wait_ge(S("r1_coef"), at(n, 1))
                    picked_pair(0, lambda j: pickg[:, 0, 2 * p + j, :], kq_hl, b).then_inc(S("r1_k"), 1)
                    pe.wait_ge(S("r1_scanned"), at(n, 1))
                    picked_pair(2, lambda j: pickg[:, u, 2 * p + j, :], gate_hl, half).then_inc(S("r1_e"), 1)
                    pe.wait_ge(S("r1_prod"), at(n, 1))
                    picked_pair(4, lambda j: pickg[:, 1, 2 * p + j, :], kq_hl, b).then_inc(S("r1_q"), 1)
                    if p:
                        sum_up("r1_", b, p - 1, u, P)
                    elif not first:
                        sum_up("r1_", b - 1, P - 1, 1 - u, P)

            recur1(0, 0, 0, first=True)
            recur1(1, 0, 1)
            with pe.Fori(1, B // 2) as i:
                for u in range(2):
                    recur1(2 * i + u, i, u)
            sum_up("r1_", B - 1, DK // 2 - 1, 1, DK // 2)
            stage_end(pe, 9)

            for b in range(B):
                pe.wait_ge(S("o1_sq"), at(b))
                mm(bank(0), headsum[:, 112 - H * b:240 - H * b], sq[b % 2],
                   start=b == 0, stop=b == B - 1).then_inc(S("rms_mm"), 1)
            pe.wait_ge(s_rn, 4)

            def project1(b):
                u = b % 2
                pe.wait_ge(S("yg1_ready"), at(b))
                pe.wait_ge(S("z_added"), at(b, 2))
                tokens_out(bank(5 + u), yg[u], u_o[:, :]).then_inc(S("proj_o1"), 1)

            for b in range(B):
                pe.wait_ge(S("y1_raw"), at(b, 2))
                mm(bank(3 + b % 2), expand[:, b, :], rn[:, 0:512]).then_inc(S("rms_spread"), 1)
                if b:
                    project1(b - 1)
            project1(B - 1)
            stage_end(pe, 10)

            def mlp_out(b, u):
                pe.wait_ge(S("hid11"), at(2 * b + 1))
                pe.wait_ge(S("mlp_added"), at(b, 2))
                for t in range(NT):
                    for h in range(2):
                        last = mm(tile(bank(4 + u), t), tile(hid[u][:, h, :], t), u_2[:, h, :],
                                  start=h == 0, stop=h == 1)
                last.then_inc(S("mlp_mm"), 1)

            def stage11(b, u, first, last, i):
                pe.wait_ge(S("hT11"), at(b))
                for h in range(2):
                    pe.wait_ge(S("hid11"), at(2 * b + h, 2))
                    mm(bank(2 + h), tile(u_1, h), hT2[u]).then_inc(S("hid11_mm"), 1)
                if not last:
                    transpose_ahead(b + 1, 1 - u, "xn11", "hT11", "tr11")
                if not first:
                    mlp_out(b - 1, 1 - u)

            transpose_ahead(0, 0, "xn11", "hT11", "tr11")
            skewed(pe, stage11)
            mlp_out(B - 1, 1)
            stage_end(pe, 11)

            def stage12(b, u, first, last, i):
                if not last:
                    transpose_ahead(b + 1, 1 - u, "xn12", "xs12", "tr12")
                pe.wait_ge(S("xs12"), at(b))
                pe.wait_ge(S("lg12_added"), at(b, 1))
                for t in range(NT):
                    last_mm = mm(bank(6)[:, t * E1:(t + 1) * E1], tile(xT[u], t), u_r[:, :])
                last_mm.then_inc(S("lg12_mm"), 1)

            transpose_ahead(0, 0, "xn12", "xs12", "tr12")
            skewed(pe, stage12)
            stage_end(pe, 12)

            PARTS = ((0, 0), (0, 1), (1, 0))
            AHEAD = 3

            def hidden1(b, e):
                for h in range(HC1):
                    n = (b * E1 + e) * HC1 + h
                    pe.wait_ge(S("m1_hid"), at(n, 4))
                    w = slice((e * HC1 + h) * 128, (e * HC1 + h) * 128 + 128)
                    for k, (sw, sx) in enumerate(PARTS):
                        last = mm(bank((e * HC1 + h) % 4), w1_hl[:, sw, w], x_hl[:, sx, bts(b, T)],
                                  start=k == 0, stop=k == len(PARTS) - 1)
                    last.then_inc(S("m1_hid_mm"), 1)

            def outputs1(b, e):
                n = b * E1 + e
                pe.wait_ge(S("m1_low"), at(n))
                pe.wait_ge(S("m1_acc"), at(n, 2))
                for t in range(NT):
                    for k, (sh, sw) in enumerate(PARTS):
                        for h in range(HC1):
                            w = slice((e * HC1 + h) * 128, (e * HC1 + h) * 128 + 128)
                            part = (h_high, h_low)[sh][e % 4][:, h * T + t * 128:h * T + t * 128 + 128]
                            last = mm(tile(bank(4 + e % 2), t), part, w2_hl[:, sw, w],
                                      start=k == 0 and h == 0, stop=k == len(PARTS) - 1 and h == HC1 - 1)
                last.then_inc(S("m1_out_mm"), 1)

            def bias_term(b):
                pe.wait_ge(S("m1_cs"), at(b))
                pe.wait_ge(S("m1_cT"), at(b, 1))
                for t in range(NT):
                    last = nc.tensor.transpose(tile(bank(6)[0:E1, :], t), cstage[:, t, :], ident[:, :])
                last.then_inc(S("m1_cT_mm"), 1)

            def all_experts(b, last_batch):
                for e in range(E1):
                    if e < E1 - AHEAD:
                        hidden1(b, e + AHEAD)
                    elif not last_batch:
                        hidden1(b + 1, e + AHEAD - E1)
                    outputs1(b, e)
                    if e == 1:
                        bias_term(b)
                    if e == 5:
                        pe.wait_ge(S("m1_cT"), at(b))
                        pe.wait_ge(S("m1_bias"), at(b, 1))
                        tokens_out(bank(7), cT, mb2[:, :]).then_inc(S("m1_bias_mm"), 1)

            for e in range(AHEAD):
                hidden1(0, e)
            with pe.Fori(0, B - 1) as b:
                all_experts(b, False)
            all_experts(B - 1, True)
            pe.drain().then_inc(stage_done, 1)


W_LOADS = 34

_INS = ["L0_attn_x", "L0_attn_Wq", "L0_attn_Wk", "L0_attn_Wv", "L0_attn_Wbeta", "L0_attn_Wg", "L0_attn_Wout",
        "L0_attn_ln_g", "L0_attn_ln_b", "L0_ffn_rw1", "L0_ffn_rb1", "L0_ffn_rw2", "L0_ffn_rb2", "L0_ffn_ew1",
        "L0_ffn_eb1", "L0_ffn_ew2", "L0_ffn_eb2", "L1_attn_ln_w", "L1_attn_ln_b", "L1_attn_Wq", "L1_attn_Wk",
        "L1_attn_Wv", "L1_attn_gk_w1", "L1_attn_gk_w2", "L1_attn_gk_b2", "L1_attn_Wg", "L1_attn_rms_w", "L1_attn_Wo",
        "L1_attn_W1", "L1_attn_b1", "L1_attn_W2", "L1_attn_b2", "L1_ffn_router_w", "L1_ffn_router_b", "L1_ffn_w1",
        "L1_ffn_b1", "L1_ffn_w2", "L1_ffn_b2"]


def kernel(**inputs):
    import numpy as _np
    import concourse.bacc as _bacc
    from concourse import mybir as _mybir
    from concourse.bass_utils import run_bass_kernel_spmd as _run

    nc = _bacc.Bacc("TRN2", target_bir_lowering=False, num_devices=1)
    arrays, aps = {}, {}
    for name in _INS:
        a = _np.ascontiguousarray(inputs[name])
        arrays["in_" + name] = a
        aps[name] = nc.dram_tensor("in_" + name, a.shape, _mybir.dt.from_np(a.dtype), kind="ExternalInput").ap()
    shape = inputs["L0_attn_x"].shape
    out = nc.dram_tensor("out_x", shape, _mybir.dt.float32, kind="ExternalOutput").ap()
    build(nc, aps, out)
    r = _run(nc, [arrays], core_ids=[0])
    return r.results[0]["out_x"]
```

```python
import concourse.bass as bass
from concourse import mybir
from contextlib import ExitStack


class Steps:

    def __init__(self, eng, sem):
        self.eng, self.sem, self.count = eng, sem, 0

    def done(self, ins):
        ins.then_inc(self.sem, 1)
        self.count += 1
        self.eng.wait_ge(self.sem, self.count)


class LoopSteps:

    def __init__(self, eng, sem, base, per_round):
        self.eng, self.sem, self.base, self.per_round, self.value = eng, sem, base, per_round, 0

    def round(self, r, earlier=0):
        self.value = r * self.per_round + (self.base + earlier)

    def done(self, ins):
        ins.then_inc(self.sem, 1)
        self.value = self.value + 1
        self.eng.wait_ge(self.sem, self.value)


def build(nc, I, out):
    f32, f16, i32, u32 = mybir.dt.float32, mybir.dt.float16, mybir.dt.int32, mybir.dt.uint32
    ALU = mybir.AluOpType
    ACT = mybir.ActivationFunctionType
    AX = mybir.AxisListType.X
    MUL, ADD, SUB, MAX = ALU.mult, ALU.add, ALU.subtract, ALU.max

    B, T, C = I["L0_attn_x"].shape
    NT = T // 128
    TILES = B * NT
    H = 16
    D = C // H
    DK = 4
    E0, TOP0, CAP, HC0 = 8, 2, 512, 4
    ROWS = E0 * CAP
    E1, TOP1, HC1 = 16, 4, 2
    EPS = 1e-5
    GATE_NORM = 16.0
    SCALE = 1024.0
    bts = bass.ts

    ctx = ExitStack()
    with ctx:
        def sb(name, shape, dt=f32):
            return ctx.enter_context(nc.sbuf_tensor(name, shape, dt))

        def sem(name):
            return ctx.enter_context(nc.semaphore(name))

        resid = sb("resid", [128, TILES, C])
        A = [sb(f"A{n}", [128, B * T]) for n in range(1, 8)]
        A1, A2, A3, A4, A5, A6, A7 = A
        scratch = sb("scratch", [128, 11 * 1024])

        def carve(k, n=1):
            return scratch[:, k * 1024:(k + n) * 1024]

        ident = sb("ident", [128, 128])
        ones = sb("ones", [128, 128])
        center = sb("center", [128, 128])
        ones16 = sb("ones16", [128, 128], f16)
        tri = sb("tri", [128, 128], f16)
        headsum = sb("headsum", [128, 240])
        expand = sb("expand", [128, B, 128])
        meanrow = sb("meanrow", [128, 15])
        spread = sb("spread", [8, B, 128])
        pick = sb("pick", [128, D, 128], f16)
        pickg = sb("pickg", [128, 2, DK, 128], f16)
        iota_i = sb("iota_i", [128, E1], i32)
        iota = sb("iota", [128, E1])
        epsc = sb("epsc", [128, 1])

        rows = sb("rows", [76, 128])
        cols = sb("cols", [128, 76])
        brow = sb("brow", [1, 152])
        bcast = sb("bcast", [128, 152])
        LNG, LNB, RB1, EB1, LNW1, LNB1, AB1, MB1, GKB, RMSW = 0, 1, 2, 6, 38, 39, 40, 42, 74, 75

        w_q, w_k, w_v, w_g, w_o = (sb(n, [128, 128]) for n in ("w_q", "w_k", "w_v", "w_g", "w_o"))
        w_b = sb("w_b", [128, H])
        w_brep = sb("w_brep", [128, 128])
        w_r1 = sb("w_r1", [128, 512])
        w_r2 = sb("w_r2", [128, HC0, E0])
        eb2 = sb("eb2", [E0, C])
        u_kq = sb("u_kq", [128, 2, 64])
        u_v, u_g, u_o = (sb(n, [128, 128]) for n in ("u_v", "u_g", "u_o"))
        u_gk1, u_gk2 = sb("u_gk1", [128, 16]), sb("u_gk2", [16, 64])
        u_1, u_2 = sb("u_1", [128, 256]), sb("u_2", [128, 2, C])
        u_r = sb("u_r", [128, E1])
        mb2 = sb("mb2", [E1, C])

        stats = sb("stats", [128, TILES, 6])
        mean = sb("mean", [128, TILES])
        var = sb("var", [128, TILES])
        rstd = sb("rstd", [128, TILES])
        tmpa = sb("tmpa", [128, TILES])
        tmpb = sb("tmpb", [128, TILES])
        coef1 = sb("coef", [128, TILES, E1])

        PS = ctx.enter_context(nc.psum_tensor("PS", [128, 8, 512], f32))

        def bank(n, k=1):
            return PS[:, n, :] if k == 1 else PS[:, n:n + k, :]

        disp = nc.dram_tensor("disp", (ROWS, C), f32).ap()
        eo_rows = nc.dram_tensor("eo_rows", (ROWS, C), f32).ap()

        HEAD = 4

        def at(n, k=0):
            return n + (HEAD + 1 - k)

        SIGNALS = {
            "pool": ["bk_ready", "m1_low", "r_c", "r_pair", "yg_ready", "x_b2"],
            "act": ["xT1", "q_copied", "k_copied", "beta", "sgm1", "sq_k", "q_high", "bk_high",
                    "r_coef", "r0_decay", "r_o", "o_sq", "xT5", "hid5",
                    "xn5_kept", "lg5_T", "xdT", "m0_hid", "x_std", "m1_cs", "m1_cT", "m1_hid", "m1_high",
                    "xn7", "hT7", "kq_high", "v_copied7", "g1", "gk_copied", "sg_7", "o1_sq", "hT11", "hid11", "w_high",
                    "xs12", "x_high"],
            "dve": ["stats", "xn1", "v_copied", "sg_1", "bk_in", "q_norm", "r0_kk", "r_scanned", "r_prod",
                    "y_raw", "y_ready", "x_added", "xn5", "lg5_added", "picked", "placed", "slots", "eo", "moe_added", "x_var",
                    "m1_bias", "m1_acc", "h_scalars", "kq_low",
                    "y1_raw", "yg1_ready", "z_added",
                    "xn11", "mlp_added", "xn12", "x_low", "lg12_added"],
            "pe": ["tr1", "proj_q", "proj_k", "proj_b", "proj_g", "proj_v", "ss_k", "rk_mm", "rq_mm",
                   "r0_bk", "r_q", "r_acc", "centred", "o_var", "o_spread", "proj_o",
                   "tr5", "hid5_mm", "lgT5_mm", "lg5_mm", "counts", "trd",
                   "m0_hid_mm", "m0_out_mm", "m1_cT_mm", "m1_hid_mm", "m1_out_mm", "m1_bias_mm",
                   "tr7", "kq_mm", "v_mm7", "g_mm7", "g1_mm", "gk_mm", "r1_k", "r1_e",
                   "rms_mm", "rms_spread", "proj_o1", "tr11", "hid11_mm", "mlp_mm", "tr12", "lg12_mm"],
        }
        signals = {n: sem(n) for v in SIGNALS.values() for n in v}

        def S(name):
            return signals[name]

        def start_signals(eng, who):
            for n in SIGNALS[who]:
                eng.sem_inc(S(n), HEAD)

        s_x = [sem(f"x_loaded{k}") for k in range(2)]
        stage_done, s_w0, s_w, s_wm0, s_wm1, s_out = (
            sem(n) for n in ("stage_done", "w0_loaded", "w_loaded", "moe0_loaded", "moe1_loaded", "out_written"))
        s_const, s_colsT = sem("consts_ready"), sem("cols_transposed")
        s_nrm, s_rn = sem("norms"), sem("norm_reciprocals")
        s_diff, s_exp = sem("logits_less_largest"), sem("their_exp")
        s_eb2_mm, s_eb2 = sem("eb2_spread"), sem("eb2_copied")
        s_zeroed, s_scattered, s_eo = sem("disp_zeroed"), sem("tokens_scattered"), sem("eo_written")
        s_disp = [sem(f"disp_loaded{k}") for k in range(E0 // 2)]
        s_gathered = [sem(f"eo_gathered{u}") for u in range(2)]
        s_ln_high, s_log = sem("gate_ln_then_high"), sem("gate_log")
        s_routed = sem("layer1_routed")
        s_carried = sem("waits_carried")
        s_dve, s_links = sem("dve_steps"), sem("dve_loop_steps")
        s_act = sem("act_steps8")
        s_pool = sem("pool_steps0")
        s_var, s_std = sem("token_variances"), sem("token_deviations")

        LAYER0, LAYER1 = (0, 0), (B * D // 2, B)

        def stage_end(eng, k):
            eng.drain().then_inc(stage_done, 1)
            eng.wait_ge(stage_done, 4 * (k + 1))

        def wait_apart(eng):
            eng.sem_inc(s_carried, 1)

        def skewed(eng, body):
            for b in range(2):
                body(b, b % 2, b == 0, False, 0)
            with eng.Fori(1, B // 2 - 1) as i:
                for u in range(2):
                    body(2 * i + u, u, False, False, i)
            for b in range(B - 2, B):
                body(b, b % 2, False, b == B - 1, b // 2)

        def there(b, k):
            return not isinstance(b, int) or b + k < B

        q0, k0, v0, sg0, bk0 = A1, A2, A3, A4, A5
        q_hl = A6[:, :].bitcast(f16).rearrange("p (s n) -> p s n", s=2)
        bk_hl = A7[:, :].bitcast(f16).rearrange("p (s n) -> p s n", s=2)
        o0 = A1
        xn5 = A3[:, :].rearrange("p (n c) -> p n c", c=C)
        eb2_rep = A2[:, 0:E0 * C].rearrange("p (e c) -> p e c", c=C)
        xd = A5[:, :].rearrange("p (n c) -> p n c", c=C)
        eo = A4[:, :].rearrange("p (n c) -> p n c", c=C)
        e0w1 = A6[:, :].rearrange("p (e h) -> p e h", e=E0)
        e0w2 = A7[:, :].rearrange("p (e i c) -> p e i c", e=E0, c=C)
        z = A1[:, :].rearrange("p (n c) -> p n c", c=C)
        v1, sg1 = A3, A4
        kq_hl = A2[:, :].bitcast(f16).rearrange("p (s n) -> p s n", s=2)
        gate = A5[:, 0:2048]
        gate_hl = A5[:, 2048:4096].bitcast(f16).rearrange("p (s n) -> p s n", s=2)
        o1 = A3
        x_hl = A2[:, :].bitcast(f16).rearrange("p (s n) -> p s n", s=2)
        e1w1, e1w2 = A6, A7
        WC = E1 * HC1 * 128 // B
        w1_hl = A3[:, :].bitcast(f16).rearrange("p (s n) -> p s n", s=2)
        w2_hl = A4[:, :].bitcast(f16).rearrange("p (s n) -> p s n", s=2)

        xn = [carve(0)[:, u * 512:(u + 1) * 512].rearrange("p (n c) -> p n c", c=C) for u in range(2)]
        xT = [carve(1)[:, u * 512:(u + 1) * 512] for u in range(2)]

        def halves(k):
            return [carve(k)[:, u * 512:(u + 1) * 512] for u in range(2)]

        sgm = halves(2)

        def pair(k):
            return carve(k).rearrange("p (j t) -> p j t", j=2)

        cs = [pair(0), pair(1)]
        kk = [pair(2), pair(3)]
        decay = [pair(4), pair(5)]
        cbuf = [pair(6), pair(7)]
        state = pair(8)
        prod = [pair(9), pair(10)]

        y = halves(3)
        yg = halves(4)
        sq = halves(5)
        sqk = halves(6)
        nrm = carve(7)
        rn = carve(8)
        hid = [carve(2 * u + 2, 2).rearrange("p (i t) -> p i t", i=4) for u in range(2)]
        cstage = carve(2)[:, 0:64].rearrange("p (n e) -> p n e", n=4)
        cT = carve(2)[0:16, 512:1024]
        g1s = carve(7)[0:16, 0:512]
        hT2 = halves(8)
        h_full = [carve(n) for n in range(2)]
        h_high = [carve(4 + n)[:, 0:512].bitcast(f16) for n in range(4)]
        h_low = [carve(4 + n)[:, 512:1024].bitcast(f16) for n in range(4)]
        logits = carve(9)[:, 0:512].rearrange("p (n e) -> p n e", n=TILES)
        ga, gb, gm = (scratch[:, 2048 * k:2048 * (k + 1)] for k in range(3))

        top = carve(10)[:, 0:256].rearrange("p (n e) -> p n e", e=8)
        idx = carve(10)[:, 256:512].bitcast(u32).rearrange("p (n e) -> p n e", e=8)
        idf = carve(10)[:, 512:640].rearrange("p (n e) -> p n e", e=4)
        top0 = carve(10)[:, 0:64].rearrange("p (k n) -> p k n", k=TOP0)
        keep = carve(10)[:, 64:128].rearrange("p (k n) -> p k n", k=TOP0)
        coef0 = carve(10)[:, 128:192].rearrange("p (k n) -> p k n", k=TOP0)
        slot = carve(10)[:, 192:256].bitcast(i32).rearrange("p (k n) -> p k n", k=TOP0)
        slot_to = carve(10)[:, 256:320].bitcast(i32).rearrange("p (k n) -> p k n", k=TOP0)
        small = carve(9)

        def routing(col, n, dt=f32):
            return [small[:, 512 * u + col:512 * u + col + n].bitcast(dt) if dt != f32
                    else small[:, 512 * u + col:512 * u + col + n] for u in range(2)]

        def by_expert(v):
            return v.rearrange("p (n e) -> p n e", e=E0)

        lg5 = [by_expert(v) for v in routing(0, 32)]
        top5 = [by_expert(v) for v in routing(32, 32)]
        idx5 = [by_expert(v) for v in routing(64, 32, u32)]
        picked = routing(96, 32, f16)
        oh5 = [v.rearrange("p (k n e) -> p k n e", k=TOP0, e=E0) for v in routing(128, 64)]
        id5 = [v.rearrange("p (k n) -> p k n", k=TOP0) for v in routing(192, 8)]
        lg5_T = carve(8)[0:E0, 512:1024]
        place = by_expert(carve(8)[:, 0:32])
        placed = carve(8)[:, 32:96].rearrange("p (k n e) -> p k n e", k=TOP0, e=E0)
        pos, clipped, over_cap, row = (carve(8)[:, 96 + 8 * k:104 + 8 * k].rearrange("p (k n) -> p k n", k=TOP0)
                                       for k in range(4))
        carry = carve(8)[:, 128:136]
        xdT = halves(0)
        fetched = [v[:, :].rearrange("p (n c) -> p n c", c=C) for v in (A6, A7)]
        oh, ohw = (carve(8)[:, k * 512:(k + 1) * 512].rearrange("p (n e) -> p n e", e=E1) for k in range(2))

        block = ctx.enter_context(nc.Block())

        @block.sync
        def _(sp):
            xv = I["L0_attn_x"].rearrange("b (n p) c -> b p n c", p=128)
            for b in range(B):
                sp.dma_start(resid[:, b * NT:(b + 1) * NT, :], xv[b]).then_inc(s_x[b // (B // 2)], 16)
            for dst, name in ((w_b, "Wbeta"), (w_q, "Wq"), (w_k, "Wk"), (w_g, "Wg"), (w_v, "Wv")):
                sp.dma_start(dst[:, :], I["L0_attn_" + name]).then_inc(s_w0, 16)
            count = 0

            def load(dst, src):
                nonlocal count
                sp.dma_start(dst, src).then_inc(s_w, 16)
                count += 1

            def row(v, n=128):
                return v.rearrange("(a n) -> a n", n=n)

            load(w_o[:, :], I["L0_attn_Wout"])
            load(rows[LNG:LNG + 1, :], row(I["L0_attn_ln_g"]))
            load(rows[LNB:LNB + 1, :], row(I["L0_attn_ln_b"]))
            load(rows[RB1:RB1 + 4, :], row(I["L0_ffn_rb1"]))
            load(rows[EB1:EB1 + 32, :], I["L0_ffn_eb1"].rearrange("e (i n) -> (e i) n", n=128))
            load(rows[LNW1:LNW1 + 1, :], row(I["L1_attn_ln_w"]))
            load(rows[LNB1:LNB1 + 1, :], row(I["L1_attn_ln_b"]))
            load(rows[AB1:AB1 + 2, :], row(I["L1_attn_b1"]))
            load(rows[MB1:MB1 + 32, :], I["L1_ffn_b1"].rearrange("e (i n) -> (e i) n", n=128))
            for k in range(2):
                load(rows[GKB:GKB + 1, 64 * k:64 * k + 64], row(I["L1_attn_gk_b2"], 64))
            load(rows[RMSW:RMSW + 1, :].rearrange("a (h v) -> a h v", v=D),
                 row(I["L1_attn_rms_w"], D).unsqueeze(1).to_broadcast([1, H, D]))
            load(brow[:, 0:8], row(I["L0_ffn_rb2"], 8))
            load(brow[:, 8:24], row(I["L1_ffn_router_b"], 16))
            load(brow[:, 24:152], row(I["L1_attn_b2"]))
            load(w_r1[:, :], I["L0_ffn_rw1"])
            load(w_r2[:, :, :], I["L0_ffn_rw2"].rearrange("(i p) e -> p i e", p=128))
            load(eb2[:, :], I["L0_ffn_eb2"])
            load(u_kq[:, 1, :], I["L1_attn_Wq"])
            load(u_kq[:, 0, :], I["L1_attn_Wk"])
            load(u_v[:, :], I["L1_attn_Wv"])
            load(u_g[:, :], I["L1_attn_Wg"])
            load(u_o[:, :], I["L1_attn_Wo"])
            load(u_gk1[:, :], I["L1_attn_gk_w1"])
            load(u_gk2[:, :], I["L1_attn_gk_w2"])
            load(u_1[:, :], I["L1_attn_W1"])
            load(u_2[:, :, :], I["L1_attn_W2"].rearrange("(i p) c -> p i c", p=128))
            load(u_r[:, :], I["L1_ffn_router_w"])
            load(mb2[:, :], I["L1_ffn_b2"])
            assert count == W_LOADS
            sp.wait_ge(s_const, 1)
            for k in range(ROWS * C // (128 * 1024)):
                sp.dma_start(disp[bts(k, 1024), :].rearrange("(p r) c -> p (r c)", p=128), carve(10)).then_inc(s_zeroed, 16)
            sp.wait_ge(stage_done, 4 * 4)
            sp.dma_start(e0w1, I["L0_ffn_ew1"].rearrange("e c h -> c e h")).then_inc(s_wm0, 16)
            sp.dma_start(e0w2, I["L0_ffn_ew2"].rearrange("e (i p) c -> p e i c", p=128)).then_inc(s_wm0, 16)
            sp.wait_ge(s_scattered, 16 * TOP0 * TILES)
            dv, ev = (v.rearrange("(n p) c -> p n c", p=128) for v in (disp, eo_rows))
            for k in range(E0 // 2):
                sp.dma_start(xd[:, bts(k, 2 * NT), :], dv[:, bts(k, 2 * NT), :]).then_inc(s_disp[k], 16)
            for e in range(E0):
                sp.wait_ge(S("eo"), at(e))
                sp.dma_start(ev[:, bts(e, NT), :], eo[:, bts(e, NT), :]).then_inc(s_eo, 16)
            sp.wait_ge(stage_done, 4 * 8)
            sp.dma_start(e1w1[:, :].rearrange("p (e h) -> p e h", e=E1), I["L1_ffn_w1"].rearrange("e c h -> c e h")).then_inc(s_wm1, 16)
            sp.dma_start(e1w2[:, :].rearrange("p (e i c) -> p e i c", e=E1, c=C),
                         I["L1_ffn_w2"].rearrange("e (i p) c -> p e i c", p=128)).then_inc(s_wm1, 16)
            ov = out.rearrange("b (n p) c -> b p n c", p=128)
            for b in range(B):
                sp.wait_ge(S("m1_acc"), at((b + 1) * E1 - 1))
                sp.dma_start(ov[b], resid[:, b * NT:(b + 1) * NT, :]).then_inc(s_out, 16)
            sp.wait_ge(s_out, 16 * B)

        @block.gpsimd
        def _(pool):
            start_signals(pool, "pool")
            st = Steps(pool, s_pool)
            pool.memset(epsc[:, :], EPS)
            pool.memset(carve(10), 0.0)
            pool.memset(ident[:, :], 0.0)
            pool.memset(ones[:, :], 1.0)
            pool.memset(center[:, :], -1.0 / C)
            pool.memset(tri[:, :], 1.0)
            pool.memset(ones16[:, :], 1.0)
            pool.memset(headsum[:, :], 1.0)
            pool.memset(expand[:, :, :], 0.0)
            pool.memset(meanrow[:, :], 0.0)
            pool.memset(spread[:, :, :], 0.0)
            pool.memset(pick[:, :, :], 0.0)
            pool.iota(iota_i[:, :], pattern=[[1, E1]], base=0, channel_multiplier=0)
            st.done(pool.memset(pickg[:, :, :, :], 0.0))
            sel = pool.affine_select
            sel(out=ident[:, :], in_=ident[:, :], compare_op=ALU.not_equal, fill=1.0, base=0,
                pattern=[[-1, 128]], channel_multiplier=1)
            sel(out=center[:, :], in_=center[:, :], compare_op=ALU.not_equal, fill=1.0 - 1.0 / C, base=0,
                pattern=[[-1, 128]], channel_multiplier=1)
            sel(out=tri[:, :], in_=tri[:, :], compare_op=ALU.is_gt, fill=0.0, base=0,
                pattern=[[1, 128]], channel_multiplier=-1)
            sel(out=headsum[:, :], in_=headsum[:, :], compare_op=ALU.is_ge, fill=0.0, base=112 * D,
                pattern=[[-D, 240]], channel_multiplier=1)
            sel(out=expand[:, :, :].rearrange("p b (h i) -> p b h i", i=D),
                in_=expand[:, :, :].rearrange("p b (h i) -> p b h i", i=D),
                compare_op=ALU.not_equal, fill=1.0, base=0, pattern=[[-H, B], [-1, H], [0, D]], channel_multiplier=1)
            sel(out=spread[:, :, :], in_=spread[:, :, :], compare_op=ALU.not_equal, fill=1.0, base=0,
                pattern=[[-1, B], [0, 128]], channel_multiplier=1)
            pool.memset(meanrow[:, 7:8], 1.0 / C)
            sel(out=pick[:, :, :].rearrange("p j (h i) -> p j h i", i=D),
                in_=pick[:, :, :].rearrange("p j (h i) -> p j h i", i=D),
                compare_op=ALU.not_equal, fill=1.0, base=0, pattern=[[-1, D], [-D, H], [0, D]], channel_multiplier=1)
            for u in range(2):
                sel(out=pickg[:, u, :, :].rearrange("p k (h i) -> p k h i", i=D),
                    in_=pickg[:, u, :, :].rearrange("p k (h i) -> p k h i", i=D),
                    compare_op=ALU.not_equal, fill=1.0, base=-64 * u, pattern=[[-1, DK], [-DK, H], [0, D]],
                    channel_multiplier=1)
            st.done(pool.tensor_copy(iota[:, :], iota_i[:, :]))
            sel(out=headsum[:, :], in_=headsum[:, :], compare_op=ALU.is_ge, fill=0.0, base=D - 1 - 112 * D,
                pattern=[[D, 240]], channel_multiplier=-1).then_inc(s_const, 1)
            stage_end(pool, 0)
            stage_end(pool, 1)

            for b in range(B):
                c = bts(b, T)
                pool.wait_ge(S("bk_in"), at(b))
                pool.tensor_tensor(bk0[:, c], k0[:, c], bk0[:, c], MUL).then_inc(S("bk_ready"), 1)
                pool.wait_ge(S("bk_high"), at(b))
                pool.wait_ge(S("bk_ready"), at(b))
                pool.tensor_tensor(bk_hl[:, 1, c], bk0[:, c], bk_hl[:, 0, c], SUB)
            stage_end(pool, 2)

            def additions(layer, v, pairs):
                def pair_sum(n):
                    pool.wait_ge(S("r_prod"), at(n))
                    pool.tensor_tensor(prod[n % 2][:, 0, :], prod[n % 2][:, 0, :], prod[n % 2][:, 1, :],
                                       ADD).then_inc(S("r_pair"), 1)

                for b in range(B):
                    for p in range(pairs):
                        n = layer[0] + b * pairs + p
                        pool.wait_ge(S("r_coef"), at(n))
                        pool.wait_ge(S("r_scanned"), at(n, 2))
                        pool.tensor_tensor(cbuf[p % 2], cs[p % 2],
                                           v[:, bts(b, T)].unsqueeze(1).to_broadcast([128, 2, T]),
                                           MUL).then_inc(S("r_c"), 1)
                        if n > layer[0]:
                            pair_sum(n - 1)
                pair_sum(layer[0] + B * pairs - 1)

            additions(LAYER0, v0, D // 2)
            stage_end(pool, 3)

            for b in range(B):
                u = b % 2
                pool.wait_ge(S("y_ready"), at(b))
                pool.wait_ge(S("proj_o"), at(b, 2))
                pool.tensor_tensor(yg[u], y[u], sg0[:, bts(b, T)], MUL).then_inc(S("yg_ready"), 1)
            stage_end(pool, 4)

            pool.wait_ge(s_zeroed, 16 * (ROWS * C // (128 * 1024)))
            for b in range(B):
                pool.wait_ge(S("slots"), at(b))
                pool.wait_ge(S("xn5_kept"), at(b))
                for t in range(b * NT, (b + 1) * NT):
                    for k in range(TOP0):
                        pool.indirect_dma_start(out=disp[:, :], in_=xn5[:, t, :], in_offset=None,
                                                out_offset=bass.IndirectOffsetOnAxis(ap=slot_to[:, k, t:t + 1], axis=0),
                                                bounds_check=ROWS - 1, oob_is_err=False).then_inc(s_scattered, 16)
            stage_end(pool, 5)
            stage_end(pool, 6)

            pool.wait_ge(s_eo, 16 * E0)
            for b in range(B):
                if b >= 2:
                    pool.wait_ge(s_gathered[b % 2], 16 * TOP0 * NT * (b // 2))
                for t in range(NT):
                    for k in range(TOP0):
                        g = b * NT + t
                        pool.indirect_dma_start(out=fetched[k][:, g, :], out_offset=None, in_=eo_rows[:, :],
                                                in_offset=bass.IndirectOffsetOnAxis(ap=slot[:, k, g:g + 1], axis=0),
                                                bounds_check=ROWS - 1,
                                                oob_is_err=False).then_inc(s_gathered[b % 2], 16)
            stage_end(pool, 7)
            stage_end(pool, 8)
            additions(LAYER1, v1, DK // 2)
            stage_end(pool, 9)

            pool.wait_ge(s_wm1, 32)
            for w in (e1w1, e1w2):
                pool.tensor_scalar(w[:, :], w[:, :], SCALE, 1.0, MUL, MUL)
            stage_end(pool, 10)

            for b in range(B):
                xs, zs = resid[:, bts(b, NT), :], z[:, bts(b, NT), :]
                st.done(pool.tensor_tensor(xs, xs, zs, ADD))
                pool.tensor_tensor(xs, xs, bcast[:, 24:152].unsqueeze(1).to_broadcast([128, NT, C]),
                                   ADD).then_inc(S("x_b2"), 1)
                pool.wait_ge(S("w_high"), at(b))
                for w, hl in ((e1w1, w1_hl), (e1w2, w2_hl)):
                    pool.tensor_tensor(hl[:, 1, bts(b, WC)], w[:, bts(b, WC)], hl[:, 0, bts(b, WC)], SUB)
            stage_end(pool, 11)

            for n in range(B * E1):
                pool.wait_ge(S("m1_high"), at(n))
                pool.wait_ge(S("m1_out_mm"), at(n, 4))
                pool.tensor_tensor(h_low[n % 4], h_full[n % 2], h_high[n % 4], SUB).then_inc(S("m1_low"), 1)
            pool.drain().then_inc(stage_done, 1)

        @block.scalar
        def _(act):
            A_ = nc.scalar.activation

            def norm_std(n):
                act.wait_ge(s_var, n + 1)
                A_(rstd[:, :], var[:, :], ACT.Sqrt, bias=epsc[:, 0:1]).then_inc(s_std, 1)

            start_signals(act, "act")
            act.wait_ge(s_const, 1)
            norm_std(0)
            stage_end(act, 0)

            def xT_copy(b, u):
                act.wait_ge(S("tr1"), at(b))
                act.wait_ge(S("proj_v"), at(b, 2))
                A_(xT[u], bank(u), ACT.Copy).then_inc(S("xT1"), 1)

            def stage1(b, u, first, last, i):
                c = bts(b, T)
                if not last:
                    xT_copy(b + 1, 1 - u)
                act.wait_ge(S("proj_q"), at(b))
                A_(q0[:, c], bank(2), ACT.Copy).then_inc(S("q_copied"), 1)
                act.wait_ge(S("proj_k"), at(b))
                A_(k0[:, c], bank(3), ACT.Copy).then_inc(S("k_copied"), 1)
                act.wait_ge(S("proj_b"), at(b))
                A_(bk0[:, c], bank(6), ACT.Sigmoid).then_inc(S("beta"), 1)
                act.wait_ge(S("proj_g"), at(b))
                act.wait_ge(S("sg_1"), at(b, 2))
                A_(sgm[u], bank(5), ACT.Sigmoid).then_inc(S("sgm1"), 1)

            xT_copy(0, 0)
            skewed(act, stage1)
            stage_end(act, 1)

            for b in range(B):
                act.wait_ge(S("ss_k"), at(b, 2))
                A_(sq[b % 2], q0[:, bts(b, T)], ACT.Square)
                A_(sqk[b % 2], k0[:, bts(b, T)], ACT.Square).then_inc(S("sq_k"), 1)
            act.wait_ge(s_colsT, 1)
            A_(cols[:, :], bank(6)[:, 0:76], ACT.Copy)
            A_(bcast[:, :], bank(7)[:, 0:152], ACT.Copy)
            act.wait_ge(S("ss_k"), at(B - 1))
            A_(nrm[:, 0:512], bank(0), ACT.Sqrt).then_inc(s_nrm, 1)
            A_(nrm[:, 512:1024], bank(1), ACT.Sqrt).then_inc(s_nrm, 1)
            for b in range(B):
                c = bts(b, T)
                act.wait_ge(S("q_norm"), at(b))
                A_(q_hl[:, 0, c], q0[:, c], ACT.Copy).then_inc(S("q_high"), 1)
                act.wait_ge(S("bk_ready"), at(b))
                A_(bk_hl[:, 0, c], bk0[:, c], ACT.Copy).then_inc(S("bk_high"), 1)
            stage_end(act, 2)

            def outputs(layer, dst, b, u, pairs):
                act.wait_ge(S("r_acc"), at(b * pairs + (layer[0] + pairs - 1)))
                A_(dst[:, bts(b, T)], bank(6 + u), ACT.Copy).then_inc(S("r_o"), 1)

            def decays(b, u, first):
                for p in range(D // 2):
                    n = b * (D // 2) + p
                    act.wait_ge(S("r0_bk"), at(n))
                    act.wait_ge(S("r_c"), at(n, 2))
                    act.wait_ge(S("r0_kk"), at(n, 2))
                    A_(cs[p % 2], bank(2 * (p % 2), 2), ACT.Copy).then_inc(S("r_coef"), 1)
                    act.wait_ge(S("r0_kk"), at(n))
                    act.wait_ge(S("r_scanned"), at(n, 2))
                    A_(decay[p % 2], kk[p % 2], ACT.Identity, scale=-1.0, bias=1.0).then_inc(S("r0_decay"), 1)
                    if p == 2 and not first:
                        outputs(LAYER0, o0, b - 1, 1 - u, D // 2)

            decays(0, 0, True)
            decays(1, 1, False)
            with act.Fori(1, B // 2) as i:
                for u in range(2):
                    decays(2 * i + u, u, False)
            outputs(LAYER0, o0, B - 1, 1, D // 2)
            stage_end(act, 3)

            for b in range(B):
                act.wait_ge(S("centred"), at(b))
                act.wait_ge(S("o_var"), at(b, 2))
                A_(o0[:, bts(b, T)], bank(b % 2), ACT.Copy)
                A_(sq[b % 2], bank(b % 2), ACT.Square).then_inc(S("o_sq"), 1)
            act.wait_ge(S("o_var"), at(B - 1))
            A_(nrm[0:B, 0:512], bank(2)[0:B, :], ACT.Sqrt, bias=epsc[0:B, 0:1]).then_inc(s_nrm, 1)
            norm_std(1)
            stage_end(act, 4)

            def xT5_copy(b, u):
                act.wait_ge(S("tr5"), at(b))
                A_(xT[u], bank(u), ACT.Copy).then_inc(S("xT5"), 1)
                act.wait_ge(S("xn5"), at(b))
                wait_apart(act)
                A_(xn5[:, bts(b, NT), :], xn[u], ACT.Copy).then_inc(S("xn5_kept"), 1)

            def router_hidden(b, u):
                act.wait_ge(S("lgT5_mm"), at(b, 2))
                for h in range(HC0):
                    act.wait_ge(S("hid5_mm"), at(b * HC0 + h))
                    A_(hid[u][:, h, :], bank(2 + h), ACT.Relu,
                       bias=cols[:, RB1 + h:RB1 + h + 1]).then_inc(S("hid5"), 1)

            def stage5(b, u, first, last, i):
                if there(b, 1):
                    router_hidden(b + 1, 1 - u)
                act.wait_ge(S("lgT5_mm"), at(b))
                act.wait_ge(S("lg5_mm"), at(b, 1))
                A_(lg5_T, bank(6)[0:E0, :], ACT.Copy).then_inc(S("lg5_T"), 1)
                if there(b, 2):
                    xT5_copy(b + 2, u)

            xT5_copy(0, 0)
            router_hidden(0, 0)
            xT5_copy(1, 1)
            skewed(act, stage5)
            stage_end(act, 5)

            act.wait_ge(s_diff, 1)
            A_(tmpb[:, :], tmpa[:, :], ACT.Exp).then_inc(s_exp, 1)

            def xdT_copy(e):
                act.wait_ge(S("trd"), at(e))
                A_(xdT[e % 2], bank(e % 2), ACT.Copy).then_inc(S("xdT"), 1)

            def hidden0(e):
                act.wait_ge(S("m0_out_mm"), at(e, 2))
                for h in range(HC0):
                    n = e * HC0 + h
                    act.wait_ge(S("m0_hid_mm"), at(n))
                    A_(hid[e % 2][:, h, :], bank(2 + h), ACT.Relu,
                       bias=cols[:, EB1 + n:EB1 + n + 1]).then_inc(S("m0_hid"), 1)

            xdT_copy(0)
            xdT_copy(1)
            for e in range(E0):
                hidden0(e)
                if e < E0 - 2:
                    xdT_copy(e + 2)
            stage_end(act, 6)

            def deviations(b, k):
                act.wait_ge(S("x_var"), at(2 * b + k))
                wait_apart(act)
                A_(rstd[:, bts(b, NT)], var[:, bts(b, NT)], ACT.Sqrt, bias=epsc[:, 0:1]).then_inc(S("x_std"), 1)

            def make_h(b, u):
                act.wait_ge(S("tr7"), at(b, 2))
                act.wait_ge(S("h_scalars"), at(b))
                wait_apart(act)
                for t in range(NT):
                    g = b * NT + t
                    last = A_(xn[u][:, t, :], z[:, g, :], ACT.Identity, scale=rstd[:, bass.ds(g, 1)],
                              bias=mean[:, bass.ds(g, 1)])
                last.then_inc(S("xn7"), 1)

            def hT_copy(b, u):
                act.wait_ge(S("tr7"), at(b))
                A_(xT[u], bank(u), ACT.Identity, scale=cols[:, LNW1:LNW1 + 1],
                   bias=cols[:, LNB1:LNB1 + 1]).then_inc(S("hT7"), 1)

            def stage7(b, u, first, last, i):
                half = slice(64 * u, 64 * u + 64)
                if there(b, 1):
                    deviations(b + 1, 1)
                if there(b, 2):
                    deviations(b + 2, 0)
                if there(b, 1):
                    make_h(b + 1, 1 - u)
                act.wait_ge(S("g1_mm"), at(b))
                act.wait_ge(S("gk_mm"), at(b, 1))
                A_(g1s, bank(4)[0:16, :], ACT.Copy).then_inc(S("g1"), 1)
                act.wait_ge(S("kq_mm"), at(b))
                A_(kq_hl[:, 0, bts(b, T)], bank(6 + u), ACT.Copy).then_inc(S("kq_high"), 1)
                act.wait_ge(S("v_mm7"), at(b))
                A_(v1[:, bts(b, T)], bank(2), ACT.Copy).then_inc(S("v_copied7"), 1)
                act.wait_ge(S("g_mm7"), at(b))
                A_(sg1[:, bts(b, T)], bank(3), ACT.Silu).then_inc(S("sg_7"), 1)
                act.wait_ge(S("gk_mm"), at(b))
                A_(gate[half, bts(i, T)], bank(5)[half, :], ACT.Identity,
                   bias=cols[half, GKB:GKB + 1]).then_inc(S("gk_copied"), 1)
                if there(b, 1):
                    hT_copy(b + 1, 1 - u)

            deviations(0, 0)
            deviations(0, 1)
            deviations(1, 0)
            make_h(0, 0)
            hT_copy(0, 0)
            skewed(act, stage7)
            stage_end(act, 7)

            st = Steps(act, s_act)
            st.done(A_(ga, gate, ACT.Abs))
            st.done(A_(gb, ga, ACT.Exp, scale=-1.0))
            A_(ga, gb, ACT.Ln, bias=1.0).then_inc(s_ln_high, 1)
            act.wait_ge(s_log, 1)
            st.done(A_(gate, gb, ACT.Exp, scale=1.0 / GATE_NORM))
            A_(gate_hl[:, 0, :], gate, ACT.Copy).then_inc(s_ln_high, 1)
            stage_end(act, 8)

            def keys(b, u, first):
                for p in range(DK // 2):
                    n = b * (DK // 2) + (LAYER1[0] + p)
                    act.wait_ge(S("r1_k"), at(b * (DK // 2) + p))
                    act.wait_ge(S("r_c"), at(n, 2))
                    A_(cs[p % 2], bank(0, 2), ACT.Copy).then_inc(S("r_coef"), 1)
                    if p == 0 and not first:
                        outputs(LAYER1, o1, b - 2, u, DK // 2)

            keys(0, 0, True)
            keys(1, 1, True)
            with act.Fori(1, B // 2) as i:
                for u in range(2):
                    keys(2 * i + u, u, False)
            outputs(LAYER1, o1, B - 2, 0, DK // 2)
            outputs(LAYER1, o1, B - 1, 1, DK // 2)
            stage_end(act, 9)

            for b in range(B):
                act.wait_ge(S("rms_mm"), at(b, 2))
                A_(sq[b % 2], o1[:, bts(b, T)], ACT.Square).then_inc(S("o1_sq"), 1)
            act.wait_ge(S("rms_mm"), at(B - 1))
            A_(nrm[:, 0:512], bank(0), ACT.Sqrt, scale=1.0 / D, bias=epsc[:, 0:1]).then_inc(s_nrm, 1)
            norm_std(2)
            stage_end(act, 10)

            def hT2_copy(b, u):
                act.wait_ge(S("tr11"), at(b))
                act.wait_ge(S("hid11_mm"), at(2 * b + 1, 4))
                A_(hT2[u], bank(u), ACT.Identity, scale=cols[:, LNW1:LNW1 + 1],
                   bias=cols[:, LNB1:LNB1 + 1]).then_inc(S("hT11"), 1)

            def stage11(b, u, first, last, i):
                act.wait_ge(S("mlp_mm"), at(b, 2))
                for h in range(2):
                    act.wait_ge(S("hid11_mm"), at(2 * b + h))
                    A_(hid[u][:, h, :], bank(2 + h), ACT.Gelu,
                       bias=cols[:, AB1 + h:AB1 + h + 1]).then_inc(S("hid11"), 1)
                if not last:
                    hT2_copy(b + 1, 1 - u)
                for w, hl in ((e1w1, w1_hl), (e1w2, w2_hl)):
                    last_copy = A_(hl[:, 0, bts(b, WC)], w[:, bts(b, WC)], ACT.Copy)
                last_copy.then_inc(S("w_high"), 1)

            hT2_copy(0, 0)
            skewed(act, stage11)
            norm_std(3)
            stage_end(act, 11)

            def xs_copy(b, u):
                act.wait_ge(S("tr12"), at(b))
                act.wait_ge(S("lg12_mm"), at(b, 2))
                act.wait_ge(S("x_low"), at(b, 2))
                A_(xT[u], bank(u), ACT.Copy).then_inc(S("xs12"), 1)
                act.wait_ge(S("xs12"), at(b))
                A_(x_hl[:, 0, bts(b, T)], xT[u], ACT.Copy).then_inc(S("x_high"), 1)

            def stage12(b, u, first, last, i):
                if not last:
                    xs_copy(b + 1, 1 - u)

            xs_copy(0, 0)
            skewed(act, stage12)
            act.wait_ge(s_diff, 2)
            A_(coef1[:, :, :], logits, ACT.Exp).then_inc(s_exp, 1)

            act.wait_ge(S("x_low"), at(B - 1))
            def coefficients_staged(b):
                act.wait_ge(s_routed, 1)
                act.wait_ge(S("m1_cT_mm"), at(b, 1))
                A_(cstage, coef1[:, bts(b, NT), :], ACT.Copy).then_inc(S("m1_cs"), 1)

            def coefficients_transposed(b):
                act.wait_ge(S("m1_cT_mm"), at(b))
                act.wait_ge(S("m1_bias_mm"), at(b, 1))
                A_(cT, bank(6)[0:E1, :], ACT.Copy).then_inc(S("m1_cT"), 1)

            with act.Fori(0, B) as b:
                for e in range(E1):
                    n = b * E1 + e
                    act.wait_ge(S("m1_low"), at(n, 2))
                    for h in range(HC1):
                        act.wait_ge(S("m1_hid_mm"), at(n * HC1 + h))
                        A_(h_full[e % 2][:, h * T:(h + 1) * T], bank((e * HC1 + h) % 4), ACT.Gelu, scale=1.0 / SCALE,
                           bias=cols[:, MB1 + e * HC1 + h:MB1 + e * HC1 + h + 1]).then_inc(S("m1_hid"), 1)
                    act.wait_ge(S("m1_hid"), at(n * HC1 + HC1 - 1))
                    act.wait_ge(S("m1_out_mm"), at(n, 4))
                    A_(h_high[e % 4], h_full[e % 2], ACT.Copy).then_inc(S("m1_high"), 1)
                    if e == 1:
                        coefficients_staged(b)
                    if e == 4:
                        coefficients_transposed(b)
            act.drain().then_inc(stage_done, 1)

        @block.vector
        def _(dve):
            V = nc.vector
            TT, TS, STT = V.tensor_tensor, V.tensor_scalar, V.scalar_tensor_tensor

            def tile_stats(src, b):
                for t in range(NT):
                    last = V.bn_stats(stats[:, b * NT + t, :], src[:, b * NT + t, :])
                return last

            def norm_scalars(st, n):
                me, mo, ve, vo = (stats[:, :, k] for k in (1, 4, 2, 5))
                TT(tmpb[:, :], me, mo, SUB)
                TT(var[:, :], ve, vo, ADD)
                st.done(TT(tmpa[:, :], me, mo, ADD))
                TS(mean[:, :], tmpa[:, :], 0.5, None, MUL)
                st.done(STT(out=tmpb[:, :], in0=tmpb[:, :], scalar=0.25, in1=tmpb[:, :], op0=MUL, op1=MUL))
                STT(out=var[:, :], in0=var[:, :], scalar=1.0 / C, in1=tmpb[:, :], op0=MUL, op1=ADD).then_inc(s_var, 1)
                dve.wait_ge(s_std, n + 1)
                st.done(V.reciprocal(rstd[:, :], rstd[:, :]))

            def normalise(dst, src, b):
                for t in range(NT):
                    g = b * NT + t
                    last = TS(dst(t), src[:, g, :], mean[:, bass.ds(g, 1)], rstd[:, bass.ds(g, 1)], SUB, MUL)
                return last

            start_signals(dve, "dve")
            st = Steps(dve, s_dve)
            for half in range(2):
                dve.wait_ge(s_x[half], 16 * (B // 2))
                with dve.Fori(half * (B // 4), (half + 1) * (B // 4)) as i:
                    for u in range(2):
                        tile_stats(resid, 2 * i + u).then_inc(S("stats"), 1)
            dve.wait_ge(S("stats"), at(B - 1))
            dve.wait_ge(s_const, 1)
            norm_scalars(st, 0)
            dve.wait_ge(s_w0, 16 * W0_LOADS)
            V.tensor_copy(w_brep[:, :].rearrange("p (h i) -> p h i", i=D),
                          w_b[:, :].unsqueeze(2).to_broadcast([128, H, D]))
            stage_end(dve, 0)

            def xn_ahead(b, u, src, transposed, ready):
                dve.wait_ge(S(transposed), at(b, 2))
                normalise(lambda t: xn[u][:, t, :], src, b).then_inc(S(ready), 1)

            def stage1(b, u, first, last, i):
                c = bts(b, T)
                if there(b, 2):
                    xn_ahead(b + 2, u, resid, "tr1", "xn1")
                dve.wait_ge(S("sgm1"), at(b))
                TT(sg0[:, c], bank(5), sgm[u], MUL).then_inc(S("sg_1"), 1)
                dve.wait_ge(S("proj_v"), at(b))
                V.tensor_copy(v0[:, c], bank(4)).then_inc(S("v_copied"), 1)

            xn_ahead(0, 0, resid, "tr1", "xn1")
            xn_ahead(1, 1, resid, "tr1", "xn1")
            skewed(dve, stage1)
            stage_end(dve, 1)

            def q_low(b):
                c = bts(b, T)
                dve.wait_ge(S("q_high"), at(b))
                TT(q_hl[:, 1, c], q0[:, c], q_hl[:, 0, c], SUB)

            dve.wait_ge(s_w, 16 * W_LOADS)
            TS(u_kq[:, 1, :], u_kq[:, 1, :], float(DK) ** -0.5, None, MUL)
            for s in range(2):
                dve.wait_ge(s_nrm, s + 1)
                half = slice(512 * s, 512 * s + 512)
                st.done(TS(nrm[:, half], nrm[:, half], 1e-12, None, MAX))
                V.reciprocal(rn[:, half], nrm[:, half]).then_inc(s_rn, 1)
            for b in range(B):
                c = bts(b, T)
                dve.wait_ge(S("rk_mm"), at(b))
                TT(k0[:, c], k0[:, c], bank(4 + b % 2), MUL).then_inc(S("bk_in"), 1)
                dve.wait_ge(S("rq_mm"), at(b))
                TT(q0[:, c], q0[:, c], bank(2 + b % 2), MUL).then_inc(S("q_norm"), 1)
                if b:
                    q_low(b - 1)
            q_low(B - 1)
            stage_end(dve, 2)

            def beta_kk(b, p):
                n = b * (D // 2) + p
                dve.wait_ge(S("r_coef"), at(n))
                dve.wait_ge(S("r0_decay"), at(n, 2))
                TT(kk[p % 2], cs[p % 2], k0[:, bts(b, T)].unsqueeze(1).to_broadcast([128, 2, T]),
                   MUL).then_inc(S("r0_kk"), 1)

            def scan(layer, n, p, decays):
                dve.wait_ge(S("r_c"), at(n))
                dve.wait_ge(S("r_prod"), at(n, 1))
                for j in range(2):
                    last = V.tensor_tensor_scan(out=state[:, j, :], data0=decays[:, j, :], data1=cbuf[p % 2][:, j, :],
                                                initial=0.0, op0=MUL, op1=ADD)
                last.then_inc(S("r_scanned"), 1)

            def read_out(layer, n, p):
                dve.wait_ge(S("r_scanned"), at(n))
                dve.wait_ge(S("r_q"), at(n))
                dve.wait_ge(S("r_acc"), at(n, 2))
                TT(prod[p % 2], bank(4, 2), state, MUL).then_inc(S("r_prod"), 1)

            def recur0(b, last):
                for p in range(D // 2):
                    n = b * (D // 2) + p
                    if p < D // 2 - 1:
                        beta_kk(b, p + 1)
                    elif not last:
                        beta_kk(b + 1, 0)
                    dve.wait_ge(S("r0_decay"), at(n))
                    scan(LAYER0, n, p, decay[p % 2])
                    read_out(LAYER0, n, p)

            dve.wait_ge(s_zeroed, 16 * (ROWS * C // (128 * 1024)))
            beta_kk(0, 0)
            with dve.Fori(0, B - 1) as b:
                recur0(b, False)
            recur0(B - 1, True)
            stage_end(dve, 3)

            dve.wait_ge(s_nrm, 3)
            V.reciprocal(rn[0:B, 0:512], nrm[0:B, 0:512]).then_inc(s_rn, 1)

            def add_projection(b, dst, proj, added):
                u = b % 2
                dve.wait_ge(S(proj), at(b))
                xs = dst[:, b * NT:(b + 1) * NT, :]
                TT(xs, xs, bank(5 + u).rearrange("p (n c) -> p n c", c=C), ADD).then_inc(S(added), 1)
                dve.wait_ge(S(added), at(b))
                tile_stats(dst, b).then_inc(S("stats"), 1)

            for b in range(B):
                u = b % 2
                dve.wait_ge(S("o_spread"), at(b))
                dve.wait_ge(S("yg_ready"), at(b, 2))
                TT(y[u], o0[:, bts(b, T)], bank(3 + u), MUL).then_inc(S("y_raw"), 1)
                dve.wait_ge(S("y_raw"), at(b))
                TS(y[u], y[u], cols[:, LNG:LNG + 1], cols[:, LNB:LNB + 1], MUL, ADD).then_inc(S("y_ready"), 1)
                if b >= 1:
                    add_projection(b - 1, resid, "proj_o", "x_added")
            add_projection(B - 1, resid, "proj_o", "x_added")
            dve.wait_ge(S("stats"), at(2 * B - 1))
            norm_scalars(st, 1)
            stage_end(dve, 4)

            ROUTE, PLACE = 5, 5
            links = LoopSteps(dve, s_links, 0, ROUTE + PLACE)

            def route(b, u):
                links.round(b)
                dve.wait_ge(S("lg5_mm"), at(b))
                TT(lg5[u], bank(6)[:, 0:NT * E0].rearrange("p (n e) -> p n e", e=E0),
                   bcast[:, 0:E0].unsqueeze(1).to_broadcast([128, NT, E0]), ADD).then_inc(S("lg5_added"), 1)
                dve.wait_ge(S("lg5_added"), at(b))
                wait_apart(dve)
                for t in range(NT):
                    last = V.max(top5[u][:, t, :], lg5[u][:, t, :])
                links.done(last)
                links.done(V.tensor_copy(top0[:, :, bts(b, NT)], top5[u][:, :, 0:TOP0].rearrange("p n k -> p k n")))
                wait_apart(dve)
                for t in range(NT):
                    last = V.max_index(idx5[u][:, t, :], top5[u][:, t, :], lg5[u][:, t, :])
                links.done(last)
                links.done(V.tensor_copy(id5[u], idx5[u][:, :, 0:TOP0].rearrange("p n k -> p k n")))
                links.done(TT(oh5[u], iota[:, 0:E0].unsqueeze(1).unsqueeze(1).to_broadcast([128, TOP0, NT, E0]),
                              id5[u].unsqueeze(3).to_broadcast([128, TOP0, NT, E0]), ALU.is_equal))
                TT(by_expert(picked[u][:, 0:NT * E0]), oh5[u][:, 0], oh5[u][:, 1], ADD).then_inc(S("picked"), 1)

            def place_picks(b, u):
                links.round(b, ROUTE)
                dve.wait_ge(S("counts"), at(b))
                links.done(TT(place, by_expert(bank(7)[:, 0:NT * E0]),
                              carry.unsqueeze(1).to_broadcast([128, NT, E0]), ADD))
                TT(carry, carry, bank(7)[:, NT * E0:NT * E0 + E0], ADD).then_inc(S("placed"), 1)
                links.done(TT(placed, oh5[u], place.unsqueeze(1).to_broadcast([128, TOP0, NT, E0]), MUL))
                links.done(V.tensor_reduce(out=pos, in_=placed, axis=AX, op=ADD))
                TS(keep[:, :, bts(b, NT)], pos, float(CAP), None, ALU.is_lt)
                TS(over_cap, pos, float(CAP), float(ROWS), ALU.is_ge, MUL)
                links.done(TS(clipped, pos, float(CAP - 1), None, ALU.min))
                links.done(STT(out=row, in0=id5[u], scalar=float(CAP), in1=clipped, op0=MUL, op1=ADD))
                V.tensor_copy(slot[:, :, bts(b, NT)], row)
                TT(slot_to[:, :, bts(b, NT)], row, over_cap, ADD).then_inc(S("slots"), 1)

            def xn5_ahead(b, u):
                dve.wait_ge(S("xn5_kept"), at(b, 2))
                xn_ahead(b, u, resid, "tr5", "xn5")

            def stage5(b, u, first, last, i):
                if not first:
                    place_picks(b - 1, 1 - u)
                if there(b, 2):
                    xn5_ahead(b + 2, u)
                route(b, u)

            V.memset(carry, 0.0)
            xn5_ahead(0, 0)
            xn5_ahead(1, 1)
            skewed(dve, stage5)
            place_picks(B - 1, 1)
            stage_end(dve, 5)

            TT(tmpa[:, :], top0[:, 1, :], top0[:, 0, :], SUB).then_inc(s_diff, 1)
            dve.wait_ge(s_eb2_mm, 1)
            V.tensor_copy(eb2_rep, bank(6, 2).rearrange("p k (e c) -> p (k e) c", c=C)).then_inc(s_eb2, 1)
            dve.wait_ge(s_exp, 1)
            st.done(TS(tmpa[:, :], tmpb[:, :], 1.0, None, ADD))
            st.done(V.reciprocal(tmpa[:, :], tmpa[:, :]))
            st.done(TT(tmpb[:, :], tmpb[:, :], tmpa[:, :], MUL))
            TT(coef0[:, 0, :], keep[:, 0, :], tmpa[:, :], MUL)
            TT(coef0[:, 1, :], keep[:, 1, :], tmpb[:, :], MUL)
            dve.wait_ge(s_eb2, 1)
            for e in range(E0):
                dve.wait_ge(S("m0_out_mm"), at(e))
                TT(eo[:, bts(e, NT), :], bank(6 + e % 2).rearrange("p (n c) -> p n c", c=C),
                   eb2_rep[:, e, :].unsqueeze(1).to_broadcast([128, NT, C]), ADD).then_inc(S("eo"), 1)
            stage_end(dve, 6)

            COMBINE, MAKE_Z, H_SCALARS = 4, 5, 1
            links7 = LoopSteps(dve, s_links, B * (ROUTE + PLACE) + COMBINE, COMBINE + MAKE_Z + H_SCALARS)

            def variances(src, b):
                ts = bts(b, NT)
                wait_apart(dve)
                links7.done(tile_stats(src, b))
                TT(tmpb[:, ts], stats[:, ts, 1], stats[:, ts, 4], SUB)
                TT(var[:, ts], stats[:, ts, 2], stats[:, ts, 5], ADD)
                links7.done(TT(tmpa[:, ts], stats[:, ts, 1], stats[:, ts, 4], ADD))
                TS(mean[:, ts], tmpa[:, ts], 0.5, None, MUL)
                links7.done(STT(out=tmpb[:, ts], in0=tmpb[:, ts], scalar=0.25, in1=tmpb[:, ts], op0=MUL, op1=MUL))
                STT(out=var[:, ts], in0=var[:, ts], scalar=1.0 / C, in1=tmpb[:, ts], op0=MUL,
                    op1=ADD).then_inc(S("x_var"), 1)

            def invert(b, k):
                dve.wait_ge(S("x_std"), at(2 * b + k))
                wait_apart(dve)
                links7.done(V.reciprocal(rstd[:, bts(b, NT)], rstd[:, bts(b, NT)]))

            def combine(b, u, i):
                links7.round(b, -COMBINE)
                if not isinstance(b, int) or b:
                    links7.round(b - 1, MAKE_Z)
                dve.wait_ge(s_gathered[u], 16 * TOP0 * NT * (i + 1))
                for k in range(TOP0):
                    for t in range(NT):
                        g = b * NT + t
                        last = STT(out=resid[:, g, :], in0=fetched[k][:, g, :], scalar=coef0[:, k, bass.ds(g, 1)],
                                   in1=resid[:, g, :], op0=MUL, op1=ADD)
                    if k < TOP0 - 1:
                        links7.done(last)
                last.then_inc(S("moe_added"), 1)
                dve.wait_ge(S("moe_added"), at(b))
                variances(resid, b)

            def make_z(b):
                links7.round(b)
                invert(b, 0)
                links7.done(normalise(lambda t: z[:, b * NT + t, :], resid, b))
                variances(z, b)

            def h_scalars(b):
                links7.round(b, MAKE_Z + (COMBINE if there(b, 1) else 0))
                invert(b, 1)
                ts = bts(b, NT)
                STT(out=mean[:, ts], in0=mean[:, ts], scalar=-1.0, in1=rstd[:, ts], op0=MUL,
                    op1=MUL).then_inc(S("h_scalars"), 1)

            def kq_low(b, u):
                dve.wait_ge(S("kq_high"), at(b))
                c = bts(b, T)
                TT(kq_hl[:, 1, c], bank(6 + u), kq_hl[:, 0, c], SUB).then_inc(S("kq_low"), 1)

            def stage7(b, u, first, last, i):
                if there(b, 1):
                    make_z(b + 1)
                if not first:
                    kq_low(b - 1, 1 - u)
                if there(b, 2):
                    combine(b + 2, u, i + 1)
                if there(b, 1):
                    h_scalars(b + 1)

            combine(0, 0, 0)
            make_z(0)
            combine(1, 1, 0)
            h_scalars(0)
            skewed(dve, stage7)
            kq_low(B - 1, 1)
            stage_end(dve, 7)

            st.done(TS(gm, gate, 0.0, None, ALU.min))
            dve.wait_ge(s_ln_high, 1)
            TT(gb, gm, ga, SUB).then_inc(s_log, 1)
            dve.wait_ge(s_ln_high, 2)
            TT(gate_hl[:, 1, :], gate, gate_hl[:, 0, :], SUB)
            stage_end(dve, 8)

            with dve.Fori(0, B) as b:
                for p in range(DK // 2):
                    n = b * (DK // 2) + (LAYER1[0] + p)
                    dve.wait_ge(S("r1_e"), at(b * (DK // 2) + p))
                    scan(LAYER1, n, p, bank(2, 2))
                    read_out(LAYER1, n, p)
            stage_end(dve, 9)

            dve.wait_ge(s_nrm, 4)
            V.reciprocal(rn[:, 0:512], nrm[:, 0:512]).then_inc(s_rn, 1)
            for b in range(B):
                u = b % 2
                dve.wait_ge(S("rms_spread"), at(b))
                TT(y[u], o1[:, bts(b, T)], bank(3 + u), MUL).then_inc(S("y1_raw"), 1)
                dve.wait_ge(S("y1_raw"), at(b))
                dve.wait_ge(S("proj_o1"), at(b, 2))
                STT(out=yg[u], in0=y[u], scalar=cols[:, RMSW:RMSW + 1], in1=sg1[:, bts(b, T)],
                    op0=MUL, op1=MUL).then_inc(S("yg1_ready"), 1)
                if b >= 1:
                    add_projection(b - 1, z, "proj_o1", "z_added")
            add_projection(B - 1, z, "proj_o1", "z_added")
            dve.wait_ge(S("stats"), at(3 * B - 1))
            norm_scalars(st, 2)
            stage_end(dve, 10)

            def mlp_add(b, u):
                xs = resid[:, bts(b, NT), :]
                dve.wait_ge(S("x_b2"), at(b))
                dve.wait_ge(S("mlp_mm"), at(b))
                TT(xs, xs, bank(4 + u).rearrange("p (n c) -> p n c", c=C), ADD).then_inc(S("mlp_added"), 1)
                dve.wait_ge(S("mlp_added"), at(b))
                tile_stats(resid, b).then_inc(S("stats"), 1)

            def stage11(b, u, first, last, i):
                if there(b, 2):
                    xn_ahead(b + 2, u, z, "tr11", "xn11")
                if not first:
                    mlp_add(b - 1, 1 - u)

            xn_ahead(0, 0, z, "tr11", "xn11")
            xn_ahead(1, 1, z, "tr11", "xn11")
            skewed(dve, stage11)
            mlp_add(B - 1, 1)
            dve.wait_ge(S("stats"), at(4 * B - 1))
            norm_scalars(st, 3)
            stage_end(dve, 11)

            def over(v, E):
                return v.unsqueeze(2).to_broadcast([128, TILES, E])

            def one_hot(dst, k, E):
                return TT(dst, iota[:, 0:E].unsqueeze(1).to_broadcast([128, TILES, E]), over(idf[:, :, k], E), ALU.is_equal)

            def stage12(b, u, first, last, i):
                if there(b, 2):
                    xn_ahead(b + 2, u, resid, "tr12", "xn12")
                dve.wait_ge(S("x_high"), at(b))
                TT(x_hl[:, 1, bts(b, T)], xT[u], x_hl[:, 0, bts(b, T)], SUB).then_inc(S("x_low"), 1)
                dve.wait_ge(S("lg12_mm"), at(b))
                TT(logits[:, bts(b, NT), :], bank(6)[:, 0:NT * E1].rearrange("p (n e) -> p n e", e=E1),
                   bcast[:, 8:8 + E1].unsqueeze(1).to_broadcast([128, NT, E1]), ADD).then_inc(S("lg12_added"), 1)

            xn_ahead(0, 0, resid, "tr12", "xn12")
            xn_ahead(1, 1, resid, "tr12", "xn12")
            skewed(dve, stage12)
            dve.wait_ge(S("lg12_added"), at(B - 1))
            st.done(V.tensor_reduce(out=tmpa[:, :], in_=logits, axis=AX, op=MAX))
            TT(logits, logits, over(tmpa[:, :], E1), SUB).then_inc(s_diff, 1)
            dve.wait_ge(s_exp, 2)
            st.done(V.tensor_reduce(out=tmpa[:, :], in_=coef1[:, :, :], axis=AX, op=ADD))
            st.done(V.reciprocal(tmpa[:, :], tmpa[:, :]))
            st.done(TT(logits, coef1[:, :, :], over(tmpa[:, :], E1), MUL))
            for g in range(TILES):
                last = V.max(top[:, g, :], logits[:, g, :])
            st.done(last)
            V.tensor_reduce(out=tmpb[:, :], in_=top[:, :, 0:TOP1], axis=AX, op=ADD)
            for g in range(TILES):
                last = V.max_index(idx[:, g, :], top[:, g, :], logits[:, g, :])
            st.done(last)
            V.tensor_copy(idf, idx[:, :, 0:4])
            st.done(V.reciprocal(tmpb[:, :], tmpb[:, :]))
            TS(tmpb[:, :], tmpb[:, :], 1.0 / SCALE, None, MUL)
            TS(mb2[:, :], mb2[:, :], SCALE, None, MUL)
            st.done(one_hot(oh, 0, E1))
            for k in range(1, TOP1):
                st.done(one_hot(ohw, k, E1))
                st.done(TT(oh, oh, ohw, ADD))
            st.done(TT(oh, oh, logits, MUL))
            TT(coef1[:, :, :], oh, over(tmpb[:, :], E1), MUL).then_inc(s_routed, 1)
            dve.wait_ge(s_routed, 1)

            with dve.Fori(0, B) as b:
                for e in range(E1):
                    n = b * E1 + e
                    dve.wait_ge(S("m1_out_mm"), at(n))
                    dve.wait_ge(S("m1_acc"), at(n, 1))
                    for t in range(NT):
                        g = b * NT + t
                        last = STT(out=resid[:, g, :], in0=bank(4 + e % 2)[:, t * C:(t + 1) * C],
                                   scalar=coef1[:, g, e:e + 1], in1=resid[:, g, :], op0=MUL, op1=ADD)
                    last.then_inc(S("m1_acc"), 1)
                    if e == 6:
                        dve.wait_ge(S("m1_acc"), at(n))
                        dve.wait_ge(S("m1_bias_mm"), at(b))
                        xs = resid[:, bts(b, NT), :]
                        TT(xs, xs, bank(7).rearrange("p (n c) -> p n c", c=C), ADD).then_inc(S("m1_bias"), 1)
                        dve.wait_ge(S("m1_bias"), at(b))
            dve.drain().then_inc(stage_done, 1)

        @block.tensor
        def _(pe):
            def mm(o, l, r, start=True, stop=True):
                return nc.tensor.matmul(o, l, r, start=start, stop=stop)

            def tile(v, t):
                return v[:, t * 128:(t + 1) * 128]

            def transposes(dst, src):
                for t in range(NT):
                    last = nc.tensor.transpose(tile(dst, t), src[:, t, :], ident[:, :])
                return last

            def tokens_out(dst, act_T, w):
                for t in range(NT):
                    last = mm(tile(dst, t), tile(act_T, t), w)
                return last

            start_signals(pe, "pe")
            pe.wait_ge(s_const, 1)
            pe.wait_ge(s_w0, 16 * W0_LOADS)
            stage_end(pe, 0)

            def transpose_ahead(b, u, ready, copied, done):
                pe.wait_ge(S(ready), at(b))
                pe.wait_ge(S(copied), at(b, 2))
                transposes(bank(u), xn[u]).then_inc(S(done), 1)

            def stage1(b, u, first, last, i):
                if not last:
                    transpose_ahead(b + 1, 1 - u, "xn1", "xT1", "tr1")
                pe.wait_ge(S("xT1"), at(b))
                for n, w, free, done in ((2, w_q, "q_copied", "proj_q"), (3, w_k, "k_copied", "proj_k"),
                                         (6, w_brep, "beta", "proj_b"), (5, w_g, "sg_1", "proj_g"),
                                         (4, w_v, "v_copied", "proj_v")):
                    pe.wait_ge(S(free), at(b, 1))
                    mm(bank(n), w[:, :], xT[u]).then_inc(S(done), 1)

            transpose_ahead(0, 0, "xn1", "xT1", "tr1")
            skewed(pe, stage1)
            stage_end(pe, 1)

            pe.wait_ge(s_w, 16 * W_LOADS)
            nc.tensor.transpose(bank(6)[:, 0:76], rows[:, :], ident[0:76, 0:76])
            mm(bank(7)[:, 0:152], ones[0:1, :], brow[:, :]).then_inc(s_colsT, 1)
            for b in range(B):
                window = headsum[:, 112 - H * b:240 - H * b]
                pe.wait_ge(S("sq_k"), at(b))
                mm(bank(0), window, sq[b % 2], start=b == 0, stop=b == B - 1)
                mm(bank(1), window, sqk[b % 2], start=b == 0, stop=b == B - 1).then_inc(S("ss_k"), 1)
            pe.wait_ge(s_rn, 2)
            for b in range(B):
                pe.wait_ge(S("bk_in"), at(b, 2))
                mm(bank(4 + b % 2), expand[:, b, :], rn[:, 512:1024]).then_inc(S("rk_mm"), 1)
                pe.wait_ge(S("q_norm"), at(b, 2))
                mm(bank(2 + b % 2), expand[:, b, :], rn[:, 0:512]).then_inc(S("rq_mm"), 1)
            stage_end(pe, 2)

            def picked_pair(dst, weights, src, b):
                for j in range(2):
                    for s in range(2):
                        last = mm(bank(dst + j), weights(j), src[:, s, bts(b, T)], start=s == 0, stop=s == 1)
                return last

            def beta_k(b, p):
                n = b * (D // 2) + p
                pe.wait_ge(S("r_coef"), at(n, 2))
                picked_pair(2 * (p % 2), lambda j: pick[:, 2 * p + j, :], bk_hl, b).then_inc(S("r0_bk"), 1)

            def sum_up(layer, b, p, u, pairs):
                n = b * pairs + (layer[0] + p)
                pe.wait_ge(S("r_pair"), at(n))
                if p == 0:
                    pe.wait_ge(S("r_o"), at(b + layer[1], 2))
                mm(bank(6 + u), ident[:, :], prod[p % 2][:, 0, :], start=p == 0,
                   stop=p == pairs - 1).then_inc(S("r_acc"), 1)

            def recur0(b, u, first=False, last=False):
                P = D // 2
                for p in range(P):
                    n = b * P + p
                    pe.wait_ge(S("r_prod"), at(n, 1))
                    picked_pair(4, lambda j: pick[:, 2 * p + j, :], q_hl, b).then_inc(S("r_q"), 1)
                    if p < P - 2:
                        beta_k(b, p + 2)
                    elif not last:
                        beta_k(b + 1, p + 2 - P)
                    if p:
                        sum_up(LAYER0, b, p - 1, u, P)
                    elif not first:
                        sum_up(LAYER0, b - 1, P - 1, 1 - u, P)

            beta_k(0, 0)
            beta_k(0, 1)
            recur0(0, 0, first=True)
            recur0(1, 1)
            with pe.Fori(1, B // 2 - 1) as i:
                for u in range(2):
                    recur0(2 * i + u, u)
            recur0(B - 2, 0)
            recur0(B - 1, 1, last=True)
            sum_up(LAYER0, B - 1, D // 2 - 1, 1, D // 2)
            stage_end(pe, 3)

            def variance(b):
                pe.wait_ge(S("o_sq"), at(b))
                mm(bank(2)[0:B, :], meanrow[:, 7 - b:15 - b], sq[b % 2],
                   start=b == 0, stop=b == B - 1).then_inc(S("o_var"), 1)

            for b in range(B):
                pe.wait_ge(S("o_sq"), at(b, 2))
                mm(bank(b % 2), center[:, :], o0[:, bts(b, T)]).then_inc(S("centred"), 1)
                if b:
                    variance(b - 1)
            variance(B - 1)
            pe.wait_ge(s_rn, 3)

            def project0(b):
                u = b % 2
                pe.wait_ge(S("yg_ready"), at(b))
                pe.wait_ge(S("x_added"), at(b, 2))
                tokens_out(bank(5 + u), yg[u], w_o[:, :]).then_inc(S("proj_o"), 1)

            for b in range(B):
                pe.wait_ge(S("y_raw"), at(b, 2))
                mm(bank(3 + b % 2), spread[:, b, :], rn[0:B, 0:512]).then_inc(S("o_spread"), 1)
                if b:
                    project0(b - 1)
            project0(B - 1)
            stage_end(pe, 4)

            def count_picks(b, u):
                pe.wait_ge(S("picked"), at(b))
                pe.wait_ge(S("placed"), at(b, 1))
                N = NT * E0
                mm(bank(7)[:, 0:N], tri[:, :], picked[u][:, 0:N], stop=False)
                for t in range(1, NT):
                    mm(bank(7)[:, t * E0:N], ones16[:, :], picked[u][:, 0:N - t * E0], start=False, stop=t == NT - 1)
                for t in range(NT):
                    last = mm(bank(7)[:, N:N + E0], ones16[:, :], picked[u][:, t * E0:(t + 1) * E0],
                              start=t == 0, stop=t == NT - 1)
                last.then_inc(S("counts"), 1)

            def router_hidden(b, u):
                pe.wait_ge(S("xT5"), at(b))
                for h in range(HC0):
                    pe.wait_ge(S("hid5"), at(b * HC0 + h, HC0))
                    mm(bank(2 + h), tile(w_r1, h), xT[u]).then_inc(S("hid5_mm"), 1)

            def stage5(b, u, first, last, i):
                if there(b, 1):
                    router_hidden(b + 1, 1 - u)
                if not first:
                    count_picks(b - 1, 1 - u)
                pe.wait_ge(S("hid5"), at(b * HC0 + HC0 - 1))
                pe.wait_ge(S("lg5_added"), at(b, 1))
                for h in range(HC0):
                    last_mm = mm(bank(6)[0:E0, :], w_r2[:, h, :], hid[u][:, h, :], start=h == 0, stop=h == HC0 - 1)
                last_mm.then_inc(S("lgT5_mm"), 1)
                if there(b, 2):
                    transpose_ahead(b + 2, u, "xn5", "xT5", "tr5")
                pe.wait_ge(S("lg5_T"), at(b))
                wait_apart(pe)
                for t in range(NT):
                    last_mm = nc.tensor.transpose(bank(6)[:, t * E0:(t + 1) * E0], tile(lg5_T, t), ident[0:E0, 0:E0])
                last_mm.then_inc(S("lg5_mm"), 1)

            transpose_ahead(0, 0, "xn5", "xT5", "tr5")
            router_hidden(0, 0)
            transpose_ahead(1, 1, "xn5", "xT5", "tr5")
            skewed(pe, stage5)
            count_picks(B - 1, 1)
            stage_end(pe, 5)

            def transpose_rows(e):
                pe.wait_ge(s_disp[e // 2], 16)
                pe.wait_ge(S("xdT"), at(e, 2))
                transposes(bank(e % 2), xd[:, bts(e, NT), :]).then_inc(S("trd"), 1)

            def hidden0(e):
                pe.wait_ge(S("xdT"), at(e))
                for h in range(HC0):
                    pe.wait_ge(S("m0_hid"), at(e * HC0 + h, HC0))
                    mm(bank(2 + h), e0w1[:, e, h * 128:(h + 1) * 128], xdT[e % 2]).then_inc(S("m0_hid_mm"), 1)

            def outputs0(e):
                pe.wait_ge(S("m0_hid"), at(e * HC0 + HC0 - 1))
                pe.wait_ge(S("eo"), at(e, 2))
                for t in range(NT):
                    for h in range(HC0):
                        last = mm(tile(bank(6 + e % 2), t), tile(hid[e % 2][:, h, :], t), e0w2[:, e, h, :],
                                  start=h == 0, stop=h == HC0 - 1)
                last.then_inc(S("m0_out_mm"), 1)

            for e in range(E0):
                last = mm(tile(bank(6 + e // 4), e % 4), spread[:, e, :], eb2[:, :])
            last.then_inc(s_eb2_mm, 1)
            pe.wait_ge(s_wm0, 32)
            transpose_rows(0)
            transpose_rows(1)
            hidden0(0)
            pe.wait_ge(s_eb2, 1)
            for e in range(E0):
                if e < E0 - 1:
                    hidden0(e + 1)
                if e < E0 - 2:
                    transpose_rows(e + 2)
                outputs0(e)
            stage_end(pe, 6)

            def stage7(b, u, first, last, i):
                h_T = xT[u]
                pe.wait_ge(S("hT7"), at(b))
                pe.wait_ge(S("g1"), at(b, 1))
                mm(bank(4)[0:16, :], u_gk1[:, :], h_T).then_inc(S("g1_mm"), 1)
                pe.wait_ge(S("kq_low"), at(b, 2))
                mm(bank(6 + u), u_kq[:, :, :].rearrange("p s n -> p (s n)"), h_T).then_inc(S("kq_mm"), 1)
                pe.wait_ge(S("v_copied7"), at(b, 1))
                mm(bank(2), u_v[:, :], h_T).then_inc(S("v_mm7"), 1)
                pe.wait_ge(S("sg_7"), at(b, 1))
                mm(bank(3), u_g[:, :], h_T).then_inc(S("g_mm7"), 1)
                pe.wait_ge(S("g1"), at(b))
                pe.wait_ge(S("gk_copied"), at(b, 1))
                mm(bank(5)[64 * u:64 * u + 64, :], u_gk2[:, :], g1s).then_inc(S("gk_mm"), 1)
                if not last:
                    transpose_ahead(b + 1, 1 - u, "xn7", "hT7", "tr7")

            transpose_ahead(0, 0, "xn7", "hT7", "tr7")
            skewed(pe, stage7)
            stage_end(pe, 7)
            stage_end(pe, 8)

            def keys(b, p):
                pe.wait_ge(S("r_coef"), at(b * (DK // 2) + (LAYER1[0] + p), 1))
                picked_pair(0, lambda j: pickg[:, 0, 2 * p + j, :], kq_hl, b).then_inc(S("r1_k"), 1)

            def recur1(b, half, u, first=False, last=False):
                P = DK // 2
                for p in range(P):
                    n = b * P + (LAYER1[0] + p)
                    pe.wait_ge(S("r_scanned"), at(n, 1))
                    picked_pair(2, lambda j: pickg[:, u, 2 * p + j, :], gate_hl, half).then_inc(S("r1_e"), 1)
                    if p < P - 1:
                        keys(b, p + 1)
                    elif not last:
                        keys(b + 1, 0)
                    pe.wait_ge(S("r_prod"), at(n, 1))
                    picked_pair(4, lambda j: pickg[:, 1, 2 * p + j, :], kq_hl, b).then_inc(S("r_q"), 1)
                    if p:
                        sum_up(LAYER1, b, p - 1, u, P)
                    elif not first:
                        sum_up(LAYER1, b - 1, P - 1, 1 - u, P)

            keys(0, 0)
            recur1(0, 0, 0, first=True)
            recur1(1, 0, 1)
            with pe.Fori(1, B // 2 - 1) as i:
                for u in range(2):
                    recur1(2 * i + u, i, u)
            recur1(B - 2, B // 2 - 1, 0)
            recur1(B - 1, B // 2 - 1, 1, last=True)
            sum_up(LAYER1, B - 1, DK // 2 - 1, 1, DK // 2)
            stage_end(pe, 9)

            for b in range(B):
                pe.wait_ge(S("o1_sq"), at(b))
                mm(bank(0), headsum[:, 112 - H * b:240 - H * b], sq[b % 2],
                   start=b == 0, stop=b == B - 1).then_inc(S("rms_mm"), 1)
            pe.wait_ge(s_rn, 4)

            def project1(b):
                u = b % 2
                pe.wait_ge(S("yg1_ready"), at(b))
                pe.wait_ge(S("z_added"), at(b, 2))
                tokens_out(bank(5 + u), yg[u], u_o[:, :]).then_inc(S("proj_o1"), 1)

            for b in range(B):
                pe.wait_ge(S("y1_raw"), at(b, 2))
                mm(bank(3 + b % 2), expand[:, b, :], rn[:, 0:512]).then_inc(S("rms_spread"), 1)
                if b:
                    project1(b - 1)
            project1(B - 1)
            stage_end(pe, 10)

            def mlp_out(b, u):
                pe.wait_ge(S("hid11"), at(2 * b + 1))
                pe.wait_ge(S("mlp_added"), at(b, 2))
                for t in range(NT):
                    for h in range(2):
                        last = mm(tile(bank(4 + u), t), tile(hid[u][:, h, :], t), u_2[:, h, :],
                                  start=h == 0, stop=h == 1)
                last.then_inc(S("mlp_mm"), 1)

            def stage11(b, u, first, last, i):
                pe.wait_ge(S("hT11"), at(b))
                for h in range(2):
                    pe.wait_ge(S("hid11"), at(2 * b + h, 2))
                    mm(bank(2 + h), tile(u_1, h), hT2[u]).then_inc(S("hid11_mm"), 1)
                if not last:
                    transpose_ahead(b + 1, 1 - u, "xn11", "hT11", "tr11")
                if not first:
                    mlp_out(b - 1, 1 - u)

            transpose_ahead(0, 0, "xn11", "hT11", "tr11")
            skewed(pe, stage11)
            mlp_out(B - 1, 1)
            stage_end(pe, 11)

            def stage12(b, u, first, last, i):
                if not last:
                    transpose_ahead(b + 1, 1 - u, "xn12", "xs12", "tr12")
                pe.wait_ge(S("xs12"), at(b))
                pe.wait_ge(S("lg12_added"), at(b, 1))
                for t in range(NT):
                    last_mm = mm(bank(6)[:, t * E1:(t + 1) * E1], tile(xT[u], t), u_r[:, :])
                last_mm.then_inc(S("lg12_mm"), 1)

            transpose_ahead(0, 0, "xn12", "xs12", "tr12")
            skewed(pe, stage12)
            pe.wait_ge(S("x_low"), at(B - 1))

            PARTS = ((0, 0), (0, 1), (1, 0))
            AHEAD = 3

            def hidden1(b, e):
                for h in range(HC1):
                    n = (b * E1 + e) * HC1 + h
                    pe.wait_ge(S("m1_hid"), at(n, 4))
                    w = slice((e * HC1 + h) * 128, (e * HC1 + h) * 128 + 128)
                    for k, (sw, sx) in enumerate(PARTS):
                        last = mm(bank((e * HC1 + h) % 4), w1_hl[:, sw, w], x_hl[:, sx, bts(b, T)],
                                  start=k == 0, stop=k == len(PARTS) - 1)
                    last.then_inc(S("m1_hid_mm"), 1)

            def outputs1(b, e):
                n = b * E1 + e
                pe.wait_ge(S("m1_low"), at(n))
                pe.wait_ge(S("m1_acc"), at(n, 2))
                for t in range(NT):
                    for k, (sh, sw) in enumerate(PARTS):
                        for h in range(HC1):
                            w = slice((e * HC1 + h) * 128, (e * HC1 + h) * 128 + 128)
                            part = (h_high, h_low)[sh][e % 4][:, h * T + t * 128:h * T + t * 128 + 128]
                            last = mm(tile(bank(4 + e % 2), t), part, w2_hl[:, sw, w],
                                      start=k == 0 and h == 0, stop=k == len(PARTS) - 1 and h == HC1 - 1)
                last.then_inc(S("m1_out_mm"), 1)

            def coefficients_transposed(b):
                pe.wait_ge(S("m1_cs"), at(b))
                pe.wait_ge(S("m1_cT"), at(b, 1))
                for t in range(NT):
                    last = nc.tensor.transpose(tile(bank(6)[0:E1, :], t), cstage[:, t, :], ident[:, :])
                last.then_inc(S("m1_cT_mm"), 1)

            def all_experts(b, last_batch):
                for e in range(E1):
                    if e < E1 - AHEAD:
                        hidden1(b, e + AHEAD)
                    elif not last_batch:
                        hidden1(b + 1, e + AHEAD - E1)
                    outputs1(b, e)
                    if e == 1:
                        coefficients_transposed(b)
                    if e == 5:
                        pe.wait_ge(s_routed, 1)
                        pe.wait_ge(S("m1_cT"), at(b))
                        pe.wait_ge(S("m1_bias"), at(b, 1))
                        tokens_out(bank(7), cT, mb2[:, :]).then_inc(S("m1_bias_mm"), 1)

            for e in range(AHEAD):
                hidden1(0, e)
            with pe.Fori(0, B - 1) as b:
                all_experts(b, False)
            all_experts(B - 1, True)
            pe.drain().then_inc(stage_done, 1)


W0_LOADS = 5
W_LOADS = 29

_INS = ["L0_attn_x", "L0_attn_Wq", "L0_attn_Wk", "L0_attn_Wv", "L0_attn_Wbeta", "L0_attn_Wg", "L0_attn_Wout",
        "L0_attn_ln_g", "L0_attn_ln_b", "L0_ffn_rw1", "L0_ffn_rb1", "L0_ffn_rw2", "L0_ffn_rb2", "L0_ffn_ew1",
        "L0_ffn_eb1", "L0_ffn_ew2", "L0_ffn_eb2", "L1_attn_ln_w", "L1_attn_ln_b", "L1_attn_Wq", "L1_attn_Wk",
        "L1_attn_Wv", "L1_attn_gk_w1", "L1_attn_gk_w2", "L1_attn_gk_b2", "L1_attn_Wg", "L1_attn_rms_w", "L1_attn_Wo",
        "L1_attn_W1", "L1_attn_b1", "L1_attn_W2", "L1_attn_b2", "L1_ffn_router_w", "L1_ffn_router_b", "L1_ffn_w1",
        "L1_ffn_b1", "L1_ffn_w2", "L1_ffn_b2"]


def kernel(**inputs):
    import numpy as _np
    import concourse.bacc as _bacc
    from concourse import mybir as _mybir
    from concourse.bass_utils import run_bass_kernel_spmd as _run

    nc = _bacc.Bacc("TRN2", target_bir_lowering=False, num_devices=1)
    arrays, aps = {}, {}
    for name in _INS:
        a = _np.ascontiguousarray(inputs[name])
        arrays["in_" + name] = a
        aps[name] = nc.dram_tensor("in_" + name, a.shape, _mybir.dt.from_np(a.dtype), kind="ExternalInput").ap()
    shape = inputs["L0_attn_x"].shape
    out = nc.dram_tensor("out_x", shape, _mybir.dt.float32, kind="ExternalOutput").ap()
    build(nc, aps, out)
    r = _run(nc, [arrays], core_ids=[0])
    return r.results[0]["out_x"]
```
